# Optimizing a Trainium2 kernel written in Bass

```python
import numpy as np
import jax
import jax.numpy as jnp

def _softmax(x, axis=-1):
    return jax.nn.softmax(x, axis=axis)

def _gelu(x):
    return jax.nn.gelu(x, approximate=True)

def _silu(x):
    return jax.nn.silu(x)

def _sigmoid(x):
    return jax.nn.sigmoid(x)

def _layernorm(x, axis=-1, eps=1e-05):
    m = jnp.mean(x, axis=axis, keepdims=True)
    v = jnp.var(x, axis=axis, keepdims=True)
    return (x - m) / jnp.sqrt(v + eps)

def _scatter_add(tgt, idx, src, axis=0):
    return tgt.at[idx].add(src)

def _segment_sum(src, seg, n):
    return jax.ops.segment_sum(src, seg, n)
kernel_name = 'mk_decoder_preln_d4_seqx_r8_cfd6b9'

def setup_inputs(seed: int=0):
    np.random.seed(seed)
    _w = jnp.asarray

    def _rec_inputs():
        import jax
        import jax.numpy as jnp
        _rk = jax.random.key(seed)
        x = 7.22e-05 + 1 * jax.random.normal(jax.random.fold_in(_rk, 1), (4, 256, 128), jnp.float32)
        _lenS = 256 - jax.random.randint(jax.random.fold_in(_rk, 7), (4,), 0, max(1, 256 // 4) + 1, jnp.int32)
        _lenS2 = 64 - jax.random.randint(jax.random.fold_in(_rk, 8), (4,), 0, max(1, 64 // 4) + 1, jnp.int32)
        _ctx_1024P = jax.random.normal(jax.random.fold_in(_rk, 11), (4, 16, 128), jnp.float32)
        _ctx_1024c = jax.random.dirichlet(jax.random.fold_in(_rk, 511), 0.3 * jnp.ones((16,), jnp.float32), (4, 64))
        _ctx_1024t = jnp.einsum('bsk,bkd->bsd', _ctx_1024c, _ctx_1024P)
        _ctx_1024t = _ctx_1024t * jax.lax.rsqrt(jnp.mean(jnp.square(_ctx_1024t)) + 1e-12) * 0.953939
        ctx_1024 = 4.13588e-05 + 0.999923 * (_ctx_1024t + 0.3 * jax.random.normal(jax.random.fold_in(_rk, 611), (4, 64, 128), jnp.float32))
        itok_BxS_0_255 = jax.random.randint(jax.random.fold_in(_rk, 13), (4, 256), 0, 32, jnp.int32)
        itok_BxS_0_1023 = jax.random.randint(jax.random.fold_in(_rk, 14), (4, 256), 0, 128, jnp.int32)
        itok_BxS2_0_2047 = jax.random.randint(jax.random.fold_in(_rk, 15), (4, 64), 0, 256, jnp.int32)
        _validS = jnp.arange(256)[None, :] < _lenS[:, None]
        _validS2 = jnp.arange(64)[None, :] < _lenS2[:, None]
        _causal = jnp.tril(jnp.ones((256, 256), dtype=bool))
        mask_BxS2_ff1 = jnp.where(jnp.ones((4, 64), dtype=bool), 1.0, 0.0).astype(jnp.float32)
        return (x, ctx_1024, itok_BxS_0_255, itok_BxS_0_1023, itok_BxS2_0_2047, mask_BxS2_ff1)
    x, ctx_1024, itok_BxS_0_255, itok_BxS_0_1023, itok_BxS2_0_2047, mask_BxS2_ff1 = _rec_inputs()

    def _L0_attn_setup():
        import jax, jax.numpy as jnp
        import numpy as np
        B, S, D = (4, 512, 128)
        GROUP = 32
        HEAD = 128
        INNER = 256
        key = jax.random.key(seed)
        ks = jax.random.split(key, 16)
        s = 0.02
        return {'x': jax.random.normal(ks[0], (B, S, D), jnp.float32), 'Wv': jax.random.normal(ks[1], (D, INNER), jnp.float32) * s, 'bv': jnp.zeros((INNER,), jnp.float32), 'Wg': jax.random.normal(ks[2], (D, INNER), jnp.float32) * s, 'bg': jnp.zeros((INNER,), jnp.float32), 'Win': jax.random.normal(ks[3], (D, HEAD), jnp.float32) * s, 'bin_': jnp.zeros((HEAD,), jnp.float32), 'Wout': jax.random.normal(ks[4], (INNER, D), jnp.float32) * s, 'bout': jnp.zeros((D,), jnp.float32), 'g_qq': 1.0 + jax.random.normal(ks[5], (HEAD,), jnp.float32) * s, 'b_qq': jnp.zeros((HEAD,), jnp.float32), 'g_qk': 1.0 + jax.random.normal(ks[6], (HEAD,), jnp.float32) * s, 'b_qk': jnp.zeros((HEAD,), jnp.float32), 'g_lq': 1.0 + jax.random.normal(ks[7], (HEAD,), jnp.float32) * s, 'b_lq': jnp.zeros((HEAD,), jnp.float32), 'g_lk': 1.0 + jax.random.normal(ks[8], (HEAD,), jnp.float32) * s, 'b_lk': jnp.zeros((HEAD,), jnp.float32)}
    _L0_attn_all = _L0_attn_setup()
    _L0_attn_in = {k: v for k, v in _L0_attn_all.items() if k in ('Wv', 'bv', 'Wg', 'bg', 'Win', 'bin_', 'Wout', 'bout', 'g_qq', 'b_qq', 'g_qk', 'b_qk', 'g_lq', 'b_lq', 'g_lk', 'b_lk')}
    del _L0_attn_all

    def _L0_xattn_setup():
        import jax, jax.numpy as jnp
        import numpy as np
        EMBED_DIM = 128
        NUM_HEADS = 16
        HEAD_DIM = EMBED_DIM // NUM_HEADS
        BSZ, TGT, SRC = (4, 256, 256)

        def _split_heads(x, bsz, seqlen):
            return x.reshape(bsz, seqlen, NUM_HEADS, HEAD_DIM).transpose(0, 2, 1, 3)
        key = jax.random.key(seed)
        ks = jax.random.split(key, 8)
        s = EMBED_DIM ** (-0.5)
        return {'query': jax.random.normal(ks[0], (BSZ, TGT, EMBED_DIM), jnp.float32), 'key': jax.random.normal(ks[1], (BSZ, SRC, EMBED_DIM), jnp.float32), 'key_padding_mask': jnp.ones((BSZ, SRC), jnp.float32), 'Wq': jax.random.normal(ks[2], (EMBED_DIM, EMBED_DIM), jnp.float32) * s, 'bq': jnp.zeros((EMBED_DIM,), jnp.float32), 'Wk': jax.random.normal(ks[3], (EMBED_DIM, EMBED_DIM), jnp.float32) * s, 'bk': jnp.zeros((EMBED_DIM,), jnp.float32), 'Wv': jax.random.normal(ks[4], (EMBED_DIM, EMBED_DIM), jnp.float32) * s, 'bv': jnp.zeros((EMBED_DIM,), jnp.float32), 'Wo': jax.random.normal(ks[5], (EMBED_DIM, EMBED_DIM), jnp.float32) * s, 'bo': jnp.zeros((EMBED_DIM,), jnp.float32)}
    _L0_xattn_all = _L0_xattn_setup()
    _L0_xattn_in = {k: v for k, v in _L0_xattn_all.items() if k in ('Wq', 'bq', 'Wk', 'bk', 'Wv', 'bv', 'Wo', 'bo')}
    del _L0_xattn_all

    def _L0_ffn_setup():
        import jax, jax.numpy as jnp
        import numpy as np
        BLOCK = 16
        _GRID = jnp.array([0.0, 0.5, 1.0, 1.5, 2.0, 3.0, 4.0, 6.0], dtype=jnp.float32)
        _MID = jnp.array([0.25, 0.75, 1.25, 1.75, 2.5, 3.5, 5.0], dtype=jnp.float32)

        def fp4_quant_dequant(x):
            shape = x.shape
            xb = x.reshape(shape[:-1] + (shape[-1] // BLOCK, BLOCK))
            scale = jnp.max(jnp.abs(xb), axis=-1, keepdims=True) / 6.0
            scale = jnp.maximum(scale, jnp.float32(1e-12))
            xn = xb / scale
            idx = jnp.searchsorted(_MID, jnp.abs(xn))
            q = _GRID[idx] * jnp.sign(xn) * scale
            return q.reshape(shape)

        def fp4_linear(x, w):
            xq = fp4_quant_dequant(x)
            wq = fp4_quant_dequant(w)
            return jnp.einsum('bsk,nk->bsn', xq, wq)
        key = jax.random.key(seed)
        k1, k2, k3, k4 = jax.random.split(key, 4)
        H, I = (128, 352)
        x = jax.random.normal(k1, (4, 512, H), dtype=jnp.float32)
        w_gate = jax.random.normal(k2, (I, H), dtype=jnp.float32) * 0.02
        w_up = jax.random.normal(k3, (I, H), dtype=jnp.float32) * 0.02
        w_down = jax.random.normal(k4, (H, I), dtype=jnp.float32) * 0.02
        return {'x': x, 'w_gate': w_gate, 'w_up': w_up, 'w_down': w_down}
    _L0_ffn_all = _L0_ffn_setup()
    _L0_ffn_in = {k: v for k, v in _L0_ffn_all.items() if k in ('w_gate', 'w_up', 'w_down')}
    del _L0_ffn_all

    def _L1_attn_setup():
        import jax, jax.numpy as jnp
        import numpy as np
        D_MODEL, N_HEADS = (128, 16)
        D_H = D_MODEL // N_HEADS
        D_HR = D_H // 2
        D_LATENT = 32
        THETA = 10000.0

        def rope(x, theta=THETA):
            S, d = (x.shape[-2], x.shape[-1])
            inv = theta ** (-jnp.arange(0, d, 2, dtype=jnp.float32) / d)
            ang = jnp.arange(S, dtype=jnp.float32)[:, None] * inv
            cos, sin = (jnp.cos(ang), jnp.sin(ang))
            x1, x2 = (x[..., 0::2], x[..., 1::2])
            r1 = x1 * cos - x2 * sin
            r2 = x1 * sin + x2 * cos
            return jnp.stack([r1, r2], axis=-1).reshape(x.shape)
        key = jax.random.key(seed)
        ks = jax.random.split(key, 9)
        s = lambda fan_in: 1.0 / np.sqrt(fan_in)
        return {'x': jax.random.normal(ks[0], (4, 256, D_MODEL), jnp.float32), 'W_DQ': jax.random.normal(ks[1], (D_MODEL, D_LATENT), jnp.float32) * s(D_MODEL), 'W_UQ': jax.random.normal(ks[2], (D_LATENT, N_HEADS * D_H), jnp.float32) * s(D_LATENT), 'W_QR': jax.random.normal(ks[3], (D_LATENT, N_HEADS * D_HR), jnp.float32) * s(D_LATENT), 'W_DKV': jax.random.normal(ks[4], (D_MODEL, D_LATENT), jnp.float32) * s(D_MODEL), 'W_UK': jax.random.normal(ks[5], (D_LATENT, N_HEADS * D_H), jnp.float32) * s(D_LATENT), 'W_UV': jax.random.normal(ks[6], (D_LATENT, N_HEADS * D_H), jnp.float32) * s(D_LATENT), 'W_KR': jax.random.normal(ks[7], (D_MODEL, D_HR), jnp.float32) * s(D_MODEL), 'W_O': jax.random.normal(ks[8], (N_HEADS * D_H, D_MODEL), jnp.float32) * s(N_HEADS * D_H)}
    _L1_attn_all = _L1_attn_setup()
    _L1_attn_in = {k: v for k, v in _L1_attn_all.items() if k in ('W_DQ', 'W_UQ', 'W_QR', 'W_DKV', 'W_UK', 'W_UV', 'W_KR', 'W_O')}
    del _L1_attn_all

    def _L1_xattn_setup():
        import jax, jax.numpy as jnp
        import numpy as np
        N_LAYERS = 4
        H = 16
        LOOKBACK = 128
        EPS = 1e-06
        ROPE_BASE = 10000.0
        NEG = jnp.float32(-1e+30)

        def rmsnorm(x, w):
            return x * jax.lax.rsqrt(jnp.mean(x * x, axis=-1, keepdims=True) + EPS) * w

        def rope_cache(L, hd):
            inv = 1.0 / ROPE_BASE ** (jnp.arange(0, hd, 2, dtype=jnp.float32) / hd)
            t = jnp.arange(L, dtype=jnp.float32)
            f = t[:, None] * inv[None, :]
            emb = jnp.concatenate([f, f], axis=-1)
            return (jnp.cos(emb), jnp.sin(emb))

        def apply_rope(x, cos, sin):
            d = x.shape[-1]
            x1, x2 = (x[..., :d // 2], x[..., d // 2:])
            rot = jnp.concatenate([-x2, x1], axis=-1)
            return x * cos + rot * sin

        def split_heads(x, n_heads):
            B, L, D = x.shape
            return x.reshape(B, L, n_heads, D // n_heads).transpose(0, 2, 1, 3)

        def merge_heads(x):
            B, h, L, d = x.shape
            return x.transpose(0, 2, 1, 3).reshape(B, L, h * d)

        def sdpa(q, k, v, bias):
            scale = q.shape[-1] ** (-0.5)
            s = jnp.einsum('bhqd,bhkd->bhqk', q, k) * scale + bias
            p = jax.nn.softmax(s, axis=-1)
            return jnp.einsum('bhqk,bhkd->bhqd', p, v)

        def forward(x, memory, seg_ids, Wqkv, bqkv, Wo, bo, Wq_c, Wkv_c, Wo_c, Wg, Wu, Wd, n1, n2, n3, nf):
            B, L, D = x.shape
            S = memory.shape[1]
            hd = D // H
            cos, sin = rope_cache(L, hd)
            i = jnp.arange(L)
            causal_bias = jnp.where(i[None, :] <= i[:, None], 0.0, NEG)[None, None]
            j = jnp.arange(S)
            allowed = (j[None, None, :] <= seg_ids[:, :, None]) & (j[None, None, :] > seg_ids[:, :, None] - LOOKBACK)
            cross_bias = jnp.where(allowed, 0.0, NEG)[:, None]
            for l in range(N_LAYERS):
                h = rmsnorm(x, n1[l])
                qkv = h @ Wqkv[l].T + bqkv[l]
                q, k, v = jnp.split(qkv, 3, axis=-1)
                q = apply_rope(split_heads(q, H), cos, sin)
                k = apply_rope(split_heads(k, H), cos, sin)
                v = split_heads(v, H)
                o = merge_heads(sdpa(q, k, v, causal_bias)) @ Wo[l].T + bo[l]
                x = x + o
                h2 = rmsnorm(x, n2[l])
                qc = split_heads(h2 @ Wq_c[l].T, H)
                kv = memory @ Wkv_c[l].T
                kc, vc = jnp.split(kv, 2, axis=-1)
                kc, vc = (split_heads(kc, H), split_heads(vc, H))
                oc = merge_heads(sdpa(qc, kc, vc, cross_bias)) @ Wo_c[l].T
                x = x + oc
                h3 = rmsnorm(x, n3[l])
                x = x + jax.nn.silu(h3 @ Wg[l].T) * (h3 @ Wu[l].T) @ Wd[l].T
            return rmsnorm(x, nf)
        key = jax.random.key(seed)
        ks = jax.random.split(key, 16)
        B, L, S, D, F = (2, 256, 32, 128, 512)
        w = 0.02
        inp = {'x': jax.random.normal(ks[0], (B, L, D), jnp.float32), 'memory': jax.random.normal(ks[1], (B, S, D), jnp.float32), 'seg_ids': jnp.sort(jax.random.randint(ks[2], (B, L), 0, S), axis=-1), 'Wqkv': jax.random.normal(ks[3], (N_LAYERS, 3 * D, D), jnp.float32) * w, 'bqkv': jnp.zeros((N_LAYERS, 3 * D), jnp.float32), 'Wo': jax.random.normal(ks[4], (N_LAYERS, D, D), jnp.float32) * w, 'bo': jnp.zeros((N_LAYERS, D), jnp.float32), 'Wq_c': jax.random.normal(ks[5], (N_LAYERS, D, D), jnp.float32) * w, 'Wkv_c': jax.random.normal(ks[6], (N_LAYERS, 2 * D, D), jnp.float32) * w, 'Wo_c': jax.random.normal(ks[7], (N_LAYERS, D, D), jnp.float32) * w, 'Wg': jax.random.normal(ks[8], (N_LAYERS, F, D), jnp.float32) * w, 'Wu': jax.random.normal(ks[9], (N_LAYERS, F, D), jnp.float32) * w, 'Wd': jax.random.normal(ks[10], (N_LAYERS, D, F), jnp.float32) * w, 'n1': jnp.ones((N_LAYERS, D), jnp.float32), 'n2': jnp.ones((N_LAYERS, D), jnp.float32), 'n3': jnp.ones((N_LAYERS, D), jnp.float32), 'nf': jnp.ones((D,), jnp.float32)}
        return inp
    _L1_xattn_all = _L1_xattn_setup()
    _L1_xattn_in = {k: v for k, v in _L1_xattn_all.items() if k in ('Wqkv', 'bqkv', 'Wo', 'bo', 'Wq_c', 'Wkv_c', 'Wo_c', 'Wg', 'Wu', 'Wd', 'n1', 'n2', 'n3', 'nf')}
    del _L1_xattn_all

    def _L1_ffn_setup():
        import jax, jax.numpy as jnp
        import numpy as np
        B, L, D, E, K, DFF = (2, 256, 128, 8, 2, 512)
        key = jax.random.key(seed)
        kx, kr, kg, ku, kd = jax.random.split(key, 5)
        scale = 0.02
        return {'x': jax.random.normal(kx, (B, L, D), dtype=jnp.float32), 'Wr': jax.random.normal(kr, (E, D), dtype=jnp.float32) * scale, 'Wg': jax.random.normal(kg, (E, DFF, D), dtype=jnp.float32) * scale, 'Wu': jax.random.normal(ku, (E, DFF, D), dtype=jnp.float32) * scale, 'Wd': jax.random.normal(kd, (E, D, DFF), dtype=jnp.float32) * scale}
    _L1_ffn_all = _L1_ffn_setup()
    _L1_ffn_in = {k: v for k, v in _L1_ffn_all.items() if k in ('Wr', 'Wg', 'Wu', 'Wd')}
    del _L1_ffn_all

    def _L2_attn_setup():
        import jax, jax.numpy as jnp
        import numpy as np
        EMB = 128
        HEADS = 16
        HEAD_DIM = EMB // HEADS
        ROPE_BASE = 10000.0

        def rotate_half(x):
            x1 = x[..., ::2]
            x2 = x[..., 1::2]
            return jnp.stack((-x2, x1), axis=-1).reshape(x.shape)

        def rope_cos_sin(seq_len, head_dim):
            inv_freq = 1.0 / ROPE_BASE ** (jnp.arange(0, head_dim, 2, dtype=jnp.float32) / head_dim)
            pos = jnp.arange(seq_len, dtype=jnp.float32)
            freqs = jnp.outer(pos, inv_freq)
            emb = jnp.concatenate([freqs, freqs], -1)
            return (jnp.cos(emb)[None, None], jnp.sin(emb)[None, None])
        key = jax.random.key(seed)
        ks = jax.random.split(key, 5)
        B, S = (2, 256)
        x = jax.random.normal(ks[0], (B, S, EMB), dtype=jnp.float32)
        scale = EMB ** (-0.5)
        Wq = jax.random.normal(ks[1], (EMB, EMB), dtype=jnp.float32) * scale
        Wk = jax.random.normal(ks[2], (EMB, EMB), dtype=jnp.float32) * scale
        Wv = jax.random.normal(ks[3], (EMB, EMB), dtype=jnp.float32) * scale
        Wo = jax.random.normal(ks[4], (EMB, EMB), dtype=jnp.float32) * scale
        return {'x': x, 'Wq': Wq, 'Wk': Wk, 'Wv': Wv, 'Wo': Wo}
    _L2_attn_all = _L2_attn_setup()
    _L2_attn_in = {k: v for k, v in _L2_attn_all.items() if k in ('Wq', 'Wk', 'Wv', 'Wo')}
    del _L2_attn_all

    def _L2_xattn_setup():
        import jax, jax.numpy as jnp
        import numpy as np
        DIM = 128
        H = 16
        HD = DIM // H
        SCALE = HD ** (-0.5)
        LAMBDA_INIT = 0.1
        EPS = 1e-06

        def _split_heads(x, B, N):
            return x.reshape(B, N, H, HD).transpose(0, 2, 1, 3)
        key0 = jax.random.key(seed)
        ks = jax.random.split(key0, 12)
        B, Nq, Nk = (2, 128, 256)
        w = 0.02
        inp = {'query': jax.random.normal(ks[0], (B, Nq, DIM), jnp.float32), 'key': jax.random.normal(ks[1], (B, Nk, DIM), jnp.float32), 'value': jax.random.normal(ks[2], (B, Nk, DIM), jnp.float32), 'qpos': jax.random.randint(ks[3], (B, Nq), 0, Nq, jnp.int32), 'kpos': jax.random.randint(ks[4], (B, Nk), 0, Nk, jnp.int32), 'q1_w': jax.random.normal(ks[5], (DIM, DIM), jnp.float32) * w, 'q2_w': jax.random.normal(ks[6], (DIM, DIM), jnp.float32) * w, 'kv1_w': jax.random.normal(ks[7], (2 * DIM, DIM), jnp.float32) * w, 'kv2_w': jax.random.normal(ks[8], (2 * DIM, DIM), jnp.float32) * w, 'proj_w': jax.random.normal(ks[9], (DIM, DIM), jnp.float32) * w, 'proj_b': jnp.zeros((DIM,), jnp.float32), 'norm_w': jnp.ones((DIM,), jnp.float32), 'lambda_1': jnp.ones((1, H, 1, 1), jnp.float32), 'lambda_2': jnp.full((1, H, 1, 1), 1.0 - LAMBDA_INIT * (1.0 / 12.0), jnp.float32)}
        return inp
    _L2_xattn_all = _L2_xattn_setup()
    _L2_xattn_in = {k: v for k, v in _L2_xattn_all.items() if k in ('q1_w', 'q2_w', 'kv1_w', 'kv2_w', 'proj_w', 'proj_b', 'norm_w', 'lambda_1', 'lambda_2')}
    del _L2_xattn_all

    def _L2_ffn_setup():
        import jax, jax.numpy as jnp
        import numpy as np
        B, S, D, F, E = (4, 256, 128, 512, 8)
        key = jax.random.key(seed)
        ks = jax.random.split(key, 7)
        s1 = 1.0 / np.sqrt(D)
        s2 = 1.0 / np.sqrt(F)
        x = jax.random.normal(ks[0], (B, S, D), dtype=jnp.float32)
        W1 = jax.random.uniform(ks[1], (E, D, F), jnp.float32, -s1, s1)
        b1 = jax.random.uniform(ks[2], (E, F), jnp.float32, -s1, s1)
        W2 = jax.random.uniform(ks[3], (E, F, D), jnp.float32, -s2, s2)
        b2 = jax.random.uniform(ks[4], (E, D), jnp.float32, -s2, s2)
        Wr = jax.random.uniform(ks[5], (D, E), jnp.float32, -s1, s1)
        br = jax.random.uniform(ks[6], (E,), jnp.float32, -s1, s1)
        return {'x': x, 'W1': W1, 'b1': b1, 'W2': W2, 'b2': b2, 'Wr': Wr, 'br': br}
    _L2_ffn_all = _L2_ffn_setup()
    _L2_ffn_in = {k: v for k, v in _L2_ffn_all.items() if k in ('W1', 'b1', 'W2', 'b2', 'Wr', 'br')}
    del _L2_ffn_all

    def _L3_attn_setup():
        import jax, jax.numpy as jnp
        import numpy as np
        import math
        E = 128
        H = 16
        B = 2
        T = 256

        def _rotary(x):
            D = x.shape[-1]
            inv_freq = 1.0 / 10000.0 ** (jnp.arange(0, D, 2, dtype=jnp.float32) / D)
            t = jnp.arange(x.shape[-2], dtype=jnp.float32)
            freqs = t[:, None] * inv_freq[None, :]
            emb = jnp.concatenate([freqs, freqs], axis=-1)
            cos = jnp.cos(emb)
            sin = jnp.sin(emb)
            x1 = x[..., ::2]
            x2 = x[..., 1::2]
            x_rot = jnp.stack([-x2, x1], axis=-1).reshape(x.shape)
            return x * cos + x_rot * sin
        key = jax.random.key(seed)
        ks = jax.random.split(key, 10)
        s = 0.02
        inp = {'x': jax.random.normal(ks[0], (B, T, E), dtype=jnp.float32), 'Wq': jax.random.normal(ks[1], (E, E), dtype=jnp.float32) * s, 'bq': jnp.zeros((E,), jnp.float32), 'Wk': jax.random.normal(ks[2], (E, E), dtype=jnp.float32) * s, 'bk': jnp.zeros((E,), jnp.float32), 'Wv': jax.random.normal(ks[3], (E, E), dtype=jnp.float32) * s, 'bv': jnp.zeros((E,), jnp.float32), 'Wg': jax.random.normal(ks[4], (E, E), dtype=jnp.float32) * s, 'bg': jnp.zeros((E,), jnp.float32), 'gamma': jax.random.normal(ks[5], (H,), dtype=jnp.float32)}
        return inp
    _L3_attn_all = _L3_attn_setup()
    _L3_attn_in = {k: v for k, v in _L3_attn_all.items() if k in ('Wq', 'bq', 'Wk', 'bk', 'Wv', 'bv', 'Wg', 'bg', 'gamma')}
    del _L3_attn_all

    def _L3_xattn_setup():
        import jax, jax.numpy as jnp
        import numpy as np
        B, L, D_MODEL = (2, 256, 128)
        N_HEADS, D_K = (16, 64)
        key = jax.random.key(seed)
        ks = jax.random.split(key, 8)
        std = float(np.sqrt(2.0 / (D_MODEL + D_K)))
        std_p = float(np.sqrt(1.0 / (N_HEADS * D_K)))
        return {'q': jax.random.normal(ks[0], (B, L, D_MODEL), jnp.float32), 'k': jax.random.normal(ks[1], (B, L, D_MODEL), jnp.float32), 'v': jax.random.normal(ks[2], (B, L, D_MODEL), jnp.float32), 'w_qs': jax.random.normal(ks[3], (N_HEADS, D_MODEL, D_K), jnp.float32) * std, 'w_ks': jax.random.normal(ks[4], (N_HEADS, D_MODEL, D_K), jnp.float32) * std, 'w_vs': jax.random.normal(ks[5], (N_HEADS, D_MODEL, D_K), jnp.float32) * std, 'w_proj': jax.random.normal(ks[6], (D_MODEL, N_HEADS * D_K), jnp.float32) * std_p, 'b_proj': jnp.zeros((D_MODEL,), jnp.float32)}
    _L3_xattn_all = _L3_xattn_setup()
    _L3_xattn_in = {k: v for k, v in _L3_xattn_all.items() if k in ('w_qs', 'w_ks', 'w_vs', 'w_proj', 'b_proj')}
    del _L3_xattn_all

    def _L3_ffn_setup():
        import jax, jax.numpy as jnp
        import numpy as np
        D_MODEL = 128
        D_FF = 512
        N_EXPERTS = 8
        TOP_K = 2
        B, S = (4, 256)
        key = jax.random.key(seed)
        ks = jax.random.split(key, 8)
        std = 0.02
        x = jax.random.normal(ks[0], (B, S, D_MODEL), dtype=jnp.float32)
        router_w = jax.random.normal(ks[1], (N_EXPERTS, D_MODEL), dtype=jnp.float32) * std
        router_b = jnp.zeros((N_EXPERTS,), dtype=jnp.float32)
        w1 = jax.random.normal(ks[2], (N_EXPERTS, D_FF, D_MODEL), dtype=jnp.float32) * std
        b1 = jnp.zeros((N_EXPERTS, D_FF), dtype=jnp.float32)
        w2 = jax.random.normal(ks[3], (N_EXPERTS, D_MODEL, D_FF), dtype=jnp.float32) * std
        b2 = jnp.zeros((N_EXPERTS, D_MODEL), dtype=jnp.float32)
        return {'x': x, 'router_w': router_w, 'router_b': router_b, 'w1': w1, 'b1': b1, 'w2': w2, 'b2': b2}
    _L3_ffn_all = _L3_ffn_setup()
    _L3_ffn_in = {k: v for k, v in _L3_ffn_all.items() if k in ('router_w', 'router_b', 'w1', 'b1', 'w2', 'b2')}
    del _L3_ffn_all
    return {'x': x, 'ctx_1024': ctx_1024, 'itok_BxS_0_255': itok_BxS_0_255, 'itok_BxS_0_1023': itok_BxS_0_1023, 'itok_BxS2_0_2047': itok_BxS2_0_2047, 'mask_BxS2_ff1': mask_BxS2_ff1, 'L0_attn_Wv': _L0_attn_in['Wv'], 'L0_attn_bv': _L0_attn_in['bv'], 'L0_attn_Wg': _L0_attn_in['Wg'], 'L0_attn_bg': _L0_attn_in['bg'], 'L0_attn_Win': _L0_attn_in['Win'], 'L0_attn_bin_': _L0_attn_in['bin_'], 'L0_attn_Wout': _L0_attn_in['Wout'], 'L0_attn_bout': _L0_attn_in['bout'], 'L0_attn_g_qq': _L0_attn_in['g_qq'], 'L0_attn_b_qq': _L0_attn_in['b_qq'], 'L0_attn_g_qk': _L0_attn_in['g_qk'], 'L0_attn_b_qk': _L0_attn_in['b_qk'], 'L0_attn_g_lq': _L0_attn_in['g_lq'], 'L0_attn_b_lq': _L0_attn_in['b_lq'], 'L0_attn_g_lk': _L0_attn_in['g_lk'], 'L0_attn_b_lk': _L0_attn_in['b_lk'], 'L0_xattn_Wq': _L0_xattn_in['Wq'], 'L0_xattn_bq': _L0_xattn_in['bq'], 'L0_xattn_Wk': _L0_xattn_in['Wk'], 'L0_xattn_bk': _L0_xattn_in['bk'], 'L0_xattn_Wv': _L0_xattn_in['Wv'], 'L0_xattn_bv': _L0_xattn_in['bv'], 'L0_xattn_Wo': _L0_xattn_in['Wo'], 'L0_xattn_bo': _L0_xattn_in['bo'], 'L0_ffn_w_gate': _L0_ffn_in['w_gate'], 'L0_ffn_w_up': _L0_ffn_in['w_up'], 'L0_ffn_w_down': _L0_ffn_in['w_down'], 'L1_attn_W_DQ': _L1_attn_in['W_DQ'], 'L1_attn_W_UQ': _L1_attn_in['W_UQ'], 'L1_attn_W_QR': _L1_attn_in['W_QR'], 'L1_attn_W_DKV': _L1_attn_in['W_DKV'], 'L1_attn_W_UK': _L1_attn_in['W_UK'], 'L1_attn_W_UV': _L1_attn_in['W_UV'], 'L1_attn_W_KR': _L1_attn_in['W_KR'], 'L1_attn_W_O': _L1_attn_in['W_O'], 'L1_xattn_Wqkv': _L1_xattn_in['Wqkv'], 'L1_xattn_bqkv': _L1_xattn_in['bqkv'], 'L1_xattn_Wo': _L1_xattn_in['Wo'], 'L1_xattn_bo': _L1_xattn_in['bo'], 'L1_xattn_Wq_c': _L1_xattn_in['Wq_c'], 'L1_xattn_Wkv_c': _L1_xattn_in['Wkv_c'], 'L1_xattn_Wo_c': _L1_xattn_in['Wo_c'], 'L1_xattn_Wg': _L1_xattn_in['Wg'], 'L1_xattn_Wu': _L1_xattn_in['Wu'], 'L1_xattn_Wd': _L1_xattn_in['Wd'], 'L1_xattn_n1': _L1_xattn_in['n1'], 'L1_xattn_n2': _L1_xattn_in['n2'], 'L1_xattn_n3': _L1_xattn_in['n3'], 'L1_xattn_nf': _L1_xattn_in['nf'], 'L1_ffn_Wr': _L1_ffn_in['Wr'], 'L1_ffn_Wg': _L1_ffn_in['Wg'], 'L1_ffn_Wu': _L1_ffn_in['Wu'], 'L1_ffn_Wd': _L1_ffn_in['Wd'], 'L2_attn_Wq': _L2_attn_in['Wq'], 'L2_attn_Wk': _L2_attn_in['Wk'], 'L2_attn_Wv': _L2_attn_in['Wv'], 'L2_attn_Wo': _L2_attn_in['Wo'], 'L2_xattn_q1_w': _L2_xattn_in['q1_w'], 'L2_xattn_q2_w': _L2_xattn_in['q2_w'], 'L2_xattn_kv1_w': _L2_xattn_in['kv1_w'], 'L2_xattn_kv2_w': _L2_xattn_in['kv2_w'], 'L2_xattn_proj_w': _L2_xattn_in['proj_w'], 'L2_xattn_proj_b': _L2_xattn_in['proj_b'], 'L2_xattn_norm_w': _L2_xattn_in['norm_w'], 'L2_xattn_lambda_1': _L2_xattn_in['lambda_1'], 'L2_xattn_lambda_2': _L2_xattn_in['lambda_2'], 'L2_ffn_W1': _L2_ffn_in['W1'], 'L2_ffn_b1': _L2_ffn_in['b1'], 'L2_ffn_W2': _L2_ffn_in['W2'], 'L2_ffn_b2': _L2_ffn_in['b2'], 'L2_ffn_Wr': _L2_ffn_in['Wr'], 'L2_ffn_br': _L2_ffn_in['br'], 'L3_attn_Wq': _L3_attn_in['Wq'], 'L3_attn_bq': _L3_attn_in['bq'], 'L3_attn_Wk': _L3_attn_in['Wk'], 'L3_attn_bk': _L3_attn_in['bk'], 'L3_attn_Wv': _L3_attn_in['Wv'], 'L3_attn_bv': _L3_attn_in['bv'], 'L3_attn_Wg': _L3_attn_in['Wg'], 'L3_attn_bg': _L3_attn_in['bg'], 'L3_attn_gamma': _L3_attn_in['gamma'], 'L3_xattn_w_qs': _L3_xattn_in['w_qs'], 'L3_xattn_w_ks': _L3_xattn_in['w_ks'], 'L3_xattn_w_vs': _L3_xattn_in['w_vs'], 'L3_xattn_w_proj': _L3_xattn_in['w_proj'], 'L3_xattn_b_proj': _L3_xattn_in['b_proj'], 'L3_ffn_router_w': _L3_ffn_in['router_w'], 'L3_ffn_router_b': _L3_ffn_in['router_b'], 'L3_ffn_w1': _L3_ffn_in['w1'], 'L3_ffn_b1': _L3_ffn_in['b1'], 'L3_ffn_w2': _L3_ffn_in['w2'], 'L3_ffn_b2': _L3_ffn_in['b2']}

def reference(x, ctx_1024, itok_BxS_0_255, itok_BxS_0_1023, itok_BxS2_0_2047, mask_BxS2_ff1, L0_attn_Wv, L0_attn_bv, L0_attn_Wg, L0_attn_bg, L0_attn_Win, L0_attn_bin_, L0_attn_Wout, L0_attn_bout, L0_attn_g_qq, L0_attn_b_qq, L0_attn_g_qk, L0_attn_b_qk, L0_attn_g_lq, L0_attn_b_lq, L0_attn_g_lk, L0_attn_b_lk, L0_xattn_Wq, L0_xattn_bq, L0_xattn_Wk, L0_xattn_bk, L0_xattn_Wv, L0_xattn_bv, L0_xattn_Wo, L0_xattn_bo, L0_ffn_w_gate, L0_ffn_w_up, L0_ffn_w_down, L1_attn_W_DQ, L1_attn_W_UQ, L1_attn_W_QR, L1_attn_W_DKV, L1_attn_W_UK, L1_attn_W_UV, L1_attn_W_KR, L1_attn_W_O, L1_xattn_Wqkv, L1_xattn_bqkv, L1_xattn_Wo, L1_xattn_bo, L1_xattn_Wq_c, L1_xattn_Wkv_c, L1_xattn_Wo_c, L1_xattn_Wg, L1_xattn_Wu, L1_xattn_Wd, L1_xattn_n1, L1_xattn_n2, L1_xattn_n3, L1_xattn_nf, L1_ffn_Wr, L1_ffn_Wg, L1_ffn_Wu, L1_ffn_Wd, L2_attn_Wq, L2_attn_Wk, L2_attn_Wv, L2_attn_Wo, L2_xattn_q1_w, L2_xattn_q2_w, L2_xattn_kv1_w, L2_xattn_kv2_w, L2_xattn_proj_w, L2_xattn_proj_b, L2_xattn_norm_w, L2_xattn_lambda_1, L2_xattn_lambda_2, L2_ffn_W1, L2_ffn_b1, L2_ffn_W2, L2_ffn_b2, L2_ffn_Wr, L2_ffn_br, L3_attn_Wq, L3_attn_bq, L3_attn_Wk, L3_attn_bk, L3_attn_Wv, L3_attn_bv, L3_attn_Wg, L3_attn_bg, L3_attn_gamma, L3_xattn_w_qs, L3_xattn_w_ks, L3_xattn_w_vs, L3_xattn_w_proj, L3_xattn_b_proj, L3_ffn_router_w, L3_ffn_router_b, L3_ffn_w1, L3_ffn_b1, L3_ffn_w2, L3_ffn_b2):
    import jax
    import jax.numpy as jnp

    def _L0_attn_ref(x, Wv, bv, Wg, bg, Win, bin_, Wout, bout, g_qq, b_qq, g_qk, b_qk, g_lq, b_lq, g_lk, b_lk):
        import jax, jax.numpy as jnp
        import numpy as np
        B, S, D = (4, 512, 128)
        GROUP = 32
        HEAD = 128
        INNER = 256
        b, s, d = x.shape
        g = s // GROUP
        xc = x.reshape(b, g, GROUP, d)
        v = jax.nn.silu(xc @ Wv + bv)
        gate = jax.nn.silu(xc @ Wg + bg)
        x_ = jax.nn.silu(xc @ Win + bin_)
        quad_q = x_ * g_qq + b_qq
        quad_k = x_ * g_qk + b_qk
        lin_q = x_ * g_lq + b_lq
        lin_k = x_ * g_lk + b_lk
        scale = jnp.asarray(INNER ** 0.5, x.dtype)
        attn = jnp.einsum('bgns,bgms->bgnm', quad_q, quad_k) / scale
        causal_mask = jnp.triu(jnp.ones((GROUP, GROUP), bool), 1)
        attn = jnp.where(causal_mask, 0.0, attn)
        attn = jnp.square(jax.nn.relu(attn))
        v_quad = jnp.einsum('bgnm,bgme->bgne', attn, v)
        kv = jnp.einsum('bgcs,bgce->bgse', lin_k, v)
        kv = jnp.cumsum(kv, axis=1) - kv
        v_lin = jnp.einsum('bgcs,bgse->bgce', lin_q, kv)
        o = (v_quad + v_lin) * gate
        o = o @ Wout + bout
        return o.reshape(b, s, d)

    def _L0_xattn_ref(query, key, key_padding_mask, Wq, bq, Wk, bk, Wv, bv, Wo, bo):
        import jax, jax.numpy as jnp
        import numpy as np
        EMBED_DIM = 128
        NUM_HEADS = 16
        HEAD_DIM = EMBED_DIM // NUM_HEADS
        BSZ, TGT, SRC = (4, 256, 256)

        def _split_heads(x, bsz, seqlen):
            return x.reshape(bsz, seqlen, NUM_HEADS, HEAD_DIM).transpose(0, 2, 1, 3)
        bsz, src_len, embed_dim = key.shape
        tgt_len = query.shape[1]
        scaling = HEAD_DIM ** (-0.5)
        q = (query @ Wq.T + bq) * scaling
        k = key @ Wk.T + bk
        v = key @ Wv.T + bv
        qh = _split_heads(q, bsz, tgt_len)
        kh = _split_heads(k, bsz, src_len)
        vh = _split_heads(v, bsz, src_len)
        scores = jnp.einsum('bhtd,bhsd->bhts', qh, kh)
        inv = 1.0 - key_padding_mask.astype(scores.dtype)
        neg = jnp.finfo(scores.dtype).min
        add_mask = jnp.where(inv.astype(bool), neg, inv)
        scores = scores + add_mask[:, None, None, :]
        probs = jax.nn.softmax(scores, axis=-1)
        out = jnp.einsum('bhts,bhsd->bhtd', probs, vh)
        out = out.transpose(0, 2, 1, 3).reshape(bsz, tgt_len, embed_dim)
        return out @ Wo.T + bo

    def _L0_ffn_ref(x, w_gate, w_up, w_down):
        import jax, jax.numpy as jnp
        import numpy as np
        BLOCK = 16
        _GRID = jnp.array([0.0, 0.5, 1.0, 1.5, 2.0, 3.0, 4.0, 6.0], dtype=jnp.float32)
        _MID = jnp.array([0.25, 0.75, 1.25, 1.75, 2.5, 3.5, 5.0], dtype=jnp.float32)

        def fp4_quant_dequant(x):
            shape = x.shape
            xb = x.reshape(shape[:-1] + (shape[-1] // BLOCK, BLOCK))
            scale = jnp.max(jnp.abs(xb), axis=-1, keepdims=True) / 6.0
            scale = jnp.maximum(scale, jnp.float32(1e-12))
            xn = xb / scale
            idx = jnp.searchsorted(_MID, jnp.abs(xn))
            q = _GRID[idx] * jnp.sign(xn) * scale
            return q.reshape(shape)

        def fp4_linear(x, w):
            xq = fp4_quant_dequant(x)
            wq = fp4_quant_dequant(w)
            return jnp.einsum('bsk,nk->bsn', xq, wq)
        gate = fp4_linear(x, w_gate)
        y = fp4_linear(x, w_up)
        h = jax.nn.silu(gate) * y
        return fp4_linear(h, w_down)

    def _L1_attn_ref(x, W_DQ, W_UQ, W_QR, W_DKV, W_UK, W_UV, W_KR, W_O):
        import jax, jax.numpy as jnp
        import numpy as np
        D_MODEL, N_HEADS = (128, 16)
        D_H = D_MODEL // N_HEADS
        D_HR = D_H // 2
        D_LATENT = 32
        THETA = 10000.0

        def rope(x, theta=THETA):
            S, d = (x.shape[-2], x.shape[-1])
            inv = theta ** (-jnp.arange(0, d, 2, dtype=jnp.float32) / d)
            ang = jnp.arange(S, dtype=jnp.float32)[:, None] * inv
            cos, sin = (jnp.cos(ang), jnp.sin(ang))
            x1, x2 = (x[..., 0::2], x[..., 1::2])
            r1 = x1 * cos - x2 * sin
            r2 = x1 * sin + x2 * cos
            return jnp.stack([r1, r2], axis=-1).reshape(x.shape)
        B, S, _ = x.shape
        d_qk = D_H + D_HR
        c_q = x @ W_DQ
        Qc = (c_q @ W_UQ).reshape(B, S, N_HEADS, D_H).transpose(0, 2, 1, 3)
        Qr = (c_q @ W_QR).reshape(B, S, N_HEADS, D_HR).transpose(0, 2, 1, 3)
        Qr = rope(Qr)
        c_kv = x @ W_DKV
        Kc = (c_kv @ W_UK).reshape(B, S, N_HEADS, D_H).transpose(0, 2, 1, 3)
        Kr = rope((x @ W_KR)[:, None, :, :])
        Kr = jnp.broadcast_to(Kr, (B, N_HEADS, S, D_HR))
        V = (c_kv @ W_UV).reshape(B, S, N_HEADS, D_H).transpose(0, 2, 1, 3)
        Q = jnp.concatenate([Qc, Qr], axis=-1)
        K = jnp.concatenate([Kc, Kr], axis=-1)
        scores = jnp.einsum('bhqd,bhkd->bhqk', Q, K)
        scores = jnp.clip(scores, -80.0, 80.0)
        causal = jnp.tril(jnp.ones((S, S), dtype=bool))
        scores = jnp.where(causal, scores, -jnp.inf)
        weights = jax.nn.softmax(scores / jnp.sqrt(jnp.float32(d_qk)), axis=-1)
        attn = jnp.einsum('bhqk,bhkd->bhqd', weights, V)
        attn = attn.transpose(0, 2, 1, 3).reshape(B, S, N_HEADS * D_H)
        return attn @ W_O

    def _L1_xattn_ref(x, memory, seg_ids, Wqkv, bqkv, Wo, bo, Wq_c, Wkv_c, Wo_c, Wg, Wu, Wd, n1, n2, n3, nf):
        import jax, jax.numpy as jnp
        import numpy as np
        N_LAYERS = 4
        H = 16
        LOOKBACK = 128
        EPS = 1e-06
        ROPE_BASE = 10000.0
        NEG = jnp.float32(-1e+30)

        def rmsnorm(x, w):
            return x * jax.lax.rsqrt(jnp.mean(x * x, axis=-1, keepdims=True) + EPS) * w

        def rope_cache(L, hd):
            inv = 1.0 / ROPE_BASE ** (jnp.arange(0, hd, 2, dtype=jnp.float32) / hd)
            t = jnp.arange(L, dtype=jnp.float32)
            f = t[:, None] * inv[None, :]
            emb = jnp.concatenate([f, f], axis=-1)
            return (jnp.cos(emb), jnp.sin(emb))

        def apply_rope(x, cos, sin):
            d = x.shape[-1]
            x1, x2 = (x[..., :d // 2], x[..., d // 2:])
            rot = jnp.concatenate([-x2, x1], axis=-1)
            return x * cos + rot * sin

        def split_heads(x, n_heads):
            B, L, D = x.shape
            return x.reshape(B, L, n_heads, D // n_heads).transpose(0, 2, 1, 3)

        def merge_heads(x):
            B, h, L, d = x.shape
            return x.transpose(0, 2, 1, 3).reshape(B, L, h * d)

        def sdpa(q, k, v, bias):
            scale = q.shape[-1] ** (-0.5)
            s = jnp.einsum('bhqd,bhkd->bhqk', q, k) * scale + bias
            p = jax.nn.softmax(s, axis=-1)
            return jnp.einsum('bhqk,bhkd->bhqd', p, v)

        def forward(x, memory, seg_ids, Wqkv, bqkv, Wo, bo, Wq_c, Wkv_c, Wo_c, Wg, Wu, Wd, n1, n2, n3, nf):
            B, L, D = x.shape
            S = memory.shape[1]
            hd = D // H
            cos, sin = rope_cache(L, hd)
            i = jnp.arange(L)
            causal_bias = jnp.where(i[None, :] <= i[:, None], 0.0, NEG)[None, None]
            j = jnp.arange(S)
            allowed = (j[None, None, :] <= seg_ids[:, :, None]) & (j[None, None, :] > seg_ids[:, :, None] - LOOKBACK)
            cross_bias = jnp.where(allowed, 0.0, NEG)[:, None]
            for l in range(N_LAYERS):
                h = rmsnorm(x, n1[l])
                qkv = h @ Wqkv[l].T + bqkv[l]
                q, k, v = jnp.split(qkv, 3, axis=-1)
                q = apply_rope(split_heads(q, H), cos, sin)
                k = apply_rope(split_heads(k, H), cos, sin)
                v = split_heads(v, H)
                o = merge_heads(sdpa(q, k, v, causal_bias)) @ Wo[l].T + bo[l]
                x = x + o
                h2 = rmsnorm(x, n2[l])
                qc = split_heads(h2 @ Wq_c[l].T, H)
                kv = memory @ Wkv_c[l].T
                kc, vc = jnp.split(kv, 2, axis=-1)
                kc, vc = (split_heads(kc, H), split_heads(vc, H))
                oc = merge_heads(sdpa(qc, kc, vc, cross_bias)) @ Wo_c[l].T
                x = x + oc
                h3 = rmsnorm(x, n3[l])
                x = x + jax.nn.silu(h3 @ Wg[l].T) * (h3 @ Wu[l].T) @ Wd[l].T
            return rmsnorm(x, nf)
        return forward(x, memory, seg_ids, Wqkv, bqkv, Wo, bo, Wq_c, Wkv_c, Wo_c, Wg, Wu, Wd, n1, n2, n3, nf)

    def _L1_ffn_ref(x, Wr, Wg, Wu, Wd):
        import jax, jax.numpy as jnp
        import numpy as np
        B, L, D, E, K, DFF = (2, 256, 128, 8, 2, 512)
        Bb, Ll, Dd = x.shape
        T = Bb * Ll
        xt = x.reshape(T, Dd)
        logits = jnp.einsum('td,ed->te', xt, Wr)
        scores = jax.nn.softmax(logits, axis=-1)
        k_scores, k_ids = jax.lax.top_k(scores, K)
        eps = jnp.finfo(x.dtype).eps
        k_w = k_scores / (k_scores.sum(axis=-1, keepdims=True) + eps)
        combine = jnp.sum(jax.nn.one_hot(k_ids, E, dtype=x.dtype) * k_w[..., None], axis=1)
        g = jnp.einsum('td,efd->etf', xt, Wg)
        u = jnp.einsum('td,efd->etf', xt, Wu)
        h = jax.nn.relu(g) * u
        out_e = jnp.einsum('etf,edf->etd', h, Wd)
        out = jnp.einsum('te,etd->td', combine, out_e)
        return out.reshape(Bb, Ll, Dd)

    def _L2_attn_ref(x, Wq, Wk, Wv, Wo):
        import jax, jax.numpy as jnp
        import numpy as np
        EMB = 128
        HEADS = 16
        HEAD_DIM = EMB // HEADS
        ROPE_BASE = 10000.0

        def rotate_half(x):
            x1 = x[..., ::2]
            x2 = x[..., 1::2]
            return jnp.stack((-x2, x1), axis=-1).reshape(x.shape)

        def rope_cos_sin(seq_len, head_dim):
            inv_freq = 1.0 / ROPE_BASE ** (jnp.arange(0, head_dim, 2, dtype=jnp.float32) / head_dim)
            pos = jnp.arange(seq_len, dtype=jnp.float32)
            freqs = jnp.outer(pos, inv_freq)
            emb = jnp.concatenate([freqs, freqs], -1)
            return (jnp.cos(emb)[None, None], jnp.sin(emb)[None, None])
        B, S, E = x.shape

        def shape_heads(t):
            return t.reshape(B, S, HEADS, HEAD_DIM).transpose(0, 2, 1, 3)
        q = shape_heads(x @ Wq.T)
        k = shape_heads(x @ Wk.T)
        v = shape_heads(x @ Wv.T)
        cos, sin = rope_cos_sin(S, HEAD_DIM)
        q = q * cos + rotate_half(q) * sin
        k = k * cos + rotate_half(k) * sin
        scale = HEAD_DIM ** (-0.5)
        scores = jnp.einsum('bhqd,bhkd->bhqk', q, k) * scale
        causal = jnp.triu(jnp.ones((S, S), dtype=bool), k=1)
        scores = jnp.where(causal, -jnp.inf, scores)
        attn = jax.nn.softmax(scores, axis=-1)
        out = jnp.einsum('bhqk,bhkd->bhqd', attn, v)
        out = out.transpose(0, 2, 1, 3).reshape(B, S, E)
        return out @ Wo.T

    def _L2_xattn_ref(query, key, value, qpos, kpos, q1_w, q2_w, kv1_w, kv2_w, proj_w, proj_b, norm_w, lambda_1, lambda_2):
        import jax, jax.numpy as jnp
        import numpy as np
        DIM = 128
        H = 16
        HD = DIM // H
        SCALE = HD ** (-0.5)
        LAMBDA_INIT = 0.1
        EPS = 1e-06

        def _split_heads(x, B, N):
            return x.reshape(B, N, H, HD).transpose(0, 2, 1, 3)
        B, Nq, C = query.shape
        Nk = key.shape[1]
        q1 = _split_heads(query @ q1_w.T, B, Nq)
        q2 = _split_heads(query @ q2_w.T, B, Nq)
        kv1 = (key @ kv1_w.T).reshape(B, Nk, 2, H, HD).transpose(2, 0, 3, 1, 4)
        k1, v1 = (kv1[0], kv1[1])
        kv2 = (key @ kv2_w.T).reshape(B, Nk, 2, H, HD).transpose(2, 0, 3, 1, 4)
        k2 = kv2[0]
        attn1 = jax.nn.softmax(jnp.einsum('bhqd,bhkd->bhqk', q1, k1) * SCALE, axis=-1)
        attn2 = jax.nn.softmax(jnp.einsum('bhqd,bhkd->bhqk', q2, k2) * SCALE, axis=-1)
        lambda_full = lambda_1 - lambda_2 + LAMBDA_INIT
        diff_attn = attn1 - lambda_full * attn2
        x = jnp.einsum('bhqk,bhkd->bhqd', diff_attn, v1)
        x = x.transpose(0, 2, 1, 3).reshape(B, Nq, C)
        xf = x.astype(jnp.float32)
        xf = xf * jax.lax.rsqrt(jnp.mean(xf * xf, axis=-1, keepdims=True) + EPS) * norm_w
        x = xf.astype(x.dtype)
        return x @ proj_w.T + proj_b

    def _L2_ffn_ref(x, W1, b1, W2, b2, Wr, br):
        import jax, jax.numpy as jnp
        import numpy as np
        B, S, D, F, E = (4, 256, 128, 512, 8)
        b, s, d = x.shape
        e = Wr.shape[1]
        logits = x @ Wr + br
        idx = jnp.argmax(logits, axis=-1)
        probs = jax.nn.softmax(logits, axis=-1)
        gates = jnp.take_along_axis(probs, idx[..., None], axis=-1)[..., 0]
        xf = x.reshape(-1, d)
        idxf = idx.reshape(-1)
        gf = gates.reshape(-1)
        out = jnp.zeros_like(xf)
        for ei in range(e):
            h = jax.nn.gelu(xf @ W1[ei] + b1[ei], approximate=False)
            y = h @ W2[ei] + b2[ei]
            mask = (idxf == ei).astype(xf.dtype)
            out = out + y * (gf * mask)[:, None]
        return out.reshape(b, s, d)

    def _L3_attn_ref(x, Wq, bq, Wk, bk, Wv, bv, Wg, bg, gamma):
        import jax, jax.numpy as jnp
        import numpy as np
        import math
        E = 128
        H = 16
        B = 2
        T = 256

        def _rotary(x):
            D = x.shape[-1]
            inv_freq = 1.0 / 10000.0 ** (jnp.arange(0, D, 2, dtype=jnp.float32) / D)
            t = jnp.arange(x.shape[-2], dtype=jnp.float32)
            freqs = t[:, None] * inv_freq[None, :]
            emb = jnp.concatenate([freqs, freqs], axis=-1)
            cos = jnp.cos(emb)
            sin = jnp.sin(emb)
            x1 = x[..., ::2]
            x2 = x[..., 1::2]
            x_rot = jnp.stack([-x2, x1], axis=-1).reshape(x.shape)
            return x * cos + x_rot * sin
        Bb, Tt, Ee = x.shape
        Hh = gamma.shape[0]
        Dd = Ee // Hh

        def proj(W, b):
            return (x @ W.T + b).reshape(Bb, Tt, Hh, Dd).transpose(0, 2, 1, 3)
        Q = _rotary(proj(Wq, bq))
        K = _rotary(proj(Wk, bk))
        V = proj(Wv, bv)
        g = jax.nn.sigmoid(gamma)
        idx = jnp.arange(Tt)
        diff = jnp.clip(idx[:, None] - idx[None, :], 0, None).astype(jnp.float32)
        t_w = jnp.exp(-g[:, None, None] * diff)
        scores = jnp.einsum('bhtd,bhsd->bhts', Q, K) / math.sqrt(Dd)
        out = jnp.einsum('bhts,bhsd->bhtd', scores * t_w[None], V)
        out = out.transpose(0, 2, 1, 3).reshape(Bb, Tt, Ee)
        gate = jax.nn.silu(x @ Wg.T + bg)
        return gate * out

    def _L3_xattn_ref(q, k, v, w_qs, w_ks, w_vs, w_proj, b_proj):
        import jax, jax.numpy as jnp
        import numpy as np
        B, L, D_MODEL = (2, 256, 128)
        N_HEADS, D_K = (16, 64)
        qh = jnp.einsum('bld,hdk->hblk', q, w_qs)
        kh = jnp.einsum('bld,hdk->hblk', k, w_ks)
        vh = jnp.einsum('bld,hdk->hblk', v, w_vs)
        attn = jax.nn.softmax(jnp.einsum('hblk,hbmk->hblm', qh, kh), axis=-1)
        out = jnp.einsum('hblm,hbmk->hblk', attn, vh) * qh
        out = out.transpose(1, 2, 0, 3).reshape(q.shape[0], q.shape[1], -1)
        return out @ w_proj.T + b_proj

    def _L3_ffn_ref(x, router_w, router_b, w1, b1, w2, b2):
        import jax, jax.numpy as jnp
        import numpy as np
        D_MODEL = 128
        D_FF = 512
        N_EXPERTS = 8
        TOP_K = 2
        B, S = (4, 256)
        Bx, Sx, D = x.shape
        E = router_b.shape[0]
        xf = x.reshape(-1, D)
        logits = xf @ router_w.T + router_b
        probs = jax.nn.softmax(logits, axis=-1)
        topk_w, topk_idx = jax.lax.top_k(probs, TOP_K)
        topk_w = topk_w / jnp.sum(topk_w, axis=-1, keepdims=True)
        onehot = jax.nn.one_hot(topk_idx, E, dtype=xf.dtype)
        w_dense = jnp.einsum('tke,tk->te', onehot, topk_w)
        out = jnp.zeros_like(xf)
        for e in range(E):
            h = jax.nn.gelu(xf @ w1[e].T + b1[e], approximate=False)
            out = out + w_dense[:, e:e + 1] * (h @ w2[e].T + b2[e])
        return out.reshape(Bx, Sx, D)
    x = x + _L0_attn_ref(_layernorm(x, axis=-1), L0_attn_Wv, L0_attn_bv, L0_attn_Wg, L0_attn_bg, L0_attn_Win, L0_attn_bin_, L0_attn_Wout, L0_attn_bout, L0_attn_g_qq, L0_attn_b_qq, L0_attn_g_qk, L0_attn_b_qk, L0_attn_g_lq, L0_attn_b_lq, L0_attn_g_lk, L0_attn_b_lk)
    x = x + _L0_xattn_ref(_layernorm(x, axis=-1), ctx_1024, mask_BxS2_ff1, L0_xattn_Wq, L0_xattn_bq, L0_xattn_Wk, L0_xattn_bk, L0_xattn_Wv, L0_xattn_bv, L0_xattn_Wo, L0_xattn_bo)
    x = x + _L0_ffn_ref(_layernorm(x, axis=-1), L0_ffn_w_gate, L0_ffn_w_up, L0_ffn_w_down)
    x = x + _L1_attn_ref(_layernorm(x, axis=-1), L1_attn_W_DQ, L1_attn_W_UQ, L1_attn_W_QR, L1_attn_W_DKV, L1_attn_W_UK, L1_attn_W_UV, L1_attn_W_KR, L1_attn_W_O)
    x = x + _L1_xattn_ref(_layernorm(x, axis=-1), ctx_1024, itok_BxS_0_255, L1_xattn_Wqkv, L1_xattn_bqkv, L1_xattn_Wo, L1_xattn_bo, L1_xattn_Wq_c, L1_xattn_Wkv_c, L1_xattn_Wo_c, L1_xattn_Wg, L1_xattn_Wu, L1_xattn_Wd, L1_xattn_n1, L1_xattn_n2, L1_xattn_n3, L1_xattn_nf)
    x = x + _L1_ffn_ref(_layernorm(x, axis=-1), L1_ffn_Wr, L1_ffn_Wg, L1_ffn_Wu, L1_ffn_Wd)
    x = x + _L2_attn_ref(_layernorm(x, axis=-1), L2_attn_Wq, L2_attn_Wk, L2_attn_Wv, L2_attn_Wo)
    x = x + _L2_xattn_ref(_layernorm(x, axis=-1), ctx_1024, ctx_1024, itok_BxS_0_1023, itok_BxS2_0_2047, L2_xattn_q1_w, L2_xattn_q2_w, L2_xattn_kv1_w, L2_xattn_kv2_w, L2_xattn_proj_w, L2_xattn_proj_b, L2_xattn_norm_w, L2_xattn_lambda_1, L2_xattn_lambda_2)
    x = x + _L2_ffn_ref(_layernorm(x, axis=-1), L2_ffn_W1, L2_ffn_b1, L2_ffn_W2, L2_ffn_b2, L2_ffn_Wr, L2_ffn_br)
    x = x + _L3_attn_ref(_layernorm(x, axis=-1), L3_attn_Wq, L3_attn_bq, L3_attn_Wk, L3_attn_bk, L3_attn_Wv, L3_attn_bv, L3_attn_Wg, L3_attn_bg, L3_attn_gamma)
    x = x + _L3_xattn_ref(_layernorm(x, axis=-1), ctx_1024, ctx_1024, L3_xattn_w_qs, L3_xattn_w_ks, L3_xattn_w_vs, L3_xattn_w_proj, L3_xattn_b_proj)
    x = x + _L3_ffn_ref(_layernorm(x, axis=-1), L3_ffn_router_w, L3_ffn_router_b, L3_ffn_w1, L3_ffn_b1, L3_ffn_w2, L3_ffn_b2)
    return x

_drawn_inputs = setup_inputs


def setup_inputs(seed=0):
    import zlib

    import numpy as np

    out = dict(_drawn_inputs(seed))
    spreads = {'L0_attn_bv': (0.0, 0.1),
     'L0_attn_bg': (0.0, 0.1),
     'L0_attn_bin_': (0.0, 0.1),
     'L0_attn_bout': (0.0, 0.1),
     'L0_attn_b_qq': (0.0, 0.8),
     'L0_attn_b_qk': (0.0, 0.8),
     'L0_attn_b_lq': (0.0, 0.333),
     'L0_attn_b_lk': (0.0, 0.1),
     'L0_xattn_bq': (0.0, 0.1),
     'L0_xattn_bk': (0.0, 2.0),
     'L0_xattn_bv': (0.0, 0.1),
     'L0_xattn_bo': (0.0, 0.1),
     'L1_xattn_bqkv': (0.0, 0.1),
     'L1_xattn_bo': (0.0, 0.1),
     'L1_xattn_n1': (1.0, 0.6),
     'L1_xattn_n2': (1.0, 0.6),
     'L1_xattn_n3': (1.0, 0.6),
     'L1_xattn_nf': (1.0, 0.2),
     'L2_xattn_proj_b': (0.0, 0.563),
     'L2_xattn_norm_w': (1.0, 0.6),
     'L2_xattn_lambda_1': (1.0, 0.6),
     'L2_xattn_lambda_2': (0.9916666746139526, 0.6),
     'L3_attn_bq': (0.0, 1.137),
     'L3_attn_bk': (0.0, 0.477),
     'L3_attn_bv': (0.0, 0.408),
     'L3_attn_bg': (0.0, 0.8),
     'L3_xattn_b_proj': (0.0, 2.0),
     'L3_ffn_router_b': (0.0, 1.166),
     'L3_ffn_b1': (0.0, 2.0),
     'L3_ffn_b2': (0.0, 2.0)}
    factors = {'L0_attn_g_qq': 8.0,
     'L0_attn_g_qk': 8.0,
     'L0_attn_g_lq': 8.0,
     'L0_attn_g_lk': 8.0,
     'L0_ffn_w_gate': 4.215,
     'L0_ffn_w_up': 3.89,
     'L0_ffn_w_down': 3.937,
     'L1_xattn_Wq_c': 8.0,
     'L1_xattn_Wg': 3.221,
     'L1_xattn_Wu': 3.186,
     'L1_xattn_Wd': 3.126,
     'L1_ffn_Wr': 7.807,
     'L1_ffn_Wg': 8.0,
     'L1_ffn_Wu': 6.933,
     'L1_ffn_Wd': 6.975,
     'L2_xattn_q1_w': 57.622,
     'L2_xattn_q2_w': 30.2,
     'L2_xattn_kv2_w': 28.746,
     'L2_ffn_b1': 64.0,
     'L2_ffn_b2': 44.279,
     'L2_ffn_br': 33.773,
     'L3_attn_gamma': 64.0,
     'L3_ffn_w1': 17.848,
     'L3_ffn_w2': 11.726,
     'L2_ffn_W1': 5.552,
     'L2_ffn_W2': 5.181,
     'L2_ffn_Wr': 4.476,
     'L3_attn_Wq': 4.43,
     'L3_attn_Wk': 4.845,
     'L3_attn_Wv': 3.652,
     'L3_attn_Wg': 2.797,
     'L3_ffn_router_w': 4.811}
    for name, (base, spread) in spreads.items():
        noise = np.random.default_rng([zlib.crc32(name.encode()), seed]).standard_normal(out[name].shape)
        drawn = base * np.exp(spread * noise) if base else spread * noise
        out[name] = jnp.asarray(drawn.astype(out[name].dtype))
    for name, factor in factors.items():
        out[name] = (out[name] * factor).astype(out[name].dtype)
    return out
```

```python
import math
from contextlib import ExitStack, contextmanager

import numpy as np

import concourse.bass as bass
from concourse import mybir
from concourse.alu_op_type import AluOpType as ALU

F32 = mybir.dt.float32
BF16 = mybir.dt.bfloat16
I32 = mybir.dt.int32
U32 = mybir.dt.uint32
ACT = mybir.ActivationFunctionType
AX = mybir.AxisListType

B, S, D = 4, 256, 128
P = 128
NT = B * S // P
HALVES = S // P
SC = 64
H, HD = 16, 8
ROWG = 4
CH = 512
NCH = B * S // CH
NEG = -1e30
LAYERS = 4
E, F = 8, 512
FK = F // P
DK3 = 64
NF0 = 352
FT0 = [(0, 128), (128, 128), (256, 96)]
MIDS = [0.25, 0.75, 1.25, 1.75, 2.5, 3.5, 5.0]
GROUP = 32
INNER = 256


def constant_arrays():
    p = np.arange(P)
    c = {"ident": np.eye(P, dtype=np.float32)}
    half = np.zeros((P, P), np.float32)
    inter = np.zeros((P, P), np.float32)
    for m in range(P):
        d = m % HD
        if d < HD // 2:
            half[m + HD // 2, m] = -1.0
        else:
            half[m - HD // 2, m] = 1.0
        if m % 2 == 0:
            inter[m + 1, m] = -1.0
        else:
            inter[m - 1, m] = 1.0
    c["rot_half"], c["rot_inter"] = half, inter
    t = np.arange(S, dtype=np.float32)
    inv8 = (1.0 / np.float32(10000.0) ** (np.arange(0, HD, 2, dtype=np.float32) / np.float32(HD))).astype(np.float32)
    ang8 = inv8[(p % HD) % (HD // 2)][:, None] * t[None]
    inv4 = (np.float32(10000.0) ** (-np.arange(0, 4, 2, dtype=np.float32) / np.float32(4))).astype(np.float32)
    ang4 = inv4[(p % 4) // 2][:, None] * t[None]
    c["cos8"], c["sin8"], c["cos4"], c["sin4"] = np.cos(ang8), np.sin(ang8), np.cos(ang4), np.sin(ang4)
    c["mask8"] = np.stack([(p % 32) // 8 == j for j in range(4)], 1)
    c["mask16"] = np.stack([p // 8 == h for h in range(H)], 1)
    c["mask4"] = np.stack([(p % 32) // 4 == j for j in range(4)], 1)
    c["causal_neg"] = np.where(p[None] <= p[:, None], 0.0, NEG)
    c["causal_one"] = (p[:, None] <= p[None]).astype(np.float32)
    q, k = np.arange(S)[None], np.arange(S)[:, None]
    in_chunk = (q // GROUP == k // GROUP) & (k <= q)
    two = lambda a: np.concatenate([a[:P], a[P:]], 1).astype(np.float32)
    c["in_chunk"] = two(in_chunk)
    c["older_chunk"] = two(k // GROUP < q // GROUP)
    c["distance"] = two(np.maximum(q - k, 0))
    c["iota8"] = np.tile(np.arange(E), (P, 1))
    c["keys"] = np.tile(np.arange(SC), (P, 1))
    c["minus_half"] = np.full((P, NT), -0.5)
    c["ones_row"] = np.ones((1, P))
    return {k: np.asarray(v, np.float32) for k, v in c.items()}


def tiles(a):
    k = a.shape[0] // P
    return a.reshape(k, P, -1).transpose(1, 0, 2).reshape(P, -1)


def col(v):
    v = np.asarray(v)
    return v.reshape(-1, min(P, v.size)).T


def row(v):
    return np.asarray(v).reshape(1, -1)


def spread(v):
    return np.broadcast_to(np.asarray(v).reshape(1, -1), (P, np.asarray(v).size))


def rope_part_columns(w):
    out = np.zeros((w.shape[0], P), w.dtype)
    for h in range(H):
        c = 32 * (h // 4) + 4 * (h % 4)
        out[:, c:c + 4] = w[:, 4 * h:4 * h + 4]
    return out


def stage_arrays(a):
    g = lambda n: np.asarray(a[n])
    ctx = g("ctx_1024")
    ctxT = ctx.transpose(2, 0, 1)
    out = {}
    out["const"] = constant_arrays()
    out["ctx"] = {
        "ctxT": ctxT.reshape(D, B * SC),
        "ctxT2": np.broadcast_to(ctxT[:, :, None], (D, B, 2, SC)).reshape(D, -1),
        "keep": spread(g("mask_BxS2_ff1")),
    }
    out["L0_attn"] = {n: g("L0_attn_" + n) for n in ("Wv", "Wg", "Win")}
    out["L0_attn"].update(
        Wout=tiles(g("L0_attn_Wout")), bv=row(g("L0_attn_bv")), bg=col(g("L0_attn_bg")),
        bin=col(g("L0_attn_bin_")), bout=row(g("L0_attn_bout")),
        **{n: col(g("L0_attn_" + n)) for n in ("g_qq", "b_qq", "g_qk", "b_qk", "g_lq", "b_lq", "g_lk", "b_lk")})
    out["L0_xattn"] = {n: g("L0_xattn_" + n).T for n in ("Wq", "Wk", "Wv", "Wo")}
    out["L0_xattn"].update(bq=col(g("L0_xattn_bq")), bk=col(g("L0_xattn_bk")), bv=row(g("L0_xattn_bv")),
                           bo=row(g("L0_xattn_bo")))
    w0 = {}
    for n in ("w_gate", "w_up"):
        w = g("L0_ffn_" + n)
        for i, (f0, fn) in enumerate(FT0):
            w0[f"{n}{i}"] = w[f0:f0 + fn]
    w0["w_down"] = g("L0_ffn_w_down")
    out["L0_ffn"] = w0
    out["L1_attn"] = {n: g("L1_attn_" + n) for n in ("W_DQ", "W_UQ", "W_DKV", "W_UK", "W_UV", "W_O")}
    out["L1_attn"].update(W_QR=rope_part_columns(g("L1_attn_W_QR")), W_KR=np.tile(g("L1_attn_W_KR"), (1, P // 4)))
    x1 = {n: g("L1_xattn_" + n) for n in ("Wqkv", "bqkv", "Wo", "bo", "Wq_c", "Wkv_c", "Wo_c", "Wg", "Wu", "Wd",
                                           "n1", "n2", "n3")}
    out["inner_attn"] = [
        {"Wq": x1["Wqkv"][l, :D].T, "Wk": x1["Wqkv"][l, D:2 * D].T, "Wv": x1["Wqkv"][l, 2 * D:].T,
         "bq": col(x1["bqkv"][l, :D]), "bk": col(x1["bqkv"][l, D:2 * D]), "bv": row(x1["bqkv"][l, 2 * D:]),
         "Wo": x1["Wo"][l].T, "bo": row(x1["bo"][l]), "Wq_c": x1["Wq_c"][l].T, "Wk_c": x1["Wkv_c"][l, :D].T,
         "Wv_c": x1["Wkv_c"][l, D:].T, "Wo_c": x1["Wo_c"][l].T, "n1": col(x1["n1"][l]), "n2": col(x1["n2"][l])}
        for l in [*range(LAYERS), 0]]
    out["inner_ffn"] = [
        {"Wg": x1["Wg"][l].T, "Wu": x1["Wu"][l].T, "Wd": tiles(x1["Wd"][l].T), "n3": col(x1["n3"][l])}
        for l in range(LAYERS)]
    out["inner_misc"] = {"nf": spread(g("L1_xattn_nf"))}
    out["L1_ffn"] = {"Wr": g("L1_ffn_Wr").T}
    out["L1_experts"] = [{"Wg": g("L1_ffn_Wg")[e].T, "Wu": g("L1_ffn_Wu")[e].T, "Wd": tiles(g("L1_ffn_Wd")[e].T)}
                         for e in [*range(E), 0]]
    out["L2_attn"] = {n: g("L2_attn_" + n).T for n in ("Wq", "Wk", "Wv", "Wo")}
    kv1, kv2 = g("L2_xattn_kv1_w"), g("L2_xattn_kv2_w")
    out["L2_xattn"] = {
        "q1": g("L2_xattn_q1_w").T, "q2": g("L2_xattn_q2_w").T, "k1": kv1[:D].T, "v1": kv1[D:].T, "k2": kv2[:D].T,
        "proj": g("L2_xattn_proj_w").T, "b": row(g("L2_xattn_proj_b")), "norm": col(g("L2_xattn_norm_w")),
        "l1": spread(g("L2_xattn_lambda_1")), "l2": spread(g("L2_xattn_lambda_2"))}
    out["L2_ffn"] = {"Wr": g("L2_ffn_Wr"), "br": row(g("L2_ffn_br")), "b2": g("L2_ffn_b2")}
    out["L2_experts"] = [{"W1": g("L2_ffn_W1")[e], "b1": col(g("L2_ffn_b1")[e]), "W2": tiles(g("L2_ffn_W2")[e])}
                         for e in [*range(E), 0]]
    out["L3_attn"] = {n: g("L3_attn_" + n).T for n in ("Wq", "Wk", "Wv", "Wg")}
    out["L3_attn"].update(bq=col(g("L3_attn_bq")), bk=col(g("L3_attn_bk")), bv=row(g("L3_attn_bv")),
                          bg=row(g("L3_attn_bg")), gamma=spread(g("L3_attn_gamma")))
    heads = lambda w: g(w).transpose(1, 0, 2).reshape(D, H * DK3)
    out["L3_xattn"] = {"Wq": heads("L3_xattn_w_qs"), "Wk": heads("L3_xattn_w_ks"), "Wv": heads("L3_xattn_w_vs"),
                       "proj": tiles(g("L3_xattn_w_proj").T), "b": row(g("L3_xattn_b_proj"))}
    out["L3_ffn"] = {"Wr": g("L3_ffn_router_w").T, "br": row(g("L3_ffn_router_b")), "b2": g("L3_ffn_b2")}
    out["L3_experts"] = [{"W1": g("L3_ffn_w1")[e].T, "b1": col(g("L3_ffn_b1")[e]), "W2": tiles(g("L3_ffn_w2")[e].T)}
                         for e in [*range(E), 0]]
    return out


def layout_of(arrays):
    at, where = 0, {}
    for name, v in arrays.items():
        where[name] = (v.shape[0], at, v.shape[1])
        at += v.shape[1]
    return where, at


def pack(arrays, where, width):
    out = np.zeros((P, width), np.float32)
    for name, v in arrays.items():
        p, at, n = where[name]
        out[:p, at:at + n] = v
    return out


class Pack:

    def __init__(self, buf, where):
        self.buf, self.where = buf, where

    def __getitem__(self, name):
        p, at, n = self.where[name]
        return self.buf[0:p, at:at + n]


class Phase:

    def __init__(self, nc):
        self.nc, self.sems = nc, []

    def sem(self, name):
        s = self.nc.alloc_semaphore(f"{name}_{self.nc.next_id()}")
        self.sems.append(s)
        return s

    def __enter__(self):
        return self

    def __exit__(self, kind, *_):
        if kind is None:
            self.nc.clear_and_free_semaphores(self.sems)
            self.nc.all_engine_barrier()


def link(eng, sem, count, ins):
    count[0] += 1
    ins.then_inc(sem, 1)
    eng.wait_ge(sem, count[0])


class Kernel:
    def __init__(self, nc, dram, where, x_dram, out_dram, seg_dram):
        self.nc, self.dram, self.where = nc, dram, where
        self.x_dram, self.out_dram, self.seg_dram = x_dram, out_dram, seg_dram
        self.stack = ExitStack()

    def sb(self, name, shape, dt=F32):
        return self.nc.sbuf_tensor(f"{name}_{self.nc.next_id()}", shape, dt)

    def keep(self, name, shape, dt=F32):
        return self.stack.enter_context(self.sb(name, shape, dt))

    def bank(self, n, count=1):
        return self.ps[:, n * CH:(n + count) * CH]

    def start(self):
        nc = self.nc
        self.s_out = nc.alloc_semaphore("output_written")
        self.ps = self.stack.enter_context(nc.psum_tensor("ps", [P, 8 * CH], F32))
        self.x = self.keep("x", [P, NT, D])
        self.xT = self.keep("xT", [P, NT * P])
        self.nrm = self.keep("nrm", [P, NT, D])
        cwhere, cwidth = self.where["const"]
        xwhere, xwidth = self.where["ctx"]
        cbuf = self.keep("constants", [P, cwidth])
        xbuf = self.keep("context", [P, xwidth])
        self.c, self.ctx = Pack(cbuf, cwhere), Pack(xbuf, xwhere)
        self.identb = self.keep("identb", [P, P], BF16)
        self.causalb = self.keep("causalb", [P, P], BF16)
        self.keepb = self.keep("keepb", [P, B, SC], BF16)
        self.tmp_keep = self.keep("tmp_keep", [P, B * SC])
        with Phase(nc) as ph:
            s_load, s_cast, s_mul = ph.sem("load"), ph.sem("cast"), ph.sem("mul")
            with nc.Block() as block:
                @block.sync
                def _(sp):
                    sp.dma_start(self.x[:, :, :], self.x_dram.rearrange("b (h p) d -> p (b h) d", p=P)).then_inc(s_load, 16)
                    sp.dma_start(xbuf[:, :], self.dram["ctx"][:, :]).then_inc(s_load, 16)
                    sp.dma_start(cbuf[:, :], self.dram["const"][:, :]).then_inc(s_load, 16)
                    sp.wait_ge(s_load, 48)

                @block.vector
                def _(dve):
                    dve.wait_ge(s_load, 48)
                    dve.tensor_copy(self.identb[:, :], self.c["ident"]).then_inc(s_cast, 1)
                    dve.tensor_copy(self.causalb[:, :], self.c["causal_neg"]).then_inc(s_cast, 1)
                    dve.tensor_scalar(self.tmp_keep[:, :], self.ctx["keep"], 1.0, NEG, ALU.not_equal, ALU.mult).then_inc(s_mul, 1)
                    dve.wait_ge(s_mul, 1)
                    dve.tensor_copy(self.keepb[:, :, :], self.tmp_keep[:, :].rearrange("p (b k) -> p b k", b=B)).then_inc(s_cast, 1)
                    dve.wait_ge(s_cast, 3)

    def finish(self):
        nc = self.nc
        s_out = self.s_out
        with nc.Block() as block:
                @block.sync
                def _(sp):
                    sp.dma_start(self.out_dram.rearrange("b (h p) d -> p (b h) d", p=P), self.x[:, :, :]).then_inc(s_out, 16)
                    sp.wait_ge(s_out, 16)
        self.stack.close()

    @contextmanager
    def weights(self, stage):
        where, width = self.where[stage]
        with self.sb("w_" + stage, [P, width]) as buf:
            with Phase(self.nc) as ph:
                s_w = ph.sem("weights")
                with self.nc.Block() as block:
                    @block.sync
                    def _(sp):
                        sp.dma_start(buf[:, :], self.dram[stage][:, :]).then_inc(s_w, 16)
                        sp.wait_ge(s_w, 16)
            yield Pack(buf, where)

    def norm(self, src, dst, dstT, layer=True, eps=1e-5, weight=None):
        nc = self.nc
        with self.sb("stats", [P, NT, 6]) as stats, self.sb("mv", [P, NT, 2]) as mv, \
                self.sb("var", [P, NT]) as var, self.sb("rstd", [P, NT]) as rstd, self.sb("sq", [P, NT, D]) as sq, Phase(nc) as ph:
            s_chain, s_var, s_rstd = ph.sem("chain"), ph.sem("var"), ph.sem("rstd")
            s_norm, s_turn, s_copy = ph.sem("norm"), ph.sem("turn"), ph.sem("copy")
            with nc.Block() as block:
                @block.vector
                def _(dve):
                    n = [0]
                    if layer:
                        for t in range(NT):
                            dve.bn_stats(stats[:, t, :], src[:, t, :]).then_inc(s_chain, 1)
                        dve.wait_ge(s_chain, NT)
                        for t in range(NT):
                            dve.bn_aggr(mv[:, t, :], stats[:, t, :]).then_inc(s_chain, 1)
                        dve.wait_ge(s_chain, 2 * NT)
                        dve.tensor_scalar(var[:, :], mv[:, :, 1], eps, None, ALU.add).then_inc(s_var, 1)
                    else:
                        dve.tensor_tensor(sq[:, :, :], src[:, :, :], src[:, :, :], ALU.mult).then_inc(s_chain, 1)
                        dve.wait_ge(s_chain, 1)
                        dve.tensor_reduce(rstd[:, :], sq[:, :, :], AX.X, ALU.add).then_inc(s_chain, 1)
                        dve.wait_ge(s_chain, 2)
                        dve.tensor_scalar(var[:, :], rstd[:, :], 1.0 / D, eps, ALU.mult, ALU.add).then_inc(s_var, 1)
                    dve.wait_ge(s_rstd, 1)
                    for t in range(NT):
                        if layer:
                            ins = dve.tensor_scalar(dst[:, t, :], src[:, t, :], mv[:, t, 0:1], rstd[:, t:t + 1],
                                                    ALU.subtract, ALU.mult)
                        else:
                            ins = dve.tensor_scalar(dst[:, t, :], src[:, t, :], rstd[:, t:t + 1], None, ALU.mult)
                        ins.then_inc(s_norm, 1)

                @block.gpsimd
                def _(pool):
                    pool.wait_ge(s_var, 1)
                    pool.tensor_tensor(rstd[:, :], var[:, :], self.c["minus_half"], ALU.pow).then_inc(s_rstd, 1)

                if dstT is not None:
                    @block.tensor
                    def _(pe):
                        for t in range(NT):
                            pe.wait_ge(s_norm, t + 1)
                            pe.transpose(self.ps[:, t * P:(t + 1) * P], dst[:, t, :], self.c["ident"]).then_inc(s_turn, 1)

                    @block.scalar
                    def _(act):
                        for g in range(NCH):
                            act.wait_ge(s_turn, (g + 1) * NT // NCH)
                            cols = slice(g * CH, (g + 1) * CH)
                            if weight is None:
                                act.activation(dstT[:, cols], self.ps[:, cols], ACT.Copy).then_inc(s_copy, 1)
                            else:
                                act.activation(dstT[:, cols], self.ps[:, cols], ACT.Copy, scale=weight).then_inc(s_copy, 1)

    def products(self, jobs):
        nc = self.nc
        R = 8
        engine = [ev[0] for _, ev, _ in jobs]
        nth = [engine[:n + 1].count(engine[n]) for n in range(len(jobs))]
        with Phase(nc) as ph:
            s_product = ph.sem("product")
            s_taken = {"act": ph.sem("taken_act"), "dve": ph.sem("taken_dve")}
            s_chain = ph.sem("chain")
            with nc.Block() as block:
                @block.tensor
                def _(pe):
                    for n, (mms, ev, after) in enumerate(jobs):
                        if n >= R:
                            pe.wait_ge(s_taken[engine[n - R]], nth[n - R])
                        if after is not None:
                            pe.wait_ge(s_taken[engine[after]], nth[after])
                        bank = self.bank(n % R)
                        for c0, c1, rows, lhsT, rhs, start, stop in mms:
                            last = pe.matmul(bank[0:rows, c0:c1], lhsT, rhs, start=start, stop=stop)
                        last.then_inc(s_product, 1)

                @block.scalar
                def _(act):
                    for n, (_, ev, _) in enumerate(jobs):
                        if ev[0] != "act":
                            continue
                        act.wait_ge(s_product, n + 1)
                        _, func, dst, pick, bias, scale = ev
                        src = pick(self.bank(n % R))
                        act.activation(dst, src, func, bias=bias, scale=scale).then_inc(s_taken["act"], 1)

                @block.vector
                def _(dve):
                    chain = [0]
                    for n, (_, ev, _) in enumerate(jobs):
                        if ev[0] != "dve":
                            continue
                        dve.wait_ge(s_product, n + 1)
                        kind, dst, pick = ev[1:4]
                        src = pick(self.bank(n % R))
                        if kind == "copy":
                            ins = dve.tensor_copy(dst, src)
                        elif kind == "affine":
                            ins = dve.tensor_scalar(dst, src, ev[4], ev[5], ALU.add, ALU.mult)
                        elif kind == "mult":
                            if len(ev) > 5:
                                dve.wait_ge(s_taken["act"], nth[ev[5]])
                            ins = dve.tensor_tensor(dst, src, ev[4], ALU.mult)
                        elif kind == "add":
                            ins = dve.tensor_tensor(dst, src, ev[4], ALU.add)
                        elif kind == "rope":
                            raw, cos, sin = ev[4:7]
                            link(dve, s_chain, chain, dve.tensor_tensor(dst, raw, cos, ALU.mult))
                            link(dve, s_chain, chain, dve.tensor_tensor(raw, src, sin, ALU.mult))
                            ins = dve.tensor_tensor(dst, dst, raw, ALU.add)
                        ins.then_inc(s_taken["dve"], 1)

    @staticmethod
    def whole(rows=P, cols=CH):
        return lambda bank: bank[0:rows, 0:cols]

    @staticmethod
    def rows_of_heads(width):
        return lambda bank: bank[:, :].rearrange("p (t h d) -> p t h d", h=H, d=HD)

    def turned(self, W, src, dst, m=P, bias=0.0, scale=1.0, func=ACT.Identity, eng="act", width=B * S):
        jobs = []
        step = min(CH, width)
        for c in range(0, width, step):
            cols = slice(c, c + step)
            mms = [(0, step, m, W, src[:, cols], True, True)]
            pick = self.whole(m, step)
            if eng == "act":
                jobs.append((mms, ("act", func, dst[:, cols], pick, bias, scale), None))
            elif isinstance(bias, float):
                jobs.append((mms, ("dve", "copy", dst[:, cols], pick), None))
            else:
                jobs.append((mms, ("dve", "affine", dst[:, cols], pick, bias, scale), None))
        return jobs

    def roped(self, jobs, W, src, dst, raw, rot, cos, sin, bias=0.0):
        first = len(jobs)
        jobs += self.turned(W, src, raw, bias=bias)
        for c in range(NCH):
            cols = slice(c * CH, (c + 1) * CH)
            two = lambda a: a.unsqueeze(1).to_broadcast([P, CH // S, S])
            v = lambda a: a.rearrange("p (b s) -> p b s", s=S)
            jobs.append(([(0, CH, P, rot, raw[:, cols], True, True)],
                         ("dve", "rope", v(dst[:, cols]), (lambda bank: v(bank[:, :])), v(raw[:, cols]), two(cos), two(sin)),
                         first + c))

    def value_rows(self, W, src, dst, bias=None, n=NT, k=P):
        jobs = []
        for g in range(0, n, 4):
            mms = []
            for t in range(g, min(g + 4, n)):
                c = (t - g) * P
                mms.append((c, c + P, P, src[0:k, t * P:(t + 1) * P], W, True, bias is None))
                if bias is not None:
                    mms.append((c, c + P, P, self.c["ones_row"], bias, False, True))
            jobs.append((mms, ("dve", "copy", dst[:, g:min(g + 4, n), :, 0:HD], self.rows_of_heads(n)), None))
        return jobs

    def expand(self, src, dst, mask, width):
        nc = self.nc
        with Phase(nc) as ph:
            s_a, s_v, s_p = ph.sem("expand_act"), ph.sem("expand_dve"), ph.sem("expand_pool")
            with nc.Block() as block:
                @block.scalar
                def _(act):
                    for j in (0,):
                        act.activation(dst[:, j, :], src[:, 0:width], ACT.Copy, scale=mask[:, j:j + 1]).then_inc(s_a, 1)

                @block.vector
                def _(dve):
                    for j in (1, 2):
                        dve.tensor_scalar(dst[:, j, :], src[:, 0:width], mask[:, j:j + 1], None, ALU.mult).then_inc(s_v, 1)

                @block.gpsimd
                def _(pool):
                    for j in (3,):
                        pool.tensor_scalar(dst[:, j, :], src[:, 0:width], mask[:, j:j + 1], None, ALU.mult).then_inc(s_p, 1)

    def expand_context(self, src, dst):
        nc = self.nc
        mask = self.c["mask16"]
        with Phase(nc) as ph:
            s_a, s_v, s_p = ph.sem("expand_act"), ph.sem("expand_dve"), ph.sem("expand_pool")

            def part(eng, hs):
                k = hs.stop - hs.start
                return eng.tensor_tensor(dst[:, hs, :], src[:, :].unsqueeze(1).to_broadcast([P, k, B * SC]),
                                         mask[:, hs].unsqueeze(2).to_broadcast([P, k, B * SC]), ALU.mult)

            with nc.Block() as block:
                @block.scalar
                def _(act):
                    for h in range(0, 5):
                        act.activation(dst[:, h, :], src[:, :], ACT.Copy, scale=mask[:, h:h + 1]).then_inc(s_a, 1)

                @block.vector
                def _(dve):
                    part(dve, slice(5, 12)).then_inc(s_v, 1)

                @block.gpsimd
                def _(pool):
                    part(pool, slice(12, H)).then_inc(s_p, 1)

    def attend(self, QT, Kx, V9, O):
        nc = self.nc
        units = [(b, q, i) for b in range(B) for q in range(HALVES) for i in range(ROWG)]
        first_pt = {}
        n_pt = 0
        for n, (b, q, i) in enumerate(units):
            first_pt[n] = n_pt
            n_pt += q + 1
        with self.sb("probs", [P, 2, 2, 4, P]) as pr, self.sb("probsT", [P, 4, 4, P]) as pT, \
                self.sb("nmax", [P, 2, 4]) as nmax, self.sb("rsum", [P, 2, H]) as rsum, Phase(nc) as ph:
            s_scores, s_max, s_exp = ph.sem("scores"), ph.sem("max"), ph.sem("exp")
            s_turn, s_pt, s_out = ph.sem("turn"), ph.sem("pt"), ph.sem("out")
            s_rec, s_norm = ph.sem("rec"), ph.sem("norm")
            s_ones = ph.sem("ones")

            def sbank(n):
                return self.bank(2 * (n % 2), 2)

            def obank(n):
                return self.bank(6 + n % 2)[:, 0:H * (HD + 1)]

            with nc.Block() as block:
                @block.gpsimd
                def _(pool):
                    pool.memset(V9[:, :, :, HD:HD + 1], 1.0).then_inc(s_ones, 1)

                @block.tensor
                def _(pe):
                    def scores(n):
                        b, q, i = units[n]
                        if n >= 2:
                            pe.wait_ge(s_exp, 4 * (n - 1))
                        rows = slice(32 * i, 32 * i + 32)
                        qs = QT[rows, b * S + q * P:b * S + (q + 1) * P]
                        for kb in range(q + 1):
                            o = sbank(n)[:, kb * CH:(kb + 1) * CH]
                            diag = kb == q
                            last = pe.matmul(o, qs, Kx[rows, :, b * S + kb * P:b * S + (kb + 1) * P],
                                             start=True, stop=not diag)
                            if diag:
                                last = pe.matmul(o, self.identb[:, :],
                                                 self.causalb[:, :].unsqueeze(1).to_broadcast([P, 4, P]),
                                                 start=False, stop=True)
                        last.then_inc(s_scores, 1)

                    def turn(n):
                        b, q, i = units[n]
                        for kb in range(q + 1):
                            m = first_pt[n] + kb
                            if m >= 2:
                                pe.wait_ge(s_pt, m - 1)
                            for j in range(4):
                                if kb == 0:
                                    pe.wait_ge(s_exp, 4 * n + j + 1)
                                last = pe.transpose(self.bank(4 + m % 2)[:, j * P:(j + 1) * P], pr[:, n % 2, kb, j, :],
                                                    self.c["ident"])
                            last.then_inc(s_turn, 1)

                    def out(n):
                        b, q, i = units[n]
                        g = n // ROWG
                        if i == 0 and g >= 2:
                            pe.wait_ge(s_norm, g - 1)
                        if n == 0:
                            pe.wait_ge(s_ones, 1)
                        pe.wait_ge(s_pt, first_pt[n] + q + 1)
                        for j in range(4):
                            h = 4 * i + j
                            for kb in range(q + 1):
                                m = first_pt[n] + kb
                                last = pe.matmul(obank(g)[:, h * (HD + 1):(h + 1) * (HD + 1)], pT[:, m % 4, j, :],
                                                 V9[:, 2 * b + kb, h, :], start=(kb == 0), stop=(kb == q))
                        last.then_inc(s_out, 1)

                    for n in range(len(units) + 2):
                        if n < len(units):
                            scores(n)
                        if 1 <= n <= len(units):
                            turn(n - 1)
                        if n >= 2:
                            out(n - 2)

                @block.scalar
                def _(act):
                    for n, (b, q, i) in enumerate(units):
                        act.wait_ge(s_max, n + 1)
                        if n >= 2:
                            act.wait_ge(s_turn, first_pt[n - 1])
                        s = sbank(n)[:, 0:(q + 1) * CH].rearrange("p (k j c) -> p j k c", j=4, c=P)
                        for j in range(4):
                            act.activation(pr[:, n % 2, 0:q + 1, j, :], s[:, j, :, :], ACT.Exp,
                                           bias=nmax[:, n % 2, j:j + 1]).then_inc(s_exp, 1)

                @block.vector
                def _(dve):
                    def copies(n):
                        b, q, i = units[n]
                        for kb in range(q + 1):
                            m = first_pt[n] + kb
                            if n >= 2 and kb == 0:
                                dve.wait_ge(s_out, n - 1)
                            dve.wait_ge(s_turn, m + 1)
                            dve.tensor_copy(pT[:, m % 4, :, :], self.bank(4 + m % 2)[:, :]).then_inc(s_pt, 1)

                    def normalise(g):
                        dve.wait_ge(s_out, ROWG * (g + 1))
                        o = obank(g).rearrange("p (h d) -> p h d", d=HD + 1)
                        dve.reciprocal(rsum[:, g % 2, :], o[:, :, HD]).then_inc(s_rec, 1)
                        dve.wait_ge(s_rec, g + 1)
                        dve.tensor_tensor(O[:, g, :].rearrange("p (h d) -> p h d", d=HD), o[:, :, 0:HD],
                                          rsum[:, g % 2, :].unsqueeze(2).to_broadcast([P, H, HD]), ALU.mult).then_inc(s_norm, 1)

                    for n in range(len(units) + 2):
                        if n < len(units):
                            b, q, i = units[n]
                            dve.wait_ge(s_scores, n + 1)
                            if n >= 2:
                                dve.wait_ge(s_exp, 4 * (n - 1))
                            s = sbank(n)[:, 0:(q + 1) * CH].rearrange("p (k j c) -> p j k c", j=4, c=P)
                            dve.tensor_reduce(nmax[:, n % 2, :], s, AX.XY, ALU.max, negate=True).then_inc(s_max, 1)
                        if 1 <= n <= len(units):
                            copies(n - 1)
                        if n >= 2 and (n - 2) % ROWG == ROWG - 1:
                            normalise((n - 2) // ROWG)

    def attend_context(self, score, V, width, O, bias=None, per_token=False, combine=None):
        nc = self.nc
        V1 = width + 1
        wide = width > HD
        G = 4 if wide else 2
        HG = H // G
        tile_of = (lambda h: (h % 4) // 2) if wide else (lambda h: h % 2)
        block_of = (lambda h: (h % 2) * 4 + h // 4) if wide else (lambda h: h // 2)
        with self.sb("sub", [P, 2, H, SC]) as sub, self.sb("probsX", [P, 2, H, SC]) as pr, \
                self.sb("probsXT", [P, 2, H // 2, P]) as pT, self.sb("nmaxX", [P, 2, H]) as nmax, \
                self.sb("rsumX", [P, 2, G, HG]) as rsum, self.sb("part", [P, 2, H, width]) as part, Phase(nc) as ph:
            s_scores, s_max, s_sub, s_exp = ph.sem("scores"), ph.sem("max"), ph.sem("sub"), ph.sem("exp")
            s_turn, s_pt, s_out, s_rec = ph.sem("turn"), ph.sem("pt"), ph.sem("out"), ph.sem("rec")
            s_norm, s_ones = ph.sem("norm"), ph.sem("ones")
            chain = ph.sem("chain")

            def out_at(h):
                c = (4 + h % G) * CH + (h // G) * V1
                return self.ps[:, c:c + V1]

            with nc.Block() as block:
                @block.gpsimd
                def _(pool):
                    pool.memset(V[:, :, :, width:V1], 1.0).then_inc(s_ones, 1)

                @block.tensor
                def _(pe):
                    pe.wait_ge(s_ones, 1)

                    def turn(t):
                        pe.wait_ge(s_exp, t + 1)
                        if t >= 1:
                            pe.wait_ge(s_pt, t)
                        for p2 in range(H // 2):
                            last = pe.transpose(self.bank(2, 2)[:, p2 * P:(p2 + 1) * P],
                                                pr[:, t % 2, 2 * p2:2 * p2 + 2, :], self.c["ident"])
                        last.then_inc(s_turn, 1)

                    def out(t):
                        pe.wait_ge(s_pt, t + 1)
                        if t >= 1:
                            pe.wait_ge(s_norm, t)
                        for h in range(H):
                            r = slice(SC * tile_of(h), SC * tile_of(h) + SC)
                            last = pe.matmul(out_at(h), pT[r, t % 2, block_of(h), :], V[r, t // HALVES, h, :], start=True, stop=True)
                        last.then_inc(s_out, 1)

                    for t in range(NT + 2):
                        if t < NT:
                            if t >= 1:
                                pe.wait_ge(s_sub, t)
                            banks = self.bank(0, 2)
                            if bias is not None:
                                bt = bias[:, t, :] if per_token else bias[:, t // HALVES, :]
                                for g in range(2):
                                    pe.matmul(banks[:, g * CH:(g + 1) * CH], self.identb[:, :],
                                              bt.unsqueeze(1).to_broadcast([P, H // 2, SC]), start=True, stop=False)
                            score(pe, t, banks, bias is None).then_inc(s_scores, 1)
                        if 1 <= t <= NT:
                            turn(t - 1)
                        if t >= 2:
                            out(t - 2)

                @block.scalar
                def _(act):
                    def copy(t):
                        act.wait_ge(s_turn, t + 1)
                        if t >= 2:
                            act.wait_ge(s_out, t - 1)
                        act.activation(pT[:, t % 2, :, :], self.bank(2, 2), ACT.Copy).then_inc(s_pt, 1)

                    for t in range(NT + 1):
                        if t < NT:
                            act.wait_ge(s_sub, t + 1)
                            if t >= 2:
                                act.wait_ge(s_turn, t - 1)
                            act.activation(pr[:, t % 2, :, :], sub[:, t % 2, :, :], ACT.Exp).then_inc(s_exp, 1)
                        if t >= 1:
                            copy(t - 1)

                @block.vector
                def _(dve):
                    def normalise(t):
                        dve.wait_ge(s_out, t + 1)
                        out_bank = lambda g: self.bank(4 + g)[:, 0:HG * V1].rearrange("p (h d) -> p h d", d=V1)
                        for g in range(G):
                            last = dve.reciprocal(rsum[:, t % 2, g, :], out_bank(g)[:, :, width])
                        last.then_inc(s_rec, 1)
                        dve.wait_ge(s_rec, (t + 1) if combine is None else (2 * t + 1))
                        if combine is not None:
                            dve.tensor_tensor(rsum[:, t % 2, :, :], rsum[:, t % 2, :, :],
                                              combine.rearrange("p (h g) -> p g h", g=G), ALU.mult).then_inc(s_rec, 1)
                            dve.wait_ge(s_rec, 2 * t + 2)
                        for g in range(G):
                            r = rsum[:, t % 2, g, :].unsqueeze(2).to_broadcast([P, HG, width])
                            d = O[:, t, g:H:G, :] if combine is None else part[:, t % 2, g:H:G, :]
                            last = dve.tensor_tensor(d, out_bank(g)[:, :, 0:width], r, ALU.mult)
                        last.then_inc(s_norm, 1)
                        if combine is not None:
                            dve.wait_ge(s_norm, t + 1)
                            dve.tensor_tensor(O[:, t, :, :], O[:, t, :, :], part[:, t % 2, :, :], ALU.subtract).then_inc(chain, 1)

                    for t in range(NT + 2):
                        if t < NT:
                            s = self.bank(0, 2).rearrange("p (h k) -> p h k", k=SC)
                            dve.wait_ge(s_scores, t + 1)
                            dve.tensor_reduce(nmax[:, t % 2, :], s, AX.X, ALU.max, negate=True).then_inc(s_max, 1)
                            dve.wait_ge(s_max, t + 1)
                            if t >= 2:
                                dve.wait_ge(s_exp, t - 1)
                            dve.tensor_tensor(sub[:, t % 2, :, :], s,
                                              nmax[:, t % 2, :].unsqueeze(2).to_broadcast([P, H, SC]), ALU.add).then_inc(s_sub, 1)
                        if t >= 2:
                            normalise(t - 2)

    def head_scores(self, QT, Kx):
        def score(pe, t, banks, first):
            b = t // HALVES
            for g in range(2):
                last = pe.matmul(banks[:, g * CH:(g + 1) * CH], QT[:, t * P:(t + 1) * P],
                                 Kx[:, g * H // 2:(g + 1) * H // 2, b * SC:(b + 1) * SC], start=first, stop=True)
            return last
        return score

    def project(self, src, W, bias, dst, scale=None, gateT=None):
        nc = self.nc
        with self.sb("srcT", [P, NT * P]) as srcT, Phase(nc) as ph:
            s_turn, s_copy, s_product, s_sum = ph.sem("turn"), ph.sem("copy"), ph.sem("product"), ph.sem("sum")
            with nc.Block() as block:
                @block.tensor
                def _(pe):
                    for t in range(NT):
                        pe.transpose(self.ps[:, t * P:(t + 1) * P], src[:, t, :], self.c["ident"]).then_inc(s_turn, 1)
                    for t in range(NT):
                        pe.wait_ge(s_copy, t // 4 + 1)
                        o = self.ps[:, (NT + t) * P:(NT + t + 1) * P]
                        last = pe.matmul(o, srcT[:, t * P:(t + 1) * P], W, start=True, stop=bias is None)
                        if bias is not None:
                            last = pe.matmul(o, self.c["ones_row"], bias, start=False, stop=True)
                        last.then_inc(s_product, 1)

                @block.scalar
                def _(act):
                    for g in range(NCH):
                        cols = slice(g * CH, (g + 1) * CH)
                        act.wait_ge(s_turn, 4 * (g + 1))
                        act.activation(srcT[:, cols], self.ps[:, cols], ACT.Copy,
                                       scale=1.0 if scale is None else scale).then_inc(s_copy, 1)

                @block.vector
                def _(dve):
                    for g in range(NCH):
                        dve.wait_ge(s_product, 4 * (g + 1))
                        dve.tensor_tensor(dst[:, 4 * g:4 * g + 4, :],
                                          self.bank(2 + g)[:, :].rearrange("p (t d) -> p t d", d=D),
                                          dst[:, 4 * g:4 * g + 4, :], ALU.add).then_inc(s_sum, 1)

    def rows_added(self, jobs, srcT, W, bias, dst, k=1):
        for g in range(NCH):
            mms = []
            for t in range(4 * g, 4 * g + 4):
                c = (t - 4 * g) * P
                for kk in range(k):
                    mms.append((c, c + P, P, srcT[:, kk, t * P:(t + 1) * P], W[:, kk * D:(kk + 1) * D],
                                kk == 0, bias is None and kk == k - 1))
                if bias is not None:
                    mms.append((c, c + P, P, self.c["ones_row"], bias, False, True))
            d = dst[:, 4 * g:4 * g + 4, :]
            jobs.append((mms, ("dve", "add", d, (lambda bank: bank[:, :].rearrange("p (t d) -> p t d", d=D)), d), None))

    def L0_attn(self):
        nc = self.nc
        self.norm(self.x, self.nrm, self.xT)
        EK = INNER // P
        with self.weights("L0_attn") as w, self.sb("v", [P, NT, INNER]) as v, self.sb("gateT", [P, EK, B * S]) as gateT, \
                self.sb("baseT", [P, B * S]) as baseT, self.sb("four", [P, 4, B * S]) as four, \
                self.sb("oT", [P, EK, B * S]) as oT:
            jobs = []
            for e in range(EK):
                jobs += self.turned(w["Wg"][:, e * P:(e + 1) * P], self.xT, gateT[:, e, :], bias=w["bg"][:, e:e + 1], func=ACT.Silu)
            jobs += self.turned(w["Win"], self.xT, baseT, bias=w["bin"], func=ACT.Silu)
            for g in range(0, NT, 2):
                mms = []
                for t in (g, g + 1):
                    c = (t - g) * INNER
                    mms.append((c, c + INNER, P, self.xT[:, t * P:(t + 1) * P], w["Wv"], True, False))
                    mms.append((c, c + INNER, P, self.c["ones_row"], w["bv"], False, True))
                jobs.append((mms, ("act", ACT.Silu, v[:, g:g + 2, :], self.whole(), 0.0, 1.0), None))
            self.products(jobs)
            QQ, QK, LQ, LK = range(4)
            with Phase(nc) as ph:
                s_aff = ph.sem("affine")
                with nc.Block() as block:
                    @block.vector
                    def _(dve):
                        for n, name in enumerate(("qq", "qk", "lq", "lk")):
                            dve.tensor_scalar(four[:, n, :], baseT[:, :], w["g_" + name], w["b_" + name],
                                              ALU.mult, ALU.add).then_inc(s_aff, 1)
            units = [(b, kb) for b in range(B) for kb in range(HALVES)]
            with self.sb("sq", [P, 2, S]) as sq, self.sb("mix", [P, 4, S]) as mix, Phase(nc) as ph:
                s_scores, s_relu, s_chain, s_mix = ph.sem("scores"), ph.sem("relu"), ph.sem("chain"), ph.sem("mix")
                s_out, s_gated = ph.sem("out"), ph.sem("gated")
                with nc.Block() as block:
                    @block.tensor
                    def _(pe):
                        def out(b):
                            pe.wait_ge(s_mix, 2 * b + 2)
                            if b >= 2:
                                pe.wait_ge(s_gated, b - 1)
                            for e in range(EK):
                                for kb in range(HALVES):
                                    last = pe.matmul(self.bank(4 + b % 2)[:, e * S:(e + 1) * S], v[:, 2 * b + kb, e * P:(e + 1) * P],
                                                     mix[:, (2 * b + kb) % 4, :], start=(kb == 0), stop=(kb == 1))
                            last.then_inc(s_out, 1)
                        for n, (b, kb) in enumerate(units):
                            if n >= 4:
                                pe.wait_ge(s_mix, n - 3)
                            ks = slice(b * S + kb * P, b * S + (kb + 1) * P)
                            qs = slice(b * S, (b + 1) * S)
                            pe.matmul(self.bank(n % 4)[:, 0:S], four[:, QK, ks], four[:, QQ, qs], start=True, stop=True)
                            pe.matmul(self.bank(n % 4)[:, S:2 * S], four[:, LK, ks], four[:, LQ, qs], start=True, stop=True).then_inc(s_scores, 1)
                            if n >= 3 and n % 2 == 1:
                                out(n // 2 - 1)
                        out(B - 1)

                    @block.scalar
                    def _(act):
                        for n in range(len(units)):
                            act.wait_ge(s_scores, n + 1)
                            if n >= 2:
                                act.wait_ge(s_mix, n - 1)
                            act.activation(sq[:, n % 2, :], self.bank(n % 4)[:, 0:S], ACT.Relu, scale=1.0 / INNER ** 0.5).then_inc(s_relu, 1)

                    @block.vector
                    def _(dve):
                        chain = [0]

                        def gate(b):
                            dve.wait_ge(s_out, b + 1)
                            dve.tensor_tensor(oT[:, :, b * S:(b + 1) * S], self.bank(4 + b % 2)[:, :].rearrange("p (e s) -> p e s", e=EK),
                                              gateT[:, :, b * S:(b + 1) * S], ALU.mult).then_inc(s_gated, 1)
                        for n, (b, kb) in enumerate(units):
                            dve.wait_ge(s_relu, n + 1)
                            if n >= 4:
                                dve.wait_ge(s_out, (n - 4) // 2 + 1)
                            m = slice(kb * S, (kb + 1) * S)
                            link(dve, s_chain, chain, dve.tensor_tensor(sq[:, n % 2, :], sq[:, n % 2, :], sq[:, n % 2, :], ALU.mult))
                            link(dve, s_chain, chain, dve.tensor_tensor(sq[:, n % 2, :], sq[:, n % 2, :], self.c["in_chunk"][:, m], ALU.mult))
                            link(dve, s_chain, chain, dve.tensor_tensor(mix[:, n % 4, :], self.bank(n % 4)[:, S:2 * S], self.c["older_chunk"][:, m], ALU.mult))
                            dve.tensor_tensor(mix[:, n % 4, :], mix[:, n % 4, :], sq[:, n % 2, :], ALU.add).then_inc(s_mix, 1)
                            if n >= 3 and n % 2 == 1:
                                gate(n // 2 - 1)
                        gate(B - 1)
            jobs = []
            self.rows_added(jobs, oT, w["Wout"], w["bout"], self.x, k=EK)
            self.products(jobs)

    def context_keys_values(self, jobs, Wk, Wv, KT, V9, bk=0.0, bv=None):
        jobs += self.turned(Wk, self.ctx["ctxT"], KT, bias=bk, width=B * SC)
        jobs += self.value_rows(Wv, self.ctx["ctxT2"], V9, bias=bv, n=B)

    def L0_xattn(self):
        nc = self.nc
        self.norm(self.x, self.nrm, self.xT)
        with self.weights("L0_xattn") as w, self.sb("QT", [P, B * S]) as QT, self.sb("KT", [P, B * SC]) as KT, \
                self.sb("Kx", [P, H, B * SC]) as Kx, self.sb("V9", [P, B, H, HD + 1]) as V9, self.sb("O", [P, NT, D]) as O:
            jobs = []
            for c in range(NCH):
                cols = slice(c * CH, (c + 1) * CH)
                jobs.append(([(0, CH, P, w["Wq"], self.xT[:, cols], True, True)],
                             ("dve", "affine", QT[:, cols], self.whole(), w["bq"], HD ** -0.5), None))
            self.context_keys_values(jobs, w["Wk"], w["Wv"], KT, V9, w["bk"], w["bv"])
            self.products(jobs)
            self.expand_context(KT, Kx)
            self.attend_context(self.head_scores(QT, Kx), V9, HD, O[:, :, :].rearrange("p t (h d) -> p t h d", d=HD), bias=self.keepb)
            self.project(O, w["Wo"], w["bo"], self.x)

    def quantise(self, tensors):
        nc = self.nc
        n_max = max(a.shape[1] for a in tensors)
        with self.sb("sc", [P, n_max]) as sc, self.sb("inv", [P, n_max]) as inv, self.sb("mag", [P, n_max, 16]) as mag, \
                self.sb("acc", [P, n_max, 16]) as acc, self.sb("sgn", [P, n_max, 16]) as sgn, Phase(nc) as ph:
            s_chain, s_scale, s_sign, s_done = ph.sem("chain"), ph.sem("scale"), ph.sem("sign"), ph.sem("done")
            with nc.Block() as block:
                @block.scalar
                def _(act):
                    for k, a in enumerate(tensors):
                        r, n = a.shape[0], a.shape[1]
                        if k:
                            act.wait_ge(s_done, k)
                        act.activation(sgn[0:r, 0:n, :], a, ACT.Sign).then_inc(s_sign, 1)

                @block.vector
                def _(dve):
                    chain = [0]
                    for k, a in enumerate(tensors):
                        r, n = a.shape[0], a.shape[1]
                        wide = lambda v: v[0:r, 0:n].unsqueeze(2).to_broadcast([r, n, 16])
                        m, q = mag[0:r, 0:n, :], acc[0:r, 0:n, :]
                        link(dve, s_chain, chain, dve.tensor_reduce(sc[0:r, 0:n], a, AX.X, ALU.max, apply_absolute_value=True))
                        link(dve, s_chain, chain, dve.tensor_scalar(sc[0:r, 0:n], sc[0:r, 0:n], 1.0 / 6.0, 1e-12, ALU.mult, ALU.max))
                        link(dve, s_chain, chain, dve.reciprocal(inv[0:r, 0:n], sc[0:r, 0:n]))
                        link(dve, s_chain, chain, dve.tensor_tensor(m, a, wide(inv), ALU.mult))
                        dve.wait_ge(s_sign, k + 1)
                        link(dve, s_chain, chain, dve.tensor_tensor(m, m, sgn[0:r, 0:n, :], ALU.mult))
                        link(dve, s_chain, chain, dve.tensor_scalar(q, m, MIDS[6], 2.0, ALU.is_gt, ALU.mult))
                        for mid in (MIDS[5], MIDS[4]):
                            link(dve, s_chain, chain, dve.scalar_tensor_tensor(q, m, mid, q, ALU.is_gt, ALU.add))
                        link(dve, s_chain, chain, dve.tensor_scalar(q, q, 2.0, None, ALU.mult))
                        for mid in MIDS[3::-1]:
                            link(dve, s_chain, chain, dve.scalar_tensor_tensor(q, m, mid, q, ALU.is_gt, ALU.add))
                        link(dve, s_chain, chain, dve.scalar_tensor_tensor(q, q, 0.5, sgn[0:r, 0:n, :], ALU.mult, ALU.mult))
                        dve.tensor_tensor(a, q, wide(sc), ALU.mult).then_inc(s_done, 1)
                        dve.wait_ge(s_done, k + 1)

    def turn_tiles(self, moves):
        nc = self.nc
        with Phase(nc) as ph:
            s_turn, s_copy = ph.sem("turn"), ph.sem("copy")
            with nc.Block() as block:
                @block.tensor
                def _(pe):
                    for n, (src, dst) in enumerate(moves):
                        r, c = src.shape[0], src.shape[1]
                        if n >= 8:
                            pe.wait_ge(s_copy, n - 7)
                        pe.transpose(self.bank(n % 8)[0:c, 0:r], src, self.c["ident"][0:r, 0:r]).then_inc(s_turn, 1)

                @block.scalar
                def _(act):
                    for n, (src, dst) in enumerate(moves):
                        r, c = src.shape[0], src.shape[1]
                        act.wait_ge(s_turn, n + 1)
                        act.activation(dst, self.bank(n % 8)[0:c, 0:r], ACT.Copy).then_inc(s_copy, 1)

    def L0_ffn(self):
        blocks = lambda a: a.rearrange("p (n s) -> p n s", s=16)
        self.norm(self.x, self.nrm, None)
        NK = len(FT0)
        with self.weights("L0_ffn") as w, self.sb("wgT", [P, NF0]) as wgT, self.sb("wuT", [P, NF0]) as wuT, \
                self.sb("wdT", [P, NK, D]) as wdT, self.sb("g", [P, NK, B * S]) as gT, self.sb("h", [P, NT, NF0]) as h:
            self.quantise([self.nrm[:, :, :].rearrange("p t (n s) -> p (t n) s", s=16)]
                          + [blocks(w[f"{n}{i}"]) for n in ("w_gate", "w_up") for i in range(NK)] + [blocks(w["w_down"])])
            moves = [(self.nrm[:, t, :], self.xT[:, t * P:(t + 1) * P]) for t in range(NT)]
            for n, dst in (("w_gate", wgT), ("w_up", wuT)):
                moves += [(w[f"{n}{i}"], dst[:, f0:f0 + fn]) for i, (f0, fn) in enumerate(FT0)]
            moves += [(w["w_down"][:, f0:f0 + fn], wdT[0:fn, i, :]) for i, (f0, fn) in enumerate(FT0)]
            self.turn_tiles(moves)
            with self.sb("act", [P, NT, NF0]) as sil:
                jobs = []
                for t in range(NT):
                    xs = self.xT[:, t * P:(t + 1) * P]
                    jobs.append(([(0, NF0, P, xs, wgT[:, :], True, True)],
                                 ("act", ACT.Silu, sil[:, t, :], self.whole(P, NF0), 0.0, 1.0), None))
                    jobs.append(([(0, NF0, P, xs, wuT[:, :], True, True)],
                                 ("dve", "mult", h[:, t, :], self.whole(P, NF0), sil[:, t, :], len(jobs) - 1), None))
                self.products(jobs)
            self.quantise([h[:, 4 * g:4 * g + 4, :].rearrange("p t (n s) -> p (t n) s", s=16) for g in range(2)])
            self.turn_tiles([(h[:, t, f0:f0 + fn], gT[0:fn, i, t * P:(t + 1) * P]) for t in range(NT) for i, (f0, fn) in enumerate(FT0)])
            jobs = []
            for g in range(NCH):
                mms = []
                for t in range(4 * g, 4 * g + 4):
                    c = (t - 4 * g) * P
                    for i, (f0, fn) in enumerate(FT0):
                        mms.append((c, c + P, P, gT[0:fn, i, t * P:(t + 1) * P], wdT[0:fn, i, :], i == 0, i == NK - 1))
                d = self.x[:, 4 * g:4 * g + 4, :]
                jobs.append((mms, ("dve", "add", d, (lambda bank: bank[:, :].rearrange("p (t d) -> p t d", d=D)), d), None))
            self.products(jobs)

    def attend_turned(self, parts, V9, O, clip=None, decay=None, scale=1.0):
        nc = self.nc
        units = [(b, i, kb) for b in range(B) for i in range(ROWG) for kb in range(HALVES)]
        W9 = HD + 1
        first = lambda kb: kb * P if clip else 0

        with self.sb("clipped", [P, 2, 4, S]) as cl, self.sb("probsK", [P, 4, 4, S]) as pr, \
                self.sb("rsumK", [P, 2, 2, H]) as rsum, Phase(nc) as ph:
            s_scores, s_clip, s_exp, s_mask = ph.sem("scores"), ph.sem("clip"), ph.sem("exp"), ph.sem("mask")
            s_out, s_rec, s_norm, s_ones = ph.sem("out"), ph.sem("rec"), ph.sem("norm"), ph.sem("ones")
            s_ready = s_mask if clip else s_clip

            def sb4(n):
                return self.bank(2 * (n % 3), 2).rearrange("p (j s) -> p j s", j=4)

            def ob(b):
                return self.bank(6 + b % 2)[:, 0:2 * H * W9].rearrange("p (q h d) -> p q h d", q=2, d=W9)

            with nc.Block() as block:
                @block.gpsimd
                def _(pool):
                    pool.memset(V9[:, :, :, HD:W9], 1.0).then_inc(s_ones, 1)
                    if clip:
                        for n, (b, i, kb) in enumerate(units):
                            pool.wait_ge(s_exp, n + 1)
                            d = pr[:, n % 4, :, kb * P:(kb + 1) * P]
                            pool.tensor_tensor(d, d, self.c["causal_one"].unsqueeze(1).to_broadcast([P, 4, P]), ALU.mult).then_inc(s_mask, 1)

                @block.tensor
                def _(pe):
                    pe.wait_ge(s_ones, 1)

                    def out(n):
                        b, i, _ = units[n]
                        if i == 0 and b >= 2:
                            pe.wait_ge(s_norm, b - 1)
                        pe.wait_ge(s_ready, n + 2)
                        for q in range(HALVES):
                            kbs = [kb for kb in range(HALVES) if not clip or kb <= q]
                            for j in range(4):
                                for kb in kbs:
                                    last = pe.matmul(ob(b)[:, q, 4 * i + j, :], pr[:, (n + kb) % 4, j, q * P:(q + 1) * P],
                                                     V9[:, 2 * b + kb, 4 * i + j, :], start=(kb == kbs[0]), stop=(kb == kbs[-1]))
                        last.then_inc(s_out, 1)
                    for n, (b, i, kb) in enumerate(units):
                        if n >= 3:
                            pe.wait_ge(s_clip, n - 2)
                        rows = slice(32 * i, 32 * i + 32)
                        for j in range(4):
                            for m, (QT, Kx) in enumerate(parts):
                                last = pe.matmul(sb4(n)[:, j, first(kb):S], Kx[rows, j, b * S + kb * P:b * S + (kb + 1) * P],
                                                 QT[rows, b * S + first(kb):(b + 1) * S], start=(m == 0), stop=(m == len(parts) - 1))
                        last.then_inc(s_scores, 1)
                        if n >= 3 and kb == 1:
                            out(n - 3)
                    out(len(units) - 2)

                if clip:
                    @block.scalar
                    def _(act):
                        for n, (b, i, kb) in enumerate(units):
                            act.wait_ge(s_clip, n + 1)
                            if n >= 4:
                                act.wait_ge(s_out, (n - 4) // 2 + 1)
                            act.activation(pr[:, n % 4, :, first(kb):S], cl[:, n % 2, :, first(kb):S], ACT.Exp, scale=scale).then_inc(s_exp, 1)

                @block.vector
                def _(dve):
                    def take(b):
                        dve.wait_ge(s_out, ROWG * (b + 1))
                        dst = O[:, 2 * b:2 * b + 2, :].rearrange("p q (h d) -> p q h d", d=HD)
                        if clip:
                            dve.reciprocal(rsum[:, b % 2, :, :], ob(b)[:, :, :, HD]).then_inc(s_rec, 1)
                            dve.wait_ge(s_rec, b + 1)
                            for q in range(HALVES):
                                last = dve.tensor_tensor(dst[:, q, :, :], ob(b)[:, q, :, 0:HD],
                                                         rsum[:, b % 2, q, :].unsqueeze(2).to_broadcast([P, H, HD]), ALU.mult)
                        else:
                            for q in range(HALVES):
                                last = dve.tensor_scalar(dst[:, q, :, :], ob(b)[:, q, :, 0:HD], scale, None, ALU.mult)
                        last.then_inc(s_norm, 1)
                    for n, (b, i, kb) in enumerate(units):
                        dve.wait_ge(s_scores, n + 1)
                        if clip:
                            if n >= 2:
                                dve.wait_ge(s_exp, n - 1)
                            dve.tensor_scalar(cl[:, n % 2, :, first(kb):S], sb4(n)[:, :, first(kb):S], -clip, clip, ALU.max, ALU.min).then_inc(s_clip, 1)
                        else:
                            if n >= 4:
                                dve.wait_ge(s_out, (n - 4) // 2 + 1)
                            dve.tensor_tensor(pr[:, n % 4, :, :], sb4(n), decay[:, 4 * i:4 * i + 4, kb, :], ALU.mult).then_inc(s_clip, 1)
                        if n % (2 * ROWG) == 3 and n > 2 * ROWG:
                            take(n // (2 * ROWG) - 1)
                    take(B - 1)

    def L1_attn(self):
        self.norm(self.x, self.nrm, self.xT)
        c = self.c
        with self.weights("L1_attn") as w, self.sb("cq", [32, B * S]) as cq, self.sb("ckv", [32, B * S]) as ckv, \
                self.sb("QT", [P, B * S]) as QT, self.sb("KT", [P, B * S]) as KT, self.sb("QR", [P, B * S]) as QR, \
                self.sb("KR", [P, B * S]) as KR, self.sb("raw", [P, 2, B * S]) as raw, self.sb("Kx", [P, 4, B * S]) as Kx, \
                self.sb("KRx", [P, 4, B * S]) as KRx, self.sb("V9", [P, NT, H, HD + 1]) as V9, self.sb("O", [P, NT, D]) as O:
            jobs = self.turned(w["W_DQ"], self.xT, cq, m=32) + self.turned(w["W_DKV"], self.xT, ckv, m=32)
            self.products(jobs)
            jobs = []
            jobs += self.turned(w["W_UQ"], cq, QT)
            jobs += self.turned(w["W_UK"], ckv, KT, eng="dve")
            self.roped(jobs, w["W_QR"], cq, QR, raw[:, 0, :], c["rot_inter"], c["cos4"], c["sin4"])
            self.roped(jobs, w["W_KR"], self.xT, KR, raw[:, 1, :], c["rot_inter"], c["cos4"], c["sin4"])
            jobs += self.value_rows(w["W_UV"], ckv, V9, k=32)
            self.products(jobs)
            self.expand(KT, Kx, c["mask8"], B * S)
            self.expand(KR, KRx, c["mask4"], B * S)
            self.attend_turned([(QT, Kx), (QR, KRx)], V9, O, clip=80.0, scale=1.0 / math.sqrt(12.0))
            self.project(O, w["W_O"], None, self.x)

    def self_attention(self, src, w, dst, rot, weight=None, rms=False, norm=True, biases=False, names=("Wq", "Wk", "Wv", "Wo")):
        c = self.c
        if norm:
            self.norm(src, self.nrm, self.xT, layer=not rms, eps=1e-6 if rms else 1e-5, weight=weight)
        with self.sb("QT", [P, B * S]) as QT, self.sb("KT", [P, B * S]) as KT, self.sb("raw", [P, 2, B * S]) as raw, \
                self.sb("Kx", [P, 4, B * S]) as Kx, self.sb("V9", [P, NT, H, HD + 1]) as V9, self.sb("O", [P, NT, D]) as O:
            jobs = []
            bq, bk, bv, bo = (w["bq"], w["bk"], w["bv"], w["bo"]) if biases else (0.0, 0.0, None, None)
            self.roped(jobs, w[names[0]], self.xT, QT, raw[:, 0, :], rot, c["cos8"], c["sin8"], bias=bq)
            self.roped(jobs, w[names[1]], self.xT, KT, raw[:, 1, :], rot, c["cos8"], c["sin8"], bias=bk)
            jobs += self.value_rows(w[names[2]], self.xT, V9, bias=bv)
            self.products(jobs)
            nc = self.nc
            with Phase(nc) as ph:
                s_q = ph.sem("scaled")
                with nc.Block() as block:
                    @block.scalar
                    def _(act):
                        act.activation(raw[:, 0, :], QT[:, :], ACT.Copy, scale=HD ** -0.5).then_inc(s_q, 1)
            self.expand(KT, Kx, c["mask8"], B * S)
            self.attend(raw[:, 0, :], Kx, V9, O)
            self.project(O, w[names[3]], bo, dst)

    def L1_xattn(self):
        nc = self.nc
        awhere, awidth = self.where["inner_attn"]
        fwhere, fwidth = self.where["inner_ffn"]
        with self.sb("y", [P, NT, D]) as y, self.sb("w_attn", [P, awidth]) as wa, self.sb("w_ffn", [P, fwidth]) as wf, \
                self.weights("inner_misc") as wm, self.sb("allow", [P, NT, SC], BF16) as allow, self.sb("seg", [P, NT], I32) as seg:
            self.norm(self.x, y, None)
            with self.sb("segf", [P, NT]) as segf, self.sb("one", [P, NT, SC]) as one, self.sb("low", [P, NT]) as low, \
                    self.sb("two", [P, NT, SC]) as two, Phase(nc) as ph:
                s_load, s_chain = ph.sem("load"), ph.sem("chain")
                with nc.Block() as block:
                    @block.sync
                    def _(sp):
                        sp.dma_start(seg[:, :], self.seg_dram[:, :]).then_inc(s_load, 16)
                        sp.dma_start(wa[:, :], self.dram["inner_attn"][0, :, :]).then_inc(s_load, 16)
                        sp.wait_ge(s_load, 32)

                    @block.vector
                    def _(dve):
                        n = [0]
                        keys = self.c["keys"].unsqueeze(1).to_broadcast([P, NT, SC])
                        wide = lambda v: v[:, :].unsqueeze(2).to_broadcast([P, NT, SC])
                        dve.wait_ge(s_load, 32)
                        link(dve, s_chain, n, dve.tensor_copy(segf[:, :], seg[:, :]))
                        link(dve, s_chain, n, dve.tensor_scalar(low[:, :], segf[:, :], -128.0, None, ALU.add))
                        link(dve, s_chain, n, dve.tensor_tensor(one[:, :, :], keys, wide(segf), ALU.is_le))
                        link(dve, s_chain, n, dve.tensor_tensor(two[:, :, :], keys, wide(low), ALU.is_gt))
                        link(dve, s_chain, n, dve.tensor_tensor(one[:, :, :], one[:, :, :], two[:, :, :], ALU.mult))
                        link(dve, s_chain, n, dve.tensor_scalar(allow[:, :, :], one[:, :, :], -1.0, -NEG, ALU.add, ALU.mult))
            w, wff = Pack(wa, awhere), Pack(wf, fwhere)
            with nc.Fori(0, LAYERS) as layer:
                with Phase(nc) as ph:
                    s_f = ph.sem("ffn_weights")
                    with nc.Block() as block:
                        @block.sync
                        def _(sp):
                            sp.dma_start(wf[:, :], self.dram["inner_ffn"][bass.ds(layer, 1), :, :].rearrange("o p n -> (o p) n")).then_inc(s_f, 16)
                            sp.wait_ge(s_f, 16)
                self.self_attention(y, w, y, self.c["rot_half"], weight=w["n1"], rms=True, biases=True)
                self.norm(y, self.nrm, self.xT, layer=False, eps=1e-6, weight=w["n2"])
                with self.sb("QT", [P, B * S]) as QT, self.sb("KT", [P, B * SC]) as KT, \
                        self.sb("Kx", [P, H, B * SC]) as Kx, self.sb("V9", [P, B, H, HD + 1]) as V9, self.sb("O", [P, NT, D]) as O:
                    jobs = self.turned(w["Wq_c"], self.xT, QT, scale=HD ** -0.5)
                    self.context_keys_values(jobs, w["Wk_c"], w["Wv_c"], KT, V9)
                    self.products(jobs)
                    self.expand_context(KT, Kx)
                    self.attend_context(self.head_scores(QT, Kx), V9, HD, O[:, :, :].rearrange("p t (h d) -> p t h d", d=HD),
                                        bias=allow, per_token=True)
                    self.project(O, w["Wo_c"], None, y)
                with Phase(nc) as ph:
                    s_a = ph.sem("attn_weights")
                    with nc.Block() as block:
                        @block.sync
                        def _(sp):
                            sp.dma_start(wa[:, :], self.dram["inner_attn"][bass.ds(layer + 1, 1), :, :].rearrange("o p n -> (o p) n")).then_inc(s_a, 16)
                            sp.wait_ge(s_a, 16)
                self.norm(y, self.nrm, self.xT, layer=False, eps=1e-6, weight=wff["n3"])
                with self.sb("sil", [P, 2, CH]) as sil, self.sb("hT", [P, FK, B * S]) as hT:
                    jobs = []
                    for n, (f, ch) in enumerate((f, ch) for f in range(FK) for ch in range(NCH)):
                        cols = slice(ch * CH, (ch + 1) * CH)
                        fs = slice(f * P, (f + 1) * P)
                        jobs.append(([(0, CH, P, wff["Wg"][:, fs], self.xT[:, cols], True, True)],
                                     ("act", ACT.Silu, hT[:, f, cols], self.whole(), 0.0, 1.0), None))
                        jobs.append(([(0, CH, P, wff["Wu"][:, fs], self.xT[:, cols], True, True)],
                                     ("dve", "mult", hT[:, f, cols], self.whole(), hT[:, f, cols], len(jobs) - 1), None))
                    self.products(jobs)
                    jobs = []
                    self.rows_added(jobs, hT, wff["Wd"], None, y, k=FK)
                    self.products(jobs)
            self.norm(y, self.nrm, None, layer=False, eps=1e-6)
            with Phase(nc) as ph:
                s_chain = ph.sem("chain")
                with nc.Block() as block:
                    @block.vector
                    def _(dve):
                        n = [0]
                        nf = wm["nf"].unsqueeze(1).to_broadcast([P, NT, D])
                        link(dve, s_chain, n, dve.tensor_tensor(self.nrm[:, :, :], self.nrm[:, :, :], nf, ALU.mult))
                        link(dve, s_chain, n, dve.tensor_tensor(self.x[:, :, :], self.x[:, :, :], self.nrm[:, :, :], ALU.add))

    def route(self, w, top, gate, bias=True):
        nc = self.nc
        eps = {"L1": float(np.finfo(np.float32).eps)}
        with self.sb("logits", [P, NT, E]) as lg, self.sb("best", [P, NT, 8]) as best, self.sb("which", [P, NT, 8], U32) as which, \
                self.sb("whichf", [P, NT, 8]) as wh, self.sb("ex", [P, NT, E]) as ex, self.sb("hot", [P, NT, E]) as hot, \
                self.sb("hot2", [P, NT, E]) as hot2, self.sb("total", [P, NT]) as total, self.sb("z", [P, NT]) as z, Phase(nc) as ph:
            s_logits, s_chain, s_sub, s_exp = ph.sem("logits"), ph.sem("chain"), ph.sem("sub"), ph.sem("exp")
            with nc.Block() as block:
                @block.tensor
                def _(pe):
                    for t in range(NT):
                        o = self.ps[:, t * E:(t + 1) * E]
                        last = pe.matmul(o, self.xT[:, t * P:(t + 1) * P], w["Wr"], start=True, stop=not bias)
                        if bias:
                            last = pe.matmul(o, self.c["ones_row"], w["br"], start=False, stop=True)
                    last.then_inc(s_logits, 1)

                @block.scalar
                def _(act):
                    act.wait_ge(s_sub, 1)
                    act.activation(ex[:, :, :], ex[:, :, :], ACT.Exp).then_inc(s_exp, 1)

                @block.vector
                def _(dve):
                    n = [0]
                    wide = lambda v: v.to_broadcast([P, NT, E])
                    iota = self.c["iota8"].unsqueeze(1).to_broadcast([P, NT, E])
                    dve.wait_ge(s_logits, 1)
                    link(dve, s_chain, n, dve.tensor_copy(lg[:, :, :], self.ps[:, 0:NT * E]))
                    for t in range(NT):
                        link(dve, s_chain, n, dve.max(best[:, t, :], lg[:, t, :]))
                    dve.tensor_tensor(ex[:, :, :], lg[:, :, :], wide(best[:, :, 0:1]), ALU.subtract).then_inc(s_sub, 1)
                    for t in range(NT):
                        link(dve, s_chain, n, dve.max_index(which[:, t, :], best[:, t, :], lg[:, t, :]))
                    link(dve, s_chain, n, dve.tensor_copy(wh[:, :, :], which[:, :, :]))
                    link(dve, s_chain, n, dve.tensor_tensor(hot[:, :, :], iota, wide(wh[:, :, 0:1]), ALU.is_equal))
                    if top == 2:
                        link(dve, s_chain, n, dve.tensor_tensor(hot2[:, :, :], iota, wide(wh[:, :, 1:2]), ALU.is_equal))
                        link(dve, s_chain, n, dve.tensor_tensor(hot[:, :, :], hot[:, :, :], hot2[:, :, :], ALU.add))
                    dve.wait_ge(s_exp, 1)
                    link(dve, s_chain, n, dve.tensor_reduce(total[:, :], ex[:, :, :], AX.X, ALU.add))
                    link(dve, s_chain, n, dve.reciprocal(z[:, :], total[:, :]))
                    link(dve, s_chain, n, dve.tensor_tensor(ex[:, :, :], ex[:, :, :], wide(z[:, :].unsqueeze(2)), ALU.mult))
                    link(dve, s_chain, n, dve.tensor_tensor(gate[:, :, :], ex[:, :, :], hot[:, :, :], ALU.mult))
                    if top == 2:
                        link(dve, s_chain, n, dve.tensor_reduce(total[:, :], gate[:, :, :], AX.X, ALU.add))
                        if not bias:
                            link(dve, s_chain, n, dve.tensor_scalar(total[:, :], total[:, :], eps["L1"], None, ALU.add))
                        link(dve, s_chain, n, dve.reciprocal(z[:, :], total[:, :]))
                        link(dve, s_chain, n, dve.tensor_tensor(gate[:, :, :], gate[:, :, :], wide(z[:, :].unsqueeze(2)), ALU.mult))

    def experts(self, stage, gate, gated):
        nc = self.nc
        where, width = self.where[stage]
        U = FK * NCH
        with self.sb("slot0", [P, width]) as w0, self.sb("slot1", [P, width]) as w1, \
                self.sb("hidden", [P, 2, FK, B * S]) as hid:
            with Phase(nc) as ph:
                s_w = ph.sem("first_weights")
                with nc.Block() as block:
                    @block.sync
                    def _(sp):
                        sp.dma_start(w0[:, :], self.dram[stage][0, :, :]).then_inc(s_w, 16)
                        sp.wait_ge(s_w, 16)
            packs = (Pack(w0, where), Pack(w1, where))
            with nc.Fori(0, E // 2) as pair, Phase(nc) as ph:
                expert = pair * 2
                s_slot1, s_slot0 = ph.sem("slot1_loaded"), ph.sem("slot0_loaded")
                s_up, s_act, s_hid = ph.sem("up"), ph.sem("act"), ph.sem("hidden")
                s_down, s_added, s_zero = ph.sem("down"), ph.sem("added"), ph.sem("zero")
                R = 6
                per = 2 if gated else 1
                s_full = s_hid if gated else s_act
                with nc.Block() as block:
                    @block.sync
                    def _(sp):
                        sp.dma_start(w1[:, :], self.dram[stage][bass.ds(expert + 1, 1), :, :].rearrange("o p n -> (o p) n")).then_inc(s_slot1, 16)
                        sp.wait_ge(s_down, NCH)
                        sp.dma_start(w0[:, :], self.dram[stage][bass.ds(expert + 2, 1), :, :].rearrange("o p n -> (o p) n")).then_inc(s_slot0, 16)
                        sp.wait_ge(s_slot0, 16)
                        sp.wait_ge(s_slot1, 16)

                    @block.tensor
                    def _(pe):
                        def up(x):
                            if x == 1:
                                pe.wait_ge(s_slot1, 16)
                            w = packs[x]
                            for u in range(U):
                                f, ch = u // NCH, u % NCH
                                for m, name in enumerate(("Wg", "Wu") if gated else ("W1",)):
                                    k = (x * U + u) * per + m
                                    if k >= R:
                                        old = (k - R) // per
                                        pe.wait_ge(s_full, old + 1)
                                    pe.matmul(self.bank(k % R), w[name][:, f * P:(f + 1) * P],
                                              self.xT[:, ch * CH:(ch + 1) * CH], start=True, stop=True).then_inc(s_up, 1)

                        def down(x):
                            w = packs[x]
                            pe.wait_ge(s_full, (x + 1) * U)
                            for g in range(NCH):
                                n = x * NCH + g
                                if n >= 2:
                                    pe.wait_ge(s_added, 4 * (n - 1))
                                for t in range(4 * g, 4 * g + 4):
                                    c = (t - 4 * g) * P
                                    for f in range(FK):
                                        last = pe.matmul(self.bank(R + n % 2)[:, c:c + P], hid[:, x, f, t * P:(t + 1) * P],
                                                         w["Wd" if gated else "W2"][:, f * D:(f + 1) * D], start=(f == 0), stop=(f == FK - 1))
                                last.then_inc(s_down, 1)
                        up(0)
                        down(0)
                        up(1)
                        down(1)

                    @block.scalar
                    def _(act):
                        for x in range(2):
                            for u in range(U):
                                f, ch = u // NCH, u % NCH
                                n = x * U + u
                                act.wait_ge(s_up, n * per + 1)
                                d = hid[:, x, f, ch * CH:(ch + 1) * CH]
                                if x == 1 and u == 0:
                                    act.wait_ge(s_slot1, 16)
                                if gated:
                                    act.activation(d, self.bank((n * per) % R), ACT.Relu).then_inc(s_act, 1)
                                else:
                                    act.activation(d, self.bank(n % R), ACT.Gelu, bias=packs[x]["b1"][:, f:f + 1]).then_inc(s_act, 1)

                    @block.vector
                    def _(dve):
                        def hidden(x, u):
                            f, ch = u // NCH, u % NCH
                            n = x * U + u
                            dve.wait_ge(s_up, 2 * n + 2)
                            dve.wait_ge(s_act, n + 1)
                            d = hid[:, x, f, ch * CH:(ch + 1) * CH]
                            dve.tensor_tensor(d, self.bank((2 * n + 1) % R), d, ALU.mult).then_inc(s_hid, 1)

                        def add(x, g):
                            n = x * NCH + g
                            dve.wait_ge(s_down, n + 1)
                            if x == 1:
                                dve.wait_ge(s_added, 4 * (g + 1))
                            for t in range(4 * g, 4 * g + 4):
                                c = (t - 4 * g) * P
                                dve.scalar_tensor_tensor(self.x[:, t, :], self.bank(R + n % 2)[:, c:c + P],
                                                         gate[:, t, bass.ds(expert + x, 1)], self.x[:, t, :],
                                                         ALU.mult, ALU.add).then_inc(s_added, 1)
                        for x in range(2):
                            if gated:
                                for u in range(U):
                                    hidden(x, u)
                            for g in range(NCH):
                                add(x, g)

    def add_gated_bias(self, gate, b2):
        nc = self.nc
        with self.sb("gateT", [E, B * S]) as gT:
            self.turn_tiles([(gate[:, t, :], gT[:, t * P:(t + 1) * P]) for t in range(NT)])
            jobs = []
            for g in range(NCH):
                mms = [((t - 4 * g) * P, (t - 4 * g + 1) * P, P, gT[:, t * P:(t + 1) * P], b2, True, True) for t in range(4 * g, 4 * g + 4)]
                d = self.x[:, 4 * g:4 * g + 4, :]
                jobs.append((mms, ("dve", "add", d, (lambda bank: bank[:, :].rearrange("p (t d) -> p t d", d=D)), d), None))
            self.products(jobs)

    def moe(self, layer, top):
        self.norm(self.x, self.nrm, self.xT)
        gated = layer == "L1"
        with self.weights(layer + "_ffn") as w, self.sb("gate", [P, NT, E]) as gate:
            self.route(w, top, gate, bias=not gated)
            if not gated:
                self.add_gated_bias(gate, w["b2"])
            self.experts(layer + "_experts", gate, gated)

    def L1_ffn(self):
        self.moe("L1", 2)

    def L2_ffn(self):
        self.moe("L2", 1)

    def L3_ffn(self):
        self.moe("L3", 2)

    def L2_attn(self):
        with self.weights("L2_attn") as w:
            self.self_attention(self.x, w, self.x, self.c["rot_inter"])

    def L2_xattn(self):
        nc = self.nc
        self.norm(self.x, self.nrm, self.xT)
        with self.weights("L2_xattn") as w, self.sb("QT", [P, 2, B * S]) as QT, self.sb("KT", [P, 2, B * SC]) as KT, \
                self.sb("Kx", [P, 2, H, B * SC]) as Kx, self.sb("V9", [P, B, H, HD + 1]) as V9, \
                self.sb("O", [P, NT, D]) as O, self.sb("lam", [P, H]) as lam:
            jobs = self.turned(w["q1"], self.xT, QT[:, 0, :], scale=HD ** -0.5) + self.turned(w["q2"], self.xT, QT[:, 1, :], scale=HD ** -0.5)
            self.context_keys_values(jobs, w["k1"], w["v1"], KT[:, 0, :], V9)
            jobs += self.turned(w["k2"], self.ctx["ctxT"], KT[:, 1, :], width=B * SC)
            self.products(jobs)
            with Phase(nc) as ph:
                s_chain = ph.sem("chain")
                with nc.Block() as block:
                    @block.vector
                    def _(dve):
                        n = [0]
                        link(dve, s_chain, n, dve.tensor_tensor(lam[:, :], w["l1"], w["l2"], ALU.subtract))
                        link(dve, s_chain, n, dve.tensor_scalar(lam[:, :], lam[:, :], 0.1, None, ALU.add))
            for m in range(2):
                self.expand_context(KT[:, m, :], Kx[:, m, :, :])
            heads = O[:, :, :].rearrange("p t (h d) -> p t h d", d=HD)
            self.attend_context(self.head_scores(QT[:, 0, :], Kx[:, 0, :, :]), V9, HD, heads)
            self.attend_context(self.head_scores(QT[:, 1, :], Kx[:, 1, :, :]), V9, HD, heads, combine=lam[:, :])
            self.norm(O, self.nrm, None, layer=False, eps=1e-6)
            self.project(self.nrm, w["proj"], w["b"], self.x, scale=w["norm"])

    def L3_attn(self):
        nc = self.nc
        c = self.c
        self.norm(self.x, self.nrm, self.xT)
        with self.weights("L3_attn") as w, self.sb("QT", [P, B * S]) as QT, self.sb("KT", [P, B * S]) as KT, \
                self.sb("raw", [P, 2, B * S]) as raw, self.sb("Kx", [P, 4, B * S]) as Kx, \
                self.sb("V9", [P, NT, H, HD + 1]) as V9, self.sb("O", [P, NT, D]) as O, self.sb("gate", [P, NT, D]) as gate, \
                self.sb("decay", [P, H, HALVES, S]) as decay, self.sb("sg", [P, H]) as sg:
            jobs = []
            self.roped(jobs, w["Wq"], self.xT, QT, raw[:, 0, :], c["rot_inter"], c["cos8"], c["sin8"], bias=w["bq"])
            self.roped(jobs, w["Wk"], self.xT, KT, raw[:, 1, :], c["rot_inter"], c["cos8"], c["sin8"], bias=w["bk"])
            jobs += self.value_rows(w["Wv"], self.xT, V9, bias=w["bv"])
            for g in range(NCH):
                mms = []
                for t in range(4 * g, 4 * g + 4):
                    k = (t - 4 * g) * P
                    mms.append((k, k + P, P, self.xT[:, t * P:(t + 1) * P], w["Wg"], True, False))
                    mms.append((k, k + P, P, c["ones_row"], w["bg"], False, True))
                jobs.append((mms, ("act", ACT.Silu, gate[:, 4 * g:4 * g + 4, :], self.whole(), 0.0, 1.0), None))
            self.products(jobs)
            self.expand(KT, Kx, c["mask8"], B * S)
            with Phase(nc) as ph:
                s_sig, s_neg, s_decay = ph.sem("sigmoid"), ph.sem("negated"), ph.sem("decay")
                with nc.Block() as block:
                    @block.scalar
                    def _(act):
                        act.activation(sg[:, :], w["gamma"], ACT.Sigmoid).then_inc(s_sig, 1)
                        act.wait_ge(s_neg, 1)
                        for h in range(H):
                            act.activation(decay[:, h, :, :], c["distance"], ACT.Exp, scale=sg[:, h:h + 1]).then_inc(s_decay, 1)

                    @block.vector
                    def _(dve):
                        dve.wait_ge(s_sig, 1)
                        dve.tensor_scalar(sg[:, :], sg[:, :], -1.0, None, ALU.mult).then_inc(s_neg, 1)
            self.attend_turned([(QT, Kx)], V9, O, decay=decay, scale=1.0 / math.sqrt(HD))
            with Phase(nc) as ph:
                s_chain = ph.sem("chain")
                with nc.Block() as block:
                    @block.vector
                    def _(dve):
                        n = [0]
                        link(dve, s_chain, n, dve.tensor_tensor(O[:, :, :], O[:, :, :], gate[:, :, :], ALU.mult))
                        link(dve, s_chain, n, dve.tensor_tensor(self.x[:, :, :], self.x[:, :, :], O[:, :, :], ALU.add))

    def L3_xattn(self):
        nc = self.nc
        self.norm(self.x, self.nrm, self.xT)
        QK = H * DK3 // P
        with self.weights("L3_xattn") as w, self.sb("QT", [P, QK, B * S]) as QT, self.sb("KT", [P, QK, B * SC]) as KT, \
                self.sb("V65", [P, B, H, DK3 + 1]) as V, self.sb("O", [P, NT, H * DK3]) as O:
            jobs = []
            for k in range(QK):
                jobs += self.turned(w["Wq"][:, k * P:(k + 1) * P], self.xT, QT[:, k, :], eng="act" if k % 2 else "dve")
                jobs += self.turned(w["Wk"][:, k * P:(k + 1) * P], self.ctx["ctxT"], KT[:, k, :], width=B * SC)
            for b in range(B):
                for m in range(2):
                    jobs.append(([(0, CH, P, self.ctx["ctxT2"][:, b * P:(b + 1) * P], w["Wv"][:, m * CH:(m + 1) * CH], True, True)],
                                 ("dve", "copy", V[:, b, m * H // 2:(m + 1) * H // 2, 0:DK3], (lambda bank: bank[:, :].rearrange("p (h d) -> p h d", d=DK3))), None))
            self.products(jobs)

            def score(pe, t, banks, first):
                for h in range(H):
                    r = slice(DK3 * (h % 2), DK3 * (h % 2) + DK3)
                    c = (h % 2) * CH + (h // 2) * SC
                    last = pe.matmul(banks[:, c:c + SC], QT[r, h // 2, t * P:(t + 1) * P],
                                     KT[r, h // 2, (t // HALVES) * SC:(t // HALVES + 1) * SC], start=True, stop=True)
                return last
            self.attend_context(score, V, DK3, O[:, :, :].rearrange("p t (h d) -> p t h d", d=DK3))
            with Phase(nc) as ph:
                s_turn, s_mult = ph.sem("turn"), ph.sem("mult")
                with nc.Block() as block:
                    @block.tensor
                    def _(pe):
                        for k in range(QK):
                            for g in range(NCH):
                                n = k * NCH + g
                                if n >= 8:
                                    pe.wait_ge(s_mult, n - 7)
                                for t in range(4 * g, 4 * g + 4):
                                    last = pe.transpose(self.bank(n % 8)[:, (t - 4 * g) * P:(t - 4 * g + 1) * P],
                                                        O[:, t, k * P:(k + 1) * P], self.c["ident"])
                                last.then_inc(s_turn, 1)

                    @block.vector
                    def _(dve):
                        for k in range(QK):
                            for g in range(NCH):
                                n = k * NCH + g
                                dve.wait_ge(s_turn, n + 1)
                                d = QT[:, k, g * CH:(g + 1) * CH]
                                dve.tensor_tensor(d, self.bank(n % 8)[:, :], d, ALU.mult).then_inc(s_mult, 1)
            jobs = []
            self.rows_added(jobs, QT, w["proj"], w["b"], self.x, k=QK)
            self.products(jobs)


STAGES = ["L0_attn", "L0_xattn", "L0_ffn", "L1_attn", "L1_xattn", "L1_ffn",
          "L2_attn", "L2_xattn", "L2_ffn", "L3_attn", "L3_xattn", "L3_ffn"]


def decoder_kernel(nc, dram, where, x, seg, out):
    k = Kernel(nc, dram, where, x, out, seg)
    k.start()
    k.L0_attn()
    k.L0_xattn()
    k.L0_ffn()
    k.L1_attn()
    k.L1_xattn()
    k.L1_ffn()
    k.L2_attn()
    k.L2_xattn()
    k.L2_ffn()
    k.L3_attn()
    k.L3_xattn()
    k.L3_ffn()
    k.finish()


def kernel(**inputs):
    import concourse.bacc as bacc
    from concourse.bass_utils import run_bass_kernel_spmd

    nc = bacc.Bacc("TRN2", target_bir_lowering=False, num_devices=1)
    arrays, dram, where = {}, {}, {}

    def give(name, a):
        a = np.ascontiguousarray(a)
        arrays["in_" + name] = a
        return nc.dram_tensor("in_" + name, a.shape, mybir.dt.from_np(a.dtype), kind="ExternalInput").ap()

    for stage, one in stage_arrays(inputs).items():
        many = isinstance(one, list)
        where[stage] = layout_of(one[0] if many else one)
        dram[stage] = give(stage, np.stack([pack(o, *where[stage]) for o in one]) if many else pack(one, *where[stage]))
    x = give("x", np.asarray(inputs["x"]))
    seg = give("seg", np.asarray(inputs["itok_BxS_0_255"]).reshape(NT, P).T)
    out = nc.dram_tensor("out_0", (B, S, D), F32, kind="ExternalOutput").ap()
    decoder_kernel(nc, dram, where, x, seg, out)
    r = run_bass_kernel_spmd(nc, [arrays], core_ids=[0])
    return r.results[0]["out_0"]
```

```python
import math
from contextlib import ExitStack, contextmanager, nullcontext

import numpy as np

import concourse.bass as bass
from concourse import mybir
from concourse.alu_op_type import AluOpType as ALU

F32 = mybir.dt.float32
F32R = mybir.dt.float32r
BF16 = mybir.dt.bfloat16
I32 = mybir.dt.int32
U32 = mybir.dt.uint32
ACT = mybir.ActivationFunctionType
AX = mybir.AxisListType

B, S, D = 4, 256, 128
P = 128
NT = B * S // P
HALVES = S // P
SC = 64
H, HD = 16, 8
ROWG = 4
CH = 512
NCH = B * S // CH
NEG = -1e30
LAYERS = 4
E, F = 8, 512
FK = F // P
LW = 12
LT, LR = 2, 8 * LW
VW = 32
DK3 = 64
NF0 = 352
FT0 = [(0, 128), (128, 128), (256, 96)]
MIDS = [0.25, 0.75, 1.25, 1.75, 2.5, 3.5, 5.0]
GROUP = 32
INNER = 256


def constant_arrays():
    p = np.arange(P)
    c = {"ident": np.eye(P, dtype=np.float32)}
    half = np.zeros((P, P), np.float32)
    inter = np.zeros((P, P), np.float32)
    for m in range(P):
        d = m % HD
        if d < HD // 2:
            half[m + HD // 2, m] = -1.0
        else:
            half[m - HD // 2, m] = 1.0
        if m % 2 == 0:
            inter[m + 1, m] = -1.0
        else:
            inter[m - 1, m] = 1.0
    c["rot_half"], c["rot_inter"] = half, inter
    t = np.arange(S, dtype=np.float32)
    inv8 = (1.0 / np.float32(10000.0) ** (np.arange(0, HD, 2, dtype=np.float32) / np.float32(HD))).astype(np.float32)
    ang8 = inv8[(p % HD) % (HD // 2)][:, None] * t[None]
    latent = (p % LW) >= HD
    inv4 = (np.float32(10000.0) ** (-np.arange(0, 4, 2, dtype=np.float32) / np.float32(4))).astype(np.float32)
    ang12 = np.where(latent, inv4[((p % LW - HD) % 4) // 2], 0)[:, None].astype(np.float32) * t[None]
    c["cos8"], c["sin8"], c["cos12"], c["sin12"] = np.cos(ang8), np.sin(ang8), np.cos(ang12)[:LR], np.sin(ang12)[:LR]
    c["cos8q"], c["sin8q"] = c["cos8"] * np.float32(HD ** -0.5), c["sin8"] * np.float32(HD ** -0.5)
    c["mask8"] = np.stack([(p % 32) // 8 == j for j in range(4)], 1)
    c["mask16"] = np.stack([p // 8 == h for h in range(H)], 1)
    c["mask12"] = np.stack([(p[:LR] % (2 * LW)) // LW == j for j in range(2)], 1)
    c["causal_neg"] = np.where(p[None] <= p[:, None], 0.0, NEG)
    c["causal_one"] = (p[:, None] <= p[None]).astype(np.float32)
    q, k = np.arange(S)[None], np.arange(S)[:, None]
    in_chunk = (q // GROUP == k // GROUP) & (k <= q)
    two = lambda a: np.concatenate([a[:P], a[P:]], 1).astype(np.float32)
    c["in_chunk"] = two(in_chunk)
    c["older_chunk"] = two(k // GROUP < q // GROUP)
    c["distance"] = two(np.maximum(q - k, 0))
    c["iota8"] = np.tile(np.arange(E), (P, 1))
    c["keys"] = np.tile(np.arange(SC), (P, 1))
    c["minus_half"] = np.full((P, NT), -0.5)
    c["ones_row"] = np.ones((1, P))
    return {k: np.asarray(v, np.float32) for k, v in c.items()}


def selection_arrays():
    c = {}
    for name, parts in (("high_a", (0, 2)), ("low_a", (1, 3)), ("high_b", (0, 1)), ("low_b", (2, 3))):
        for rows in (P, LR):
            g = rows // ROWG
            sel = np.zeros((rows, ROWG, rows), np.float32)
            for i in range(ROWG):
                for part in parts:
                    for r in range(g):
                        sel[g * i + r, i, g * part + r] = 1.0
            c[f"{name}{rows}"] = sel.reshape(rows, -1)
    return c


def tiles(a):
    k = a.shape[0] // P
    return a.reshape(k, P, -1).transpose(1, 0, 2).reshape(P, -1)


def col(v):
    v = np.asarray(v)
    return v.reshape(-1, min(P, v.size)).T


def row(v):
    return np.asarray(v).reshape(1, -1)


def spread(v):
    return np.broadcast_to(np.asarray(v).reshape(1, -1), (P, np.asarray(v).size))


def stage_arrays(a):
    g = lambda n: np.asarray(a[n])
    ctx = g("ctx_1024")
    ctxT = ctx.transpose(2, 0, 1)
    out = {}
    out["const"] = constant_arrays()
    out["selections"] = selection_arrays()
    out["ctx"] = {
        "ctxT": ctxT.reshape(D, B * SC),
        "ctxT2": np.broadcast_to(ctxT[:, :, None], (D, B, 2, SC)).reshape(D, -1),
        "keep": spread(g("mask_BxS2_ff1")),
    }
    out["L0_attn"] = {n: g("L0_attn_" + n) for n in ("Wv", "Wg", "Win")}
    out["L0_attn"].update(
        Wout=tiles(g("L0_attn_Wout")), bv=row(g("L0_attn_bv")), bg=col(g("L0_attn_bg")),
        bin=col(g("L0_attn_bin_")), bout=row(g("L0_attn_bout")),
        **{n: col(g("L0_attn_" + n)) for n in ("g_qq", "b_qq", "g_qk", "b_qk", "g_lq", "b_lq", "g_lk", "b_lk")})
    out["L0_xattn"] = {n: g("L0_xattn_" + n).T for n in ("Wq", "Wk", "Wv", "Wo")}
    out["L0_xattn"].update(bq=col(g("L0_xattn_bq")), bk=col(g("L0_xattn_bk")), bv=row(g("L0_xattn_bv")),
                           bo=row(g("L0_xattn_bo")))
    w0 = {}
    for n in ("w_gate", "w_up"):
        w = g("L0_ffn_" + n)
        for i, (f0, fn) in enumerate(FT0):
            w0[f"{n}{i}"] = w[f0:f0 + fn]
    w0["w_down"] = g("L0_ffn_w_down")
    out["L0_ffn"] = w0
    out["L1_attn"] = {n: g("L1_attn_" + n) for n in ("W_DQ", "W_DKV", "W_UV", "W_O")}
    heads12 = lambda plain, rotated: np.concatenate([plain.reshape(-1, H, HD), rotated.reshape(-1, H, LW - HD)], 2).reshape(-1, H * LW)
    out["L1_attn"].update(
        W_Q=heads12(g("L1_attn_W_UQ"), g("L1_attn_W_QR")),
        W_KC=heads12(g("L1_attn_W_UK"), np.zeros((32, H * (LW - HD)), np.float32)),
        W_KR=heads12(np.zeros((D, D), np.float32), np.tile(g("L1_attn_W_KR"), (1, H))))
    x1 = {n: g("L1_xattn_" + n) for n in ("Wqkv", "bqkv", "Wo", "bo", "Wq_c", "Wkv_c", "Wo_c", "Wg", "Wu", "Wd",
                                           "n1", "n2", "n3")}
    out["inner_attn"] = [
        {"Wq": x1["Wqkv"][l, :D].T, "Wk": x1["Wqkv"][l, D:2 * D].T, "Wv": x1["Wqkv"][l, 2 * D:].T,
         "bq": col(x1["bqkv"][l, :D]), "bk": col(x1["bqkv"][l, D:2 * D]), "bv": row(x1["bqkv"][l, 2 * D:]),
         "Wo": x1["Wo"][l].T, "bo": row(x1["bo"][l]), "Wq_c": x1["Wq_c"][l].T, "Wk_c": x1["Wkv_c"][l, :D].T,
         "Wv_c": x1["Wkv_c"][l, D:].T, "Wo_c": x1["Wo_c"][l].T, "n1": col(x1["n1"][l]), "n2": col(x1["n2"][l])}
        for l in [*range(LAYERS), 0]]
    out["inner_ffn"] = [
        {"Wg": x1["Wg"][l].T, "Wu": x1["Wu"][l].T, "Wd": tiles(x1["Wd"][l].T), "n3": col(x1["n3"][l])}
        for l in range(LAYERS)]
    out["inner_misc"] = {"nf": spread(g("L1_xattn_nf"))}
    out["L1_ffn"] = {"Wr": g("L1_ffn_Wr").T}
    out["L1_experts"] = [{"Wg": g("L1_ffn_Wg")[e].T, "Wu": g("L1_ffn_Wu")[e].T, "Wd": tiles(g("L1_ffn_Wd")[e].T)}
                         for e in [*range(E), 0]]
    out["L2_attn"] = {n: g("L2_attn_" + n).T for n in ("Wq", "Wk", "Wv", "Wo")}
    kv1, kv2 = g("L2_xattn_kv1_w"), g("L2_xattn_kv2_w")
    out["L2_xattn"] = {
        "q1": g("L2_xattn_q1_w").T, "q2": g("L2_xattn_q2_w").T, "k1": kv1[:D].T, "v1": kv1[D:].T, "k2": kv2[:D].T,
        "proj": g("L2_xattn_proj_w").T, "b": row(g("L2_xattn_proj_b")), "norm": col(g("L2_xattn_norm_w")),
        "l1": spread(g("L2_xattn_lambda_1")), "l2": spread(g("L2_xattn_lambda_2"))}
    out["L2_ffn"] = {"Wr": g("L2_ffn_Wr"), "br": row(g("L2_ffn_br")), "b2": g("L2_ffn_b2")}
    out["L2_experts"] = [{"W1": g("L2_ffn_W1")[e], "b1": col(g("L2_ffn_b1")[e]), "W2": tiles(g("L2_ffn_W2")[e])}
                         for e in [*range(E), 0]]
    out["L3_attn"] = {n: g("L3_attn_" + n).T for n in ("Wq", "Wk", "Wv", "Wg")}
    out["L3_attn"].update(bq=col(g("L3_attn_bq")), bk=col(g("L3_attn_bk")), bv=row(g("L3_attn_bv")),
                          bg=row(g("L3_attn_bg")), gamma=spread(g("L3_attn_gamma")))
    heads = lambda w: g(w).transpose(1, 0, 2).reshape(D, H * DK3)
    out["L3_xattn"] = {"Wq": heads("L3_xattn_w_qs"), "Wk": heads("L3_xattn_w_ks"), "Wv": heads("L3_xattn_w_vs"),
                       "proj": tiles(g("L3_xattn_w_proj").T), "b": row(g("L3_xattn_b_proj"))}
    out["L3_ffn"] = {"Wr": g("L3_ffn_router_w").T, "br": row(g("L3_ffn_router_b")), "b2": g("L3_ffn_b2")}
    out["L3_experts"] = [{"W1": g("L3_ffn_w1")[e].T, "b1": col(g("L3_ffn_b1")[e]), "W2": tiles(g("L3_ffn_w2")[e].T)}
                         for e in [*range(E), 0]]
    return out


def layout_of(arrays):
    at, where = 0, {}
    for name, v in arrays.items():
        where[name] = (v.shape[0], at, v.shape[1])
        at += v.shape[1]
    return where, at


def pack(arrays, where, width):
    out = np.zeros((P, width), np.float32)
    for name, v in arrays.items():
        p, at, n = where[name]
        out[:p, at:at + n] = v
    return out


class Pack:

    def __init__(self, buf, where):
        self.buf, self.where = buf, where

    def __getitem__(self, name):
        p, at, n = self.where[name]
        return self.buf[0:p, at:at + n]


class Phase:

    def __init__(self, nc):
        self.nc, self.sems = nc, []

    def sem(self, name):
        s = self.nc.alloc_semaphore(f"{name}_{self.nc.next_id()}")
        self.sems.append(s)
        return s

    def __enter__(self):
        return self

    def __exit__(self, kind, *_):
        if kind is None:
            self.nc.clear_and_free_semaphores(self.sems)
            self.nc.all_engine_barrier()


def link(eng, sem, count, ins):
    count[0] += 1
    ins.then_inc(sem, 1)
    eng.wait_ge(sem, count[0])


class Kernel:
    def __init__(self, nc, dram, where, x_dram, out_dram, seg_dram):
        self.nc, self.dram, self.where = nc, dram, where
        self.x_dram, self.out_dram, self.seg_dram = x_dram, out_dram, seg_dram
        self.stack = ExitStack()

    def sb(self, name, shape, dt=F32):
        return self.nc.sbuf_tensor(f"{name}_{self.nc.next_id()}", shape, dt)

    def keep(self, name, shape, dt=F32):
        return self.stack.enter_context(self.sb(name, shape, dt))

    def bank(self, n, count=1):
        return self.ps[:, n * CH:(n + count) * CH]

    def start(self):
        nc = self.nc
        self.s_out = nc.alloc_semaphore("output_written")
        self.ps = self.stack.enter_context(nc.psum_tensor("ps", [P, 8 * CH], F32))
        self.x = self.keep("x", [P, NT, D])
        self.xT = self.keep("xT", [P, NT * P])
        self.nrm = self.keep("nrm", [P, NT, D])
        cwhere, cwidth = self.where["const"]
        xwhere, xwidth = self.where["ctx"]
        cbuf = self.keep("constants", [P, cwidth])
        xbuf = self.keep("context", [P, xwidth])
        self.c, self.ctx = Pack(cbuf, cwhere), Pack(xbuf, xwhere)
        self.identb = self.keep("identb", [P, P], BF16)
        self.causalb = self.keep("causalb", [P, P], BF16)
        self.sel = {f"{n}{r}": self.keep(n, [r, ROWG, r], F32R) for r in (P, LR) for n in ("high_a", "low_a", "high_b", "low_b")}
        self.keepb = self.keep("keepb", [P, B, SC], BF16)
        self.tmp_keep = self.keep("tmp_keep", [P, B * SC])
        swhere, swidth = self.where["selections"]
        with self.sb("selections", [P, swidth]) as sbuf, Phase(nc) as ph:
            csel = Pack(sbuf, swhere)
            s_load, s_cast, s_mul = ph.sem("load"), ph.sem("cast"), ph.sem("mul")
            s_sel = ph.sem("selections")
            with nc.Block() as block:
                @block.scalar
                def _(act):
                    act.wait_ge(s_load, 64)
                    for name, sel in self.sel.items():
                        act.activation(sel[:, :, :], csel[name], ACT.Copy).then_inc(s_sel, 1)

                @block.sync
                def _(sp):
                    sp.dma_start(self.x[:, :, :], self.x_dram.rearrange("b (h p) d -> p (b h) d", p=P)).then_inc(s_load, 16)
                    sp.dma_start(xbuf[:, :], self.dram["ctx"][:, :]).then_inc(s_load, 16)
                    sp.dma_start(cbuf[:, :], self.dram["const"][:, :]).then_inc(s_load, 16)
                    sp.dma_start(sbuf[:, :], self.dram["selections"][:, :]).then_inc(s_load, 16)
                    sp.wait_ge(s_load, 64)

                @block.vector
                def _(dve):
                    dve.wait_ge(s_load, 64)
                    dve.tensor_copy(self.identb[:, :], self.c["ident"]).then_inc(s_cast, 1)
                    dve.tensor_copy(self.causalb[:, :], self.c["causal_neg"]).then_inc(s_cast, 1)
                    dve.tensor_scalar(self.tmp_keep[:, :], self.ctx["keep"], 1.0, NEG, ALU.not_equal, ALU.mult).then_inc(s_mul, 1)
                    dve.wait_ge(s_mul, 1)
                    dve.tensor_copy(self.keepb[:, :, :], self.tmp_keep[:, :].rearrange("p (b k) -> p b k", b=B)).then_inc(s_cast, 1)
                    dve.wait_ge(s_cast, 3)

    def finish(self):
        nc = self.nc
        s_out = self.s_out
        with nc.Block() as block:
                @block.sync
                def _(sp):
                    sp.dma_start(self.out_dram.rearrange("b (h p) d -> p (b h) d", p=P), self.x[:, :, :]).then_inc(s_out, 16)
                    sp.wait_ge(s_out, 16)
        self.stack.close()

    @contextmanager
    def weights(self, stage):
        where, width = self.where[stage]
        with self.sb("w_" + stage, [P, width]) as buf:
            with Phase(self.nc) as ph:
                s_w = ph.sem("weights")
                with self.nc.Block() as block:
                    @block.sync
                    def _(sp):
                        sp.dma_start(buf[:, :], self.dram[stage][:, :]).then_inc(s_w, 16)
                        sp.wait_ge(s_w, 16)
            yield Pack(buf, where)

    def norm(self, src, dst, dstT, layer=True, eps=1e-5, weight=None):
        nc = self.nc
        with self.sb("stats", [P, NT, 6]) as stats, self.sb("mv", [P, NT, 2]) as mv, \
                self.sb("var", [P, NT]) as var, self.sb("rstd", [P, NT]) as rstd, self.sb("sq", [P, NT, D]) as sq, Phase(nc) as ph:
            s_chain, s_var, s_rstd = ph.sem("chain"), ph.sem("var"), ph.sem("rstd")
            s_norm, s_turn, s_copy = ph.sem("norm"), ph.sem("turn"), ph.sem("copy")
            with nc.Block() as block:
                @block.vector
                def _(dve):
                    n = [0]
                    if layer:
                        for t in range(NT):
                            dve.bn_stats(stats[:, t, :], src[:, t, :]).then_inc(s_chain, 1)
                        dve.wait_ge(s_chain, NT)
                        for t in range(NT):
                            dve.bn_aggr(mv[:, t, :], stats[:, t, :]).then_inc(s_chain, 1)
                        dve.wait_ge(s_chain, 2 * NT)
                        dve.tensor_scalar(var[:, :], mv[:, :, 1], eps, None, ALU.add).then_inc(s_var, 1)
                    else:
                        dve.tensor_tensor(sq[:, :, :], src[:, :, :], src[:, :, :], ALU.mult).then_inc(s_chain, 1)
                        dve.wait_ge(s_chain, 1)
                        dve.tensor_reduce(rstd[:, :], sq[:, :, :], AX.X, ALU.add).then_inc(s_chain, 1)
                        dve.wait_ge(s_chain, 2)
                        dve.tensor_scalar(var[:, :], rstd[:, :], 1.0 / D, eps, ALU.mult, ALU.add).then_inc(s_var, 1)
                    dve.wait_ge(s_rstd, 1)
                    for t in range(NT):
                        if layer:
                            ins = dve.tensor_scalar(dst[:, t, :], src[:, t, :], mv[:, t, 0:1], rstd[:, t:t + 1],
                                                    ALU.subtract, ALU.mult)
                        else:
                            ins = dve.tensor_scalar(dst[:, t, :], src[:, t, :], rstd[:, t:t + 1], None, ALU.mult)
                        ins.then_inc(s_norm, 1)

                @block.gpsimd
                def _(pool):
                    pool.wait_ge(s_var, 1)
                    pool.tensor_tensor(rstd[:, :], var[:, :], self.c["minus_half"], ALU.pow).then_inc(s_rstd, 1)

                if dstT is not None:
                    @block.tensor
                    def _(pe):
                        for t in range(NT):
                            pe.wait_ge(s_norm, t + 1)
                            pe.transpose(self.ps[:, t * P:(t + 1) * P], dst[:, t, :], self.c["ident"]).then_inc(s_turn, 1)

                    @block.scalar
                    def _(act):
                        for g in range(NCH):
                            act.wait_ge(s_turn, (g + 1) * NT // NCH)
                            cols = slice(g * CH, (g + 1) * CH)
                            if weight is None:
                                act.activation(dstT[:, cols], self.ps[:, cols], ACT.Copy).then_inc(s_copy, 1)
                            else:
                                act.activation(dstT[:, cols], self.ps[:, cols], ACT.Copy, scale=weight).then_inc(s_copy, 1)

    def products(self, jobs):
        nc = self.nc
        R = 8
        engine = [ev[0] for _, ev, _ in jobs]
        nth = [engine[:n + 1].count(engine[n]) for n in range(len(jobs))]
        with Phase(nc) as ph:
            s_product = ph.sem("product")
            s_taken = {"act": ph.sem("taken_act"), "dve": ph.sem("taken_dve")}
            s_chain = ph.sem("chain")
            with nc.Block() as block:
                @block.tensor
                def _(pe):
                    for n, (mms, ev, after) in enumerate(jobs):
                        if n >= R:
                            pe.wait_ge(s_taken[engine[n - R]], nth[n - R])
                        if after is not None:
                            pe.wait_ge(s_taken[engine[after]], nth[after])
                        bank = self.bank(n % R)
                        for c0, c1, rows, lhsT, rhs, start, stop in mms:
                            last = pe.matmul(bank[0:rows, c0:c1], lhsT, rhs, start=start, stop=stop)
                        last.then_inc(s_product, 1)

                @block.scalar
                def _(act):
                    for n, (_, ev, _) in enumerate(jobs):
                        if ev[0] != "act":
                            continue
                        act.wait_ge(s_product, n + 1)
                        _, func, dst, pick, bias, scale = ev
                        src = pick(self.bank(n % R))
                        act.activation(dst, src, func, bias=bias, scale=scale).then_inc(s_taken["act"], 1)

                @block.vector
                def _(dve):
                    chain = [0]
                    for n, (_, ev, _) in enumerate(jobs):
                        if ev[0] != "dve":
                            continue
                        dve.wait_ge(s_product, n + 1)
                        kind, dst, pick = ev[1:4]
                        src = pick(self.bank(n % R))
                        if kind == "copy":
                            ins = dve.tensor_copy(dst, src)
                        elif kind == "affine":
                            ins = dve.tensor_scalar(dst, src, ev[4], ev[5], ALU.add, ALU.mult)
                        elif kind == "mult":
                            if len(ev) > 5:
                                dve.wait_ge(s_taken["act"], nth[ev[5]])
                            ins = dve.tensor_tensor(dst, src, ev[4], ALU.mult)
                        elif kind == "add":
                            ins = dve.tensor_tensor(dst, src, ev[4], ALU.add)
                        elif kind == "rope":
                            raw, cos, sin = ev[4:7]
                            link(dve, s_chain, chain, dve.tensor_tensor(dst, raw, cos, ALU.mult))
                            link(dve, s_chain, chain, dve.tensor_tensor(raw, src, sin, ALU.mult))
                            ins = dve.tensor_tensor(dst, dst, raw, ALU.add)
                        ins.then_inc(s_taken["dve"], 1)

    @staticmethod
    def whole(rows=P, cols=CH):
        return lambda bank: bank[0:rows, 0:cols]

    @staticmethod
    def rows_of_heads(width):
        return lambda bank: bank[:, :].rearrange("p (t h d) -> p t h d", h=H, d=HD)

    def turned(self, W, src, dst, m=P, bias=0.0, scale=1.0, func=ACT.Identity, eng="act", width=B * S):
        jobs = []
        step = min(CH, width)
        for c in range(0, width, step):
            cols = slice(c, c + step)
            mms = [(0, step, m, W, src[:, cols], True, True)]
            pick = self.whole(m, step)
            if eng == "act":
                jobs.append((mms, ("act", func, dst[:, cols], pick, bias, scale), None))
            elif isinstance(bias, float):
                jobs.append((mms, ("dve", "copy", dst[:, cols], pick), None))
            else:
                jobs.append((mms, ("dve", "affine", dst[:, cols], pick, bias, scale), None))
        return jobs

    def roped(self, jobs, sources, dst, raw, rot, cos, sin, bias=0.0, m=P):
        first = len(jobs)
        two = lambda a: a.unsqueeze(1).to_broadcast([m, CH // S, S])
        v = lambda a: a.rearrange("p (b s) -> p b s", s=S)
        for c in range(NCH):
            cols = slice(c * CH, (c + 1) * CH)
            mms = [(0, CH, m, W, src[:, cols], k == 0, k == len(sources) - 1) for k, (W, src) in enumerate(sources)]
            jobs.append((mms, ("act", ACT.Identity, raw[:, cols], self.whole(m), bias, 1.0), None))
        for c in range(NCH):
            cols = slice(c * CH, (c + 1) * CH)
            jobs.append(([(0, CH, m, rot[0:m, 0:m], raw[:, cols], True, True)],
                         ("dve", "rope", v(dst[:, cols]), (lambda bank: v(bank[0:m, :])), v(raw[:, cols]), two(cos), two(sin)),
                         first + c))

    def value_rows(self, W, src, dst, bias=None, n=NT, k=P):
        jobs = []
        for g in range(0, n, 4):
            mms = []
            for t in range(g, min(g + 4, n)):
                c = (t - g) * P
                mms.append((c, c + P, P, src[0:k, t * P:(t + 1) * P], W, True, bias is None))
                if bias is not None:
                    mms.append((c, c + P, P, self.c["ones_row"], bias, False, True))
            jobs.append((mms, ("dve", "copy", dst[:, g:min(g + 4, n), :, 0:HD], self.rows_of_heads(n)), None))
        return jobs

    def stack_operands(self, plain, masked, masks, V=None, m=P, heads=4):
        nc = self.nc
        T = plain[0].shape[1]
        dst = masked[1]
        jobs = [(masked[0], dst[:, :, heads - 1, :], "b"), (*plain, "a")]
        units = [(n, t, i, c) for n in range(2) for t in range(T) for i in range(ROWG) for c in range(NCH)]
        with self.sb("high", [m, T, B * S], F32R) as high, self.sb("low", [m, T, B * S], F32R) as low, Phase(nc) as ph:
            s_high, s_low, s_product = ph.sem("high"), ph.sem("low"), ph.sem("product")
            s_plain, s_masked, s_v = ph.sem("plain"), ph.sem("masked"), ph.sem("values_padded")
            with nc.Block() as block:
                @block.scalar
                def _(act):
                    def split(n, t, c):
                        cols = slice(c * CH, (c + 1) * CH)
                        act.activation(high[:, t, cols], jobs[n][0][:, t, cols], ACT.Copy).then_inc(s_high, 1)

                    for t in range(T):
                        for c in range(NCH):
                            split(0, t, c)
                    for k, (n, t, i, c) in enumerate(units):
                        act.wait_ge(s_product, k + 1)
                        if n == 0 and i == ROWG - 1:
                            split(1, t, c)
                        act.activation(jobs[n][1][:, t * ROWG + i, c * CH:(c + 1) * CH], self.bank(k % 8)[0:m, :], ACT.Copy).then_inc(s_plain, 1)

                @block.vector
                def _(dve):
                    def split(n, t):
                        for c in range(NCH):
                            cols = slice(c * CH, (c + 1) * CH)
                            dve.wait_ge(s_high, (n * T + t) * NCH + c + 1)
                            if n == 1:
                                dve.wait_ge(s_product, units.index((0, t, ROWG - 1, c)) + 1)
                            dve.tensor_tensor(low[:, t, cols], jobs[n][0][:, t, cols], high[:, t, cols].bitcast(F32), ALU.subtract).then_inc(s_low, 1)

                    for t in range(T):
                        split(0, t)
                    for g in range(T * ROWG):
                        if g % ROWG == ROWG - 1:
                            split(1, g // ROWG)
                        dve.wait_ge(s_plain, (g + 1) * NCH)
                        st = dst[:, g, heads - 1, :].bitcast(F32)
                        for j in range(heads):
                            if j == heads - 1:
                                dve.wait_ge(s_masked, (g + 1) * heads - 1)
                            dve.tensor_scalar(dst[:, g, j, :], st, masks[:, j:j + 1], None, ALU.mult).then_inc(s_masked, 1)

                @block.tensor
                def _(pe):
                    for k, (n, t, i, c) in enumerate(units):
                        if k >= 8:
                            pe.wait_ge(s_plain, k - 7)
                        if i == 0:
                            pe.wait_ge(s_low, (n * T + t) * NCH + c + 1)
                        side = jobs[n][2]
                        cols = slice(c * CH, (c + 1) * CH)
                        bank = self.bank(k % 8)[0:m, :]
                        pe.matmul(bank, self.sel[f"high_{side}{m}"][:, i, :], high[:, t, cols], start=True, stop=False)
                        pe.matmul(bank, self.sel[f"low_{side}{m}"][:, i, :], low[:, t, cols], start=False, stop=True).then_inc(s_product, 1)

                if V is not None:
                    @block.gpsimd
                    def _(pool):
                        pool.memset(V[:, :, :, HD:HD + 1], 1.0).then_inc(s_v, 1)
                        pool.memset(V[:, :, :, HD + 1:VW], 0.0).then_inc(s_v, 1)

    def expand_context(self, src, dst):
        nc = self.nc
        mask = self.c["mask16"]
        with Phase(nc) as ph:
            s_a, s_v, s_p = ph.sem("expand_act"), ph.sem("expand_dve"), ph.sem("expand_pool")

            def part(eng, hs):
                k = hs.stop - hs.start
                return eng.tensor_tensor(dst[:, hs, :], src[:, :].unsqueeze(1).to_broadcast([P, k, B * SC]),
                                         mask[:, hs].unsqueeze(2).to_broadcast([P, k, B * SC]), ALU.mult)

            with nc.Block() as block:
                @block.scalar
                def _(act):
                    for h in range(0, 5):
                        act.activation(dst[:, h, :], src[:, :], ACT.Copy, scale=mask[:, h:h + 1]).then_inc(s_a, 1)

                @block.vector
                def _(dve):
                    part(dve, slice(5, 12)).then_inc(s_v, 1)

                @block.gpsimd
                def _(pool):
                    part(pool, slice(12, H)).then_inc(s_p, 1)

    def attend(self, Qs, Kx, V, O):
        nc = self.nc
        units = [(b, q, i) for b in range(B) for q in range(HALVES) for i in range(ROWG)]
        N = len(units)
        first_pt, n_pt = {}, 0
        for n, (b, q, i) in enumerate(units):
            first_pt[n] = n_pt
            n_pt += q + 1
        with self.sb("probs", [P, 2, 2, 4, P]) as pr, self.sb("probsT", [P, 4, 4, P]) as pT, \
                self.sb("nmax", [P, 2, 4]) as nmax, self.sb("rsum", [P, 2, ROWG, 4]) as rsum, \
                self.sb("outT", [P, 2, ROWG, P]) as oT, Phase(nc) as ph:
            s_scores, s_max, s_exp = ph.sem("scores"), ph.sem("max"), ph.sem("exp")
            s_turn, s_pt, s_out, s_ot = ph.sem("turn"), ph.sem("pt"), ph.sem("out"), ph.sem("out_copied")
            s_back, s_rec, s_norm = ph.sem("turned_back"), ph.sem("rec"), ph.sem("norm")

            def sbank(n):
                return self.bank(2 * (n % 2), 2)

            obank, rbank = self.bank(6), self.bank(7)

            with nc.Block() as block:
                @block.tensor
                def _(pe):
                    def scores(n):
                        b, q, i = units[n]
                        if n >= 2:
                            pe.wait_ge(s_exp, 4 * (n - 1))
                        qs = Qs[:, i, b * S + q * P:b * S + (q + 1) * P]
                        for kb in range(q + 1):
                            o = sbank(n)[:, kb * CH:(kb + 1) * CH]
                            diag = kb == q
                            last = pe.matmul(o, qs, Kx[:, i, :, b * S + kb * P:b * S + (kb + 1) * P],
                                             start=True, stop=not diag)
                            if diag:
                                last = pe.matmul(o, self.identb[:, :],
                                                 self.causalb[:, :].unsqueeze(1).to_broadcast([P, 4, P]),
                                                 start=False, stop=True)
                        last.then_inc(s_scores, 1)

                    def turn(n):
                        b, q, i = units[n]
                        for kb in range(q + 1):
                            m = first_pt[n] + kb
                            if m >= 2:
                                pe.wait_ge(s_pt, m - 1)
                            for j in range(4):
                                if kb == 0:
                                    pe.wait_ge(s_exp, 4 * n + j + 1)
                                last = pe.transpose(self.bank(4 + m % 2)[:, j * P:(j + 1) * P], pr[:, n % 2, kb, j, :],
                                                    self.c["ident"])
                            last.then_inc(s_turn, 1)

                    def out(n):
                        b, q, i = units[n]
                        g = n // ROWG
                        if i == 0 and g >= 1:
                            pe.wait_ge(s_ot, g)
                        pe.wait_ge(s_pt, first_pt[n] + q + 1)
                        for kb in range(q + 1):
                            m = first_pt[n] + kb
                            for j in range(4):
                                last = pe.matmul(obank[32 * j:32 * j + 32, i * P:(i + 1) * P], V[:, 2 * b + kb, 4 * i + j, :],
                                                 pT[:, m % 4, j, :], start=(kb == 0), stop=(kb == q))
                        last.then_inc(s_out, 1)

                    def back(g):
                        pe.wait_ge(s_ot, g + 1)
                        if g >= 1:
                            pe.wait_ge(s_norm, g)
                        for i in range(ROWG):
                            last = pe.transpose(rbank[:, i * P:(i + 1) * P], oT[:, g % 2, i, :], self.c["ident"])
                        last.then_inc(s_back, 1)

                    for n in range(N + 3):
                        if n < N:
                            scores(n)
                        if 1 <= n <= N:
                            turn(n - 1)
                        if n >= 6 and (n - 2) % ROWG == 0:
                            back((n - 2) // ROWG - 1)
                        if 2 <= n < N + 2:
                            out(n - 2)

                @block.scalar
                def _(act):
                    for n in range(N + 2):
                        if n < N:
                            b, q, i = units[n]
                            act.wait_ge(s_max, n + 1)
                            if n >= 2:
                                act.wait_ge(s_turn, first_pt[n - 1])
                            s = sbank(n)[:, 0:(q + 1) * CH].rearrange("p (k j c) -> p j k c", j=4, c=P)
                            for j in range(4):
                                act.activation(pr[:, n % 2, 0:q + 1, j, :], s[:, j, :, :], ACT.Exp,
                                               bias=nmax[:, n % 2, j:j + 1]).then_inc(s_exp, 1)
                        if n >= 5 and (n - 1) % ROWG == 0:
                            g = (n - 1) // ROWG - 1
                            act.wait_ge(s_out, ROWG * (g + 1))
                            if g >= 2:
                                act.wait_ge(s_back, g - 1)
                            act.activation(oT[:, g % 2, :, :], obank, ACT.Copy).then_inc(s_ot, 1)

                @block.vector
                def _(dve):
                    def copies(n):
                        b, q, i = units[n]
                        for kb in range(q + 1):
                            m = first_pt[n] + kb
                            if n >= 2 and kb == 0:
                                dve.wait_ge(s_out, n - 1)
                            dve.wait_ge(s_turn, m + 1)
                            dve.tensor_copy(pT[:, m % 4, :, :], self.bank(4 + m % 2)[:, :]).then_inc(s_pt, 1)

                    def normalise(g):
                        dve.wait_ge(s_back, g + 1)
                        o = rbank.rearrange("p (i j d) -> p i j d", i=ROWG, d=VW)
                        dve.reciprocal(rsum[:, g % 2, :, :], o[:, :, :, HD]).then_inc(s_rec, 1)
                        dve.wait_ge(s_rec, g + 1)
                        dve.tensor_tensor(O[:, g, :].rearrange("p (h d) -> p h d", d=HD), rbank.rearrange("p (h d) -> p h d", d=VW)[:, :, 0:HD],
                                          rsum[:, g % 2, :, :].rearrange("p i j -> p (i j)").unsqueeze(2).to_broadcast([P, H, HD]), ALU.mult).then_inc(s_norm, 1)

                    for n in range(N + 3):
                        if n < N:
                            b, q, i = units[n]
                            dve.wait_ge(s_scores, n + 1)
                            if n >= 2:
                                dve.wait_ge(s_exp, 4 * (n - 1))
                            s = sbank(n)[:, 0:(q + 1) * CH].rearrange("p (k j c) -> p j k c", j=4, c=P)
                            dve.tensor_reduce(nmax[:, n % 2, :], s, AX.XY, ALU.max, negate=True).then_inc(s_max, 1)
                        if 1 <= n <= N:
                            copies(n - 1)
                        if n >= 6 and (n - 2) % ROWG == 0:
                            normalise((n - 2) // ROWG - 1)

    def attend_context(self, score, V, width, O, bias=None, per_token=False, combine=None):
        nc = self.nc
        V1 = width + 1
        wide = width > HD
        G = 4 if wide else 2
        HG = H // G
        tile_of = (lambda h: (h % 4) // 2) if wide else (lambda h: h % 2)
        block_of = (lambda h: (h % 2) * 4 + h // 4) if wide else (lambda h: h // 2)
        with self.sb("sub", [P, 2, H, SC]) as sub, self.sb("probsX", [P, 2, H, SC]) as pr, \
                self.sb("probsXT", [P, 2, H // 2, P]) as pT, self.sb("nmaxX", [P, 2, H]) as nmax, \
                self.sb("rsumX", [P, 2, G, HG]) as rsum, self.sb("part", [P, 2, H, width]) as part, Phase(nc) as ph:
            s_scores, s_max, s_sub, s_exp = ph.sem("scores"), ph.sem("max"), ph.sem("sub"), ph.sem("exp")
            s_turn, s_pt, s_out, s_rec = ph.sem("turn"), ph.sem("pt"), ph.sem("out"), ph.sem("rec")
            s_norm, s_ones = ph.sem("norm"), ph.sem("ones")
            chain = ph.sem("chain")

            def out_at(h):
                c = (4 + h % G) * CH + (h // G) * V1
                return self.ps[:, c:c + V1]

            with nc.Block() as block:
                @block.gpsimd
                def _(pool):
                    pool.memset(V[:, :, :, width:V1], 1.0).then_inc(s_ones, 1)

                @block.tensor
                def _(pe):
                    pe.wait_ge(s_ones, 1)

                    def turn(t):
                        pe.wait_ge(s_exp, t + 1)
                        if t >= 1:
                            pe.wait_ge(s_pt, t)
                        for p2 in range(H // 2):
                            last = pe.transpose(self.bank(2, 2)[:, p2 * P:(p2 + 1) * P],
                                                pr[:, t % 2, 2 * p2:2 * p2 + 2, :], self.c["ident"])
                        last.then_inc(s_turn, 1)

                    def out(t):
                        pe.wait_ge(s_pt, t + 1)
                        if t >= 1:
                            pe.wait_ge(s_norm, t)
                        for h in range(H):
                            r = slice(SC * tile_of(h), SC * tile_of(h) + SC)
                            last = pe.matmul(out_at(h), pT[r, t % 2, block_of(h), :], V[r, t // HALVES, h, :], start=True, stop=True)
                        last.then_inc(s_out, 1)

                    for t in range(NT + 2):
                        if t < NT:
                            if t >= 1:
                                pe.wait_ge(s_sub, t)
                            banks = self.bank(0, 2)
                            if bias is not None:
                                bt = bias[:, t, :] if per_token else bias[:, t // HALVES, :]
                                for g in range(2):
                                    pe.matmul(banks[:, g * CH:(g + 1) * CH], self.identb[:, :],
                                              bt.unsqueeze(1).to_broadcast([P, H // 2, SC]), start=True, stop=False)
                            score(pe, t, banks, bias is None).then_inc(s_scores, 1)
                        if 1 <= t <= NT:
                            turn(t - 1)
                        if t >= 2:
                            out(t - 2)

                @block.scalar
                def _(act):
                    def copy(t):
                        act.wait_ge(s_turn, t + 1)
                        if t >= 2:
                            act.wait_ge(s_out, t - 1)
                        act.activation(pT[:, t % 2, :, :], self.bank(2, 2), ACT.Copy).then_inc(s_pt, 1)

                    for t in range(NT + 1):
                        if t < NT:
                            act.wait_ge(s_sub, t + 1)
                            if t >= 2:
                                act.wait_ge(s_turn, t - 1)
                            act.activation(pr[:, t % 2, :, :], sub[:, t % 2, :, :], ACT.Exp).then_inc(s_exp, 1)
                        if t >= 1:
                            copy(t - 1)

                @block.vector
                def _(dve):
                    def normalise(t):
                        dve.wait_ge(s_out, t + 1)
                        out_bank = lambda g: self.bank(4 + g)[:, 0:HG * V1].rearrange("p (h d) -> p h d", d=V1)
                        for g in range(G):
                            last = dve.reciprocal(rsum[:, t % 2, g, :], out_bank(g)[:, :, width])
                        last.then_inc(s_rec, 1)
                        dve.wait_ge(s_rec, (t + 1) if combine is None else (2 * t + 1))
                        if combine is not None:
                            dve.tensor_tensor(rsum[:, t % 2, :, :], rsum[:, t % 2, :, :],
                                              combine.rearrange("p (h g) -> p g h", g=G), ALU.mult).then_inc(s_rec, 1)
                            dve.wait_ge(s_rec, 2 * t + 2)
                        for g in range(G):
                            r = rsum[:, t % 2, g, :].unsqueeze(2).to_broadcast([P, HG, width])
                            d = O[:, t, g:H:G, :] if combine is None else part[:, t % 2, g:H:G, :]
                            last = dve.tensor_tensor(d, out_bank(g)[:, :, 0:width], r, ALU.mult)
                        last.then_inc(s_norm, 1)
                        if combine is not None:
                            dve.wait_ge(s_norm, t + 1)
                            dve.tensor_tensor(O[:, t, :, :], O[:, t, :, :], part[:, t % 2, :, :], ALU.subtract).then_inc(chain, 1)

                    for t in range(NT + 2):
                        if t < NT:
                            s = self.bank(0, 2).rearrange("p (h k) -> p h k", k=SC)
                            dve.wait_ge(s_scores, t + 1)
                            dve.tensor_reduce(nmax[:, t % 2, :], s, AX.X, ALU.max, negate=True).then_inc(s_max, 1)
                            dve.wait_ge(s_max, t + 1)
                            if t >= 2:
                                dve.wait_ge(s_exp, t - 1)
                            dve.tensor_tensor(sub[:, t % 2, :, :], s,
                                              nmax[:, t % 2, :].unsqueeze(2).to_broadcast([P, H, SC]), ALU.add).then_inc(s_sub, 1)
                        if t >= 2:
                            normalise(t - 2)

    def head_scores(self, QT, Kx):
        def score(pe, t, banks, first):
            b = t // HALVES
            for g in range(2):
                last = pe.matmul(banks[:, g * CH:(g + 1) * CH], QT[:, t * P:(t + 1) * P],
                                 Kx[:, g * H // 2:(g + 1) * H // 2, b * SC:(b + 1) * SC], start=first, stop=True)
            return last
        return score

    def project(self, src, W, bias, dst, scale=None, gateT=None):
        nc = self.nc
        with self.sb("srcT", [P, NT * P]) as srcT, Phase(nc) as ph:
            s_turn, s_copy, s_product, s_sum = ph.sem("turn"), ph.sem("copy"), ph.sem("product"), ph.sem("sum")
            with nc.Block() as block:
                @block.tensor
                def _(pe):
                    for t in range(NT):
                        pe.transpose(self.ps[:, t * P:(t + 1) * P], src[:, t, :], self.c["ident"]).then_inc(s_turn, 1)
                    for t in range(NT):
                        pe.wait_ge(s_copy, t // 4 + 1)
                        o = self.ps[:, (NT + t) * P:(NT + t + 1) * P]
                        last = pe.matmul(o, srcT[:, t * P:(t + 1) * P], W, start=True, stop=bias is None)
                        if bias is not None:
                            last = pe.matmul(o, self.c["ones_row"], bias, start=False, stop=True)
                        last.then_inc(s_product, 1)

                @block.scalar
                def _(act):
                    for g in range(NCH):
                        cols = slice(g * CH, (g + 1) * CH)
                        act.wait_ge(s_turn, 4 * (g + 1))
                        act.activation(srcT[:, cols], self.ps[:, cols], ACT.Copy,
                                       scale=1.0 if scale is None else scale).then_inc(s_copy, 1)

                @block.vector
                def _(dve):
                    for g in range(NCH):
                        dve.wait_ge(s_product, 4 * (g + 1))
                        dve.tensor_tensor(dst[:, 4 * g:4 * g + 4, :],
                                          self.bank(2 + g)[:, :].rearrange("p (t d) -> p t d", d=D),
                                          dst[:, 4 * g:4 * g + 4, :], ALU.add).then_inc(s_sum, 1)

    def rows_added(self, jobs, srcT, W, bias, dst, k=1):
        for g in range(NCH):
            mms = []
            for t in range(4 * g, 4 * g + 4):
                c = (t - 4 * g) * P
                for kk in range(k):
                    mms.append((c, c + P, P, srcT[:, kk, t * P:(t + 1) * P], W[:, kk * D:(kk + 1) * D],
                                kk == 0, bias is None and kk == k - 1))
                if bias is not None:
                    mms.append((c, c + P, P, self.c["ones_row"], bias, False, True))
            d = dst[:, 4 * g:4 * g + 4, :]
            jobs.append((mms, ("dve", "add", d, (lambda bank: bank[:, :].rearrange("p (t d) -> p t d", d=D)), d), None))

    def L0_attn(self):
        nc = self.nc
        self.norm(self.x, self.nrm, self.xT)
        EK = INNER // P
        with self.weights("L0_attn") as w, self.sb("v", [P, NT, INNER]) as v, self.sb("gateT", [P, EK, B * S]) as gateT, \
                self.sb("baseT", [P, B * S]) as baseT, self.sb("four", [P, 4, B * S]) as four, \
                self.sb("oT", [P, EK, B * S]) as oT:
            jobs = []
            for e in range(EK):
                jobs += self.turned(w["Wg"][:, e * P:(e + 1) * P], self.xT, gateT[:, e, :], bias=w["bg"][:, e:e + 1], func=ACT.Silu)
            jobs += self.turned(w["Win"], self.xT, baseT, bias=w["bin"], func=ACT.Silu)
            for g in range(0, NT, 2):
                mms = []
                for t in (g, g + 1):
                    c = (t - g) * INNER
                    mms.append((c, c + INNER, P, self.xT[:, t * P:(t + 1) * P], w["Wv"], True, False))
                    mms.append((c, c + INNER, P, self.c["ones_row"], w["bv"], False, True))
                jobs.append((mms, ("act", ACT.Silu, v[:, g:g + 2, :], self.whole(), 0.0, 1.0), None))
            self.products(jobs)
            QQ, QK, LQ, LK = range(4)
            with Phase(nc) as ph:
                s_aff = ph.sem("affine")
                with nc.Block() as block:
                    @block.vector
                    def _(dve):
                        for n, name in enumerate(("qq", "qk", "lq", "lk")):
                            dve.tensor_scalar(four[:, n, :], baseT[:, :], w["g_" + name], w["b_" + name],
                                              ALU.mult, ALU.add).then_inc(s_aff, 1)
            units = [(b, kb) for b in range(B) for kb in range(HALVES)]
            with self.sb("sq", [P, 2, S]) as sq, self.sb("mix", [P, 4, S]) as mix, Phase(nc) as ph:
                s_scores, s_relu, s_chain, s_mix = ph.sem("scores"), ph.sem("relu"), ph.sem("chain"), ph.sem("mix")
                s_out, s_gated = ph.sem("out"), ph.sem("gated")
                with nc.Block() as block:
                    @block.tensor
                    def _(pe):
                        def out(b):
                            pe.wait_ge(s_mix, 2 * b + 2)
                            if b >= 2:
                                pe.wait_ge(s_gated, b - 1)
                            for e in range(EK):
                                for kb in range(HALVES):
                                    last = pe.matmul(self.bank(4 + b % 2)[:, e * S:(e + 1) * S], v[:, 2 * b + kb, e * P:(e + 1) * P],
                                                     mix[:, (2 * b + kb) % 4, :], start=(kb == 0), stop=(kb == 1))
                            last.then_inc(s_out, 1)
                        for n, (b, kb) in enumerate(units):
                            if n >= 4:
                                pe.wait_ge(s_mix, n - 3)
                            ks = slice(b * S + kb * P, b * S + (kb + 1) * P)
                            qs = slice(b * S, (b + 1) * S)
                            pe.matmul(self.bank(n % 4)[:, 0:S], four[:, QK, ks], four[:, QQ, qs], start=True, stop=True)
                            pe.matmul(self.bank(n % 4)[:, S:2 * S], four[:, LK, ks], four[:, LQ, qs], start=True, stop=True).then_inc(s_scores, 1)
                            if n >= 3 and n % 2 == 1:
                                out(n // 2 - 1)
                        out(B - 1)

                    @block.scalar
                    def _(act):
                        for n in range(len(units)):
                            act.wait_ge(s_scores, n + 1)
                            if n >= 2:
                                act.wait_ge(s_mix, n - 1)
                            act.activation(sq[:, n % 2, :], self.bank(n % 4)[:, 0:S], ACT.Relu, scale=1.0 / INNER ** 0.5).then_inc(s_relu, 1)

                    @block.vector
                    def _(dve):
                        chain = [0]

                        def gate(b):
                            dve.wait_ge(s_out, b + 1)
                            dve.tensor_tensor(oT[:, :, b * S:(b + 1) * S], self.bank(4 + b % 2)[:, :].rearrange("p (e s) -> p e s", e=EK),
                                              gateT[:, :, b * S:(b + 1) * S], ALU.mult).then_inc(s_gated, 1)
                        for n, (b, kb) in enumerate(units):
                            dve.wait_ge(s_relu, n + 1)
                            if n >= 4:
                                dve.wait_ge(s_out, (n - 4) // 2 + 1)
                            m = slice(kb * S, (kb + 1) * S)
                            link(dve, s_chain, chain, dve.tensor_tensor(sq[:, n % 2, :], sq[:, n % 2, :], sq[:, n % 2, :], ALU.mult))
                            link(dve, s_chain, chain, dve.tensor_tensor(sq[:, n % 2, :], sq[:, n % 2, :], self.c["in_chunk"][:, m], ALU.mult))
                            link(dve, s_chain, chain, dve.tensor_tensor(mix[:, n % 4, :], self.bank(n % 4)[:, S:2 * S], self.c["older_chunk"][:, m], ALU.mult))
                            dve.tensor_tensor(mix[:, n % 4, :], mix[:, n % 4, :], sq[:, n % 2, :], ALU.add).then_inc(s_mix, 1)
                            if n >= 3 and n % 2 == 1:
                                gate(n // 2 - 1)
                        gate(B - 1)
            jobs = []
            self.rows_added(jobs, oT, w["Wout"], w["bout"], self.x, k=EK)
            self.products(jobs)

    def context_keys_values(self, jobs, Wk, Wv, KT, V9, bk=0.0, bv=None):
        jobs += self.turned(Wk, self.ctx["ctxT"], KT, bias=bk, width=B * SC)
        jobs += self.value_rows(Wv, self.ctx["ctxT2"], V9, bias=bv, n=B)

    def L0_xattn(self):
        nc = self.nc
        self.norm(self.x, self.nrm, self.xT)
        with self.weights("L0_xattn") as w, self.sb("QT", [P, B * S]) as QT, self.sb("KT", [P, B * SC]) as KT, \
                self.sb("Kx", [P, H, B * SC]) as Kx, self.sb("V9", [P, B, H, HD + 1]) as V9, self.sb("O", [P, NT, D]) as O:
            jobs = []
            for c in range(NCH):
                cols = slice(c * CH, (c + 1) * CH)
                jobs.append(([(0, CH, P, w["Wq"], self.xT[:, cols], True, True)],
                             ("dve", "affine", QT[:, cols], self.whole(), w["bq"], HD ** -0.5), None))
            self.context_keys_values(jobs, w["Wk"], w["Wv"], KT, V9, w["bk"], w["bv"])
            self.products(jobs)
            self.expand_context(KT, Kx)
            self.attend_context(self.head_scores(QT, Kx), V9, HD, O[:, :, :].rearrange("p t (h d) -> p t h d", d=HD), bias=self.keepb)
            self.project(O, w["Wo"], w["bo"], self.x)

    def quantise(self, tensors):
        nc = self.nc
        n_max = max(a.shape[1] for a in tensors)
        with self.sb("sc", [P, n_max]) as sc, self.sb("inv", [P, n_max]) as inv, self.sb("mag", [P, n_max, 16]) as mag, \
                self.sb("acc", [P, n_max, 16]) as acc, self.sb("sgn", [P, n_max, 16]) as sgn, Phase(nc) as ph:
            s_chain, s_scale, s_sign, s_done = ph.sem("chain"), ph.sem("scale"), ph.sem("sign"), ph.sem("done")
            with nc.Block() as block:
                @block.scalar
                def _(act):
                    for k, a in enumerate(tensors):
                        r, n = a.shape[0], a.shape[1]
                        if k:
                            act.wait_ge(s_done, k)
                        act.activation(sgn[0:r, 0:n, :], a, ACT.Sign).then_inc(s_sign, 1)

                @block.vector
                def _(dve):
                    chain = [0]
                    for k, a in enumerate(tensors):
                        r, n = a.shape[0], a.shape[1]
                        wide = lambda v: v[0:r, 0:n].unsqueeze(2).to_broadcast([r, n, 16])
                        m, q = mag[0:r, 0:n, :], acc[0:r, 0:n, :]
                        link(dve, s_chain, chain, dve.tensor_reduce(sc[0:r, 0:n], a, AX.X, ALU.max, apply_absolute_value=True))
                        link(dve, s_chain, chain, dve.tensor_scalar(sc[0:r, 0:n], sc[0:r, 0:n], 1.0 / 6.0, 1e-12, ALU.mult, ALU.max))
                        link(dve, s_chain, chain, dve.reciprocal(inv[0:r, 0:n], sc[0:r, 0:n]))
                        link(dve, s_chain, chain, dve.tensor_tensor(m, a, wide(inv), ALU.mult))
                        dve.wait_ge(s_sign, k + 1)
                        link(dve, s_chain, chain, dve.tensor_tensor(m, m, sgn[0:r, 0:n, :], ALU.mult))
                        link(dve, s_chain, chain, dve.tensor_scalar(q, m, MIDS[6], 2.0, ALU.is_gt, ALU.mult))
                        for mid in (MIDS[5], MIDS[4]):
                            link(dve, s_chain, chain, dve.scalar_tensor_tensor(q, m, mid, q, ALU.is_gt, ALU.add))
                        link(dve, s_chain, chain, dve.tensor_scalar(q, q, 2.0, None, ALU.mult))
                        for mid in MIDS[3::-1]:
                            link(dve, s_chain, chain, dve.scalar_tensor_tensor(q, m, mid, q, ALU.is_gt, ALU.add))
                        link(dve, s_chain, chain, dve.scalar_tensor_tensor(q, q, 0.5, sgn[0:r, 0:n, :], ALU.mult, ALU.mult))
                        dve.tensor_tensor(a, q, wide(sc), ALU.mult).then_inc(s_done, 1)
                        dve.wait_ge(s_done, k + 1)

    def turn_tiles(self, moves):
        nc = self.nc
        with Phase(nc) as ph:
            s_turn, s_copy = ph.sem("turn"), ph.sem("copy")
            with nc.Block() as block:
                @block.tensor
                def _(pe):
                    for n, (src, dst) in enumerate(moves):
                        r, c = src.shape[0], src.shape[1]
                        if n >= 8:
                            pe.wait_ge(s_copy, n - 7)
                        pe.transpose(self.bank(n % 8)[0:c, 0:r], src, self.c["ident"][0:r, 0:r]).then_inc(s_turn, 1)

                @block.scalar
                def _(act):
                    for n, (src, dst) in enumerate(moves):
                        r, c = src.shape[0], src.shape[1]
                        act.wait_ge(s_turn, n + 1)
                        act.activation(dst, self.bank(n % 8)[0:c, 0:r], ACT.Copy).then_inc(s_copy, 1)

    def L0_ffn(self):
        blocks = lambda a: a.rearrange("p (n s) -> p n s", s=16)
        self.norm(self.x, self.nrm, None)
        NK = len(FT0)
        with self.weights("L0_ffn") as w, self.sb("wgT", [P, NF0]) as wgT, self.sb("wuT", [P, NF0]) as wuT, \
                self.sb("wdT", [P, NK, D]) as wdT, self.sb("g", [P, NK, B * S]) as gT, self.sb("h", [P, NT, NF0]) as h:
            self.quantise([self.nrm[:, :, :].rearrange("p t (n s) -> p (t n) s", s=16)]
                          + [blocks(w[f"{n}{i}"]) for n in ("w_gate", "w_up") for i in range(NK)] + [blocks(w["w_down"])])
            moves = [(self.nrm[:, t, :], self.xT[:, t * P:(t + 1) * P]) for t in range(NT)]
            for n, dst in (("w_gate", wgT), ("w_up", wuT)):
                moves += [(w[f"{n}{i}"], dst[:, f0:f0 + fn]) for i, (f0, fn) in enumerate(FT0)]
            moves += [(w["w_down"][:, f0:f0 + fn], wdT[0:fn, i, :]) for i, (f0, fn) in enumerate(FT0)]
            self.turn_tiles(moves)
            with self.sb("act", [P, NT, NF0]) as sil:
                jobs = []
                for t in range(NT):
                    xs = self.xT[:, t * P:(t + 1) * P]
                    jobs.append(([(0, NF0, P, xs, wgT[:, :], True, True)],
                                 ("act", ACT.Silu, sil[:, t, :], self.whole(P, NF0), 0.0, 1.0), None))
                    jobs.append(([(0, NF0, P, xs, wuT[:, :], True, True)],
                                 ("dve", "mult", h[:, t, :], self.whole(P, NF0), sil[:, t, :], len(jobs) - 1), None))
                self.products(jobs)
            self.quantise([h[:, 4 * g:4 * g + 4, :].rearrange("p t (n s) -> p (t n) s", s=16) for g in range(2)])
            self.turn_tiles([(h[:, t, f0:f0 + fn], gT[0:fn, i, t * P:(t + 1) * P]) for t in range(NT) for i, (f0, fn) in enumerate(FT0)])
            jobs = []
            for g in range(NCH):
                mms = []
                for t in range(4 * g, 4 * g + 4):
                    c = (t - 4 * g) * P
                    for i, (f0, fn) in enumerate(FT0):
                        mms.append((c, c + P, P, gT[0:fn, i, t * P:(t + 1) * P], wdT[0:fn, i, :], i == 0, i == NK - 1))
                d = self.x[:, 4 * g:4 * g + 4, :]
                jobs.append((mms, ("dve", "add", d, (lambda bank: bank[:, :].rearrange("p (t d) -> p t d", d=D)), d), None))
            self.products(jobs)

    def attend_turned(self, Ks, Qx, V, O, clip=None, decay=None, scale=1.0):
        nc = self.nc
        units = [(b, i, kb) for b in range(B) for i in range(ROWG) for kb in range(HALVES)]
        N = len(units)
        first = lambda kb: kb if clip else 0
        HS = Qx.shape[2]

        def by_head(a):
            return a.rearrange("p (q j c) -> p j q c", q=2, c=P) if HS == 4 else a.rearrange("p (j q c) -> p j q c", q=2, c=P)

        with self.sb("clipped", [P, 2, 2 * CH]) if clip else nullcontext() as cl, self.sb("probsK", [P, 4, 2 * CH]) as pr, \
                self.sb("rsumK", [P, HALVES, H]) as rsum, self.sb("outT", [P, ROWG, S]) as oT, Phase(nc) as ph:
            s_scores, s_clip, s_exp, s_mask = ph.sem("scores"), ph.sem("clip"), ph.sem("exp"), ph.sem("mask")
            s_out, s_ot, s_back, s_rec, s_norm = ph.sem("out"), ph.sem("out_copied"), ph.sem("back"), ph.sem("rec"), ph.sem("norm")
            s_ready = s_mask if clip else s_clip

            def sbank(n):
                return self.bank(2 * (n % 2), 2)

            obanks, rbanks = self.bank(4, 2), self.bank(6, 2)

            with nc.Block() as block:
                if clip:
                    @block.gpsimd
                    def _(pool):
                        for n, (b, i, kb) in enumerate(units):
                            pool.wait_ge(s_exp, n + 1)
                            d = by_head(pr[:, n % 4, :])[:, :, kb, :]
                            pool.tensor_tensor(d, d, self.c["causal_one"].unsqueeze(1).to_broadcast([P, 4, P]), ALU.mult).then_inc(s_mask, 1)

                @block.tensor
                def _(pe):
                    def scores(n):
                        b, i, kb = units[n]
                        if n >= 2:
                            pe.wait_ge(s_clip, n - 1)
                        ks = slice(b * S + kb * P, b * S + (kb + 1) * P)
                        if HS == 4:
                            for q in range(first(kb), HALVES):
                                last = pe.matmul(sbank(n)[:, q * CH:(q + 1) * CH], Ks[:, i, ks],
                                                 Qx[:, i, :, b * S + q * P:b * S + (q + 1) * P], start=True, stop=True)
                        else:
                            for g in range(2):
                                q0 = first(kb) * P
                                o = sbank(n)[:, g * CH:(g + 1) * CH].rearrange("p (j s) -> p j s", j=2)[:, :, q0:S]
                                last = pe.matmul(o, Ks[:, 2 * i + g, ks], Qx[:, 2 * i + g, :, b * S + q0:(b + 1) * S], start=True, stop=True)
                        last.then_inc(s_scores, 1)

                    def out(n):
                        b, i, _ = units[n]
                        if i == 0 and b >= 1:
                            pe.wait_ge(s_ot, b)
                        pe.wait_ge(s_ready, n + 2)
                        for q in range(HALVES):
                            kbs = [kb for kb in range(HALVES) if first(kb) <= q]
                            for kb in kbs:
                                for j in range(4):
                                    last = pe.matmul(obanks[32 * j:32 * j + 32, i * S + q * P:i * S + (q + 1) * P], V[:, 2 * b + kb, 4 * i + j, :],
                                                     by_head(pr[:, (n + kb) % 4, :])[:, j, q, :], start=(kb == kbs[0]), stop=(kb == kbs[-1]))
                        last.then_inc(s_out, 1)

                    def back(b):
                        pe.wait_ge(s_ot, b + 1)
                        if b >= 1:
                            pe.wait_ge(s_norm, b)
                        for q in range(HALVES):
                            for i in range(ROWG):
                                last = pe.transpose(rbanks[:, q * CH + i * P:q * CH + (i + 1) * P], oT[:, i, q * P:(q + 1) * P], self.c["ident"])
                        last.then_inc(s_back, 1)

                    for n in range(N + 3):
                        if n < N:
                            scores(n)
                        if n >= 3 and n % 2 == 1 and n - 3 < N:
                            out(n - 3)
                        if n % 8 == 2 and n > 8:
                            back(n // 8 - 1)

                @block.scalar
                def _(act):
                    for n in range(N + 2):
                        if n < N and clip:
                            b, i, kb = units[n]
                            act.wait_ge(s_clip, n + 1)
                            if n >= 4:
                                act.wait_ge(s_out, (n - 4) // 2 + 1)
                            f = first(kb)
                            act.activation(by_head(pr[:, n % 4, :])[:, :, f:HALVES, :], by_head(cl[:, n % 2, :])[:, :, f:HALVES, :], ACT.Exp, scale=scale).then_inc(s_exp, 1)
                        if n % 8 == 1 and n > 8:
                            b = n // 8 - 1
                            act.wait_ge(s_out, ROWG * (b + 1))
                            if b >= 1:
                                act.wait_ge(s_back, b)
                            act.activation(oT[:, :, :], obanks, ACT.Copy).then_inc(s_ot, 1)

                @block.vector
                def _(dve):
                    def take(b):
                        dve.wait_ge(s_back, b + 1)
                        dst = O[:, 2 * b:2 * b + 2, :].rearrange("p q (h d) -> p (q h) d", d=HD)
                        rows = rbanks.rearrange("p (h d) -> p h d", d=VW)
                        if clip:
                            dve.reciprocal(rsum[:, :, :], rows[:, :, HD]).then_inc(s_rec, 1)
                            dve.wait_ge(s_rec, b + 1)
                            last = dve.tensor_tensor(dst, rows[:, :, 0:HD], rsum[:, :, :].rearrange("p q h -> p (q h)").unsqueeze(2).to_broadcast([P, 2 * H, HD]), ALU.mult)
                        else:
                            last = dve.tensor_scalar(dst, rows[:, :, 0:HD], scale, None, ALU.mult)
                        last.then_inc(s_norm, 1)
                    for n in range(N + 3):
                        if n < N:
                            b, i, kb = units[n]
                            dve.wait_ge(s_scores, n + 1)
                            f = first(kb)
                            s = by_head(sbank(n))
                            if clip:
                                if n >= 2:
                                    dve.wait_ge(s_exp, n - 1)
                                dve.tensor_scalar(by_head(cl[:, n % 2, :])[:, :, f:HALVES, :], s[:, :, f:HALVES, :], -clip, clip, ALU.max, ALU.min).then_inc(s_clip, 1)
                            else:
                                if n >= 4:
                                    dve.wait_ge(s_out, (n - 4) // 2 + 1)
                                dve.tensor_tensor(by_head(pr[:, n % 4, :]), s, decay[:, 4 * i:4 * i + 4, kb, :].rearrange("p j (q c) -> p j q c", c=P),
                                                  ALU.mult).then_inc(s_clip, 1)
                        if n % 8 == 2 and n > 8:
                            take(n // 8 - 1)

    def L1_attn(self):
        self.norm(self.x, self.nrm, self.xT)
        c = self.c
        with self.weights("L1_attn") as w, self.sb("Qx", [LR, 2 * ROWG, 2, B * S], F32R) as Qx, \
                self.sb("Ks", [LR, 2 * ROWG, B * S], F32R) as Ks, self.sb("V32", [P, NT, H, VW]) as V, self.sb("O", [P, NT, D]) as O:
            with self.sb("QT", [LR, LT, B * S]) as QT, self.sb("KT", [LR, LT, B * S]) as KT:
                with self.sb("cq", [32, B * S]) as cq, self.sb("ckv", [32, B * S]) as ckv, self.sb("raw", [LR, 2, B * S]) as raw:
                    self.products(self.turned(w["W_DQ"], self.xT, cq, m=32) + self.turned(w["W_DKV"], self.xT, ckv, m=32))
                    for t in range(LT):
                        ws = slice(t * LR, (t + 1) * LR)
                        jobs = self.value_rows(w["W_UV"], ckv, V, k=32) if t == 0 else []
                        self.roped(jobs, [(w["W_Q"][:, ws], cq)], QT[:, t, :], raw[:, 0, :], c["rot_inter"], c["cos12"], c["sin12"], m=LR)
                        self.roped(jobs, [(w["W_KC"][:, ws], ckv), (w["W_KR"][:, ws], self.xT)], KT[:, t, :], raw[:, 1, :],
                                   c["rot_inter"], c["cos12"], c["sin12"], m=LR)
                        self.products(jobs)
                self.stack_operands((KT, Ks), (QT, Qx), c["mask12"], V, m=LR, heads=2)
            self.attend_turned(Ks, Qx, V, O, clip=80.0, scale=1.0 / math.sqrt(12.0))
            self.project(O, w["W_O"], None, self.x)

    def self_attention(self, src, w, dst, rot, weight=None, rms=False, norm=True, biases=False, names=("Wq", "Wk", "Wv", "Wo")):
        c = self.c
        if norm:
            self.norm(src, self.nrm, self.xT, layer=not rms, eps=1e-6 if rms else 1e-5, weight=weight)
        with self.sb("Qs", [P, ROWG, B * S], F32R) as Qs, self.sb("Kx", [P, ROWG, 4, B * S], F32R) as Kx, \
                self.sb("V32", [P, NT, H, VW]) as V, self.sb("O", [P, NT, D]) as O:
            with self.sb("QT", [P, B * S]) as QT, self.sb("KT", [P, B * S]) as KT, self.sb("raw", [P, 2, B * S]) as raw:
                jobs = []
                bq, bk, bv, bo = (w["bq"], w["bk"], w["bv"], w["bo"]) if biases else (0.0, 0.0, None, None)
                self.roped(jobs, [(w[names[0]], self.xT)], QT, raw[:, 0, :], rot, c["cos8q"], c["sin8q"], bias=bq)
                self.roped(jobs, [(w[names[1]], self.xT)], KT, raw[:, 1, :], rot, c["cos8"], c["sin8"], bias=bk)
                jobs += self.value_rows(w[names[2]], self.xT, V, bias=bv)
                self.products(jobs)
                one = lambda a: a.unsqueeze(1)
                self.stack_operands((one(QT[:, :]), Qs), (one(KT[:, :]), Kx), c["mask8"], V)
            self.attend(Qs, Kx, V, O)
            self.project(O, w[names[3]], bo, dst)

    def L1_xattn(self):
        nc = self.nc
        awhere, awidth = self.where["inner_attn"]
        fwhere, fwidth = self.where["inner_ffn"]
        with self.sb("y", [P, NT, D]) as y, self.sb("w_attn", [P, awidth]) as wa, self.sb("w_ffn", [P, fwidth]) as wf, \
                self.weights("inner_misc") as wm, self.sb("allow", [P, NT, SC], BF16) as allow, self.sb("seg", [P, NT], I32) as seg:
            self.norm(self.x, y, None)
            with self.sb("segf", [P, NT]) as segf, self.sb("one", [P, NT, SC]) as one, self.sb("low", [P, NT]) as low, \
                    self.sb("two", [P, NT, SC]) as two, Phase(nc) as ph:
                s_load, s_chain = ph.sem("load"), ph.sem("chain")
                with nc.Block() as block:
                    @block.sync
                    def _(sp):
                        sp.dma_start(seg[:, :], self.seg_dram[:, :]).then_inc(s_load, 16)
                        sp.dma_start(wa[:, :], self.dram["inner_attn"][0, :, :]).then_inc(s_load, 16)
                        sp.wait_ge(s_load, 32)

                    @block.vector
                    def _(dve):
                        n = [0]
                        keys = self.c["keys"].unsqueeze(1).to_broadcast([P, NT, SC])
                        wide = lambda v: v[:, :].unsqueeze(2).to_broadcast([P, NT, SC])
                        dve.wait_ge(s_load, 32)
                        link(dve, s_chain, n, dve.tensor_copy(segf[:, :], seg[:, :]))
                        link(dve, s_chain, n, dve.tensor_scalar(low[:, :], segf[:, :], -128.0, None, ALU.add))
                        link(dve, s_chain, n, dve.tensor_tensor(one[:, :, :], keys, wide(segf), ALU.is_le))
                        link(dve, s_chain, n, dve.tensor_tensor(two[:, :, :], keys, wide(low), ALU.is_gt))
                        link(dve, s_chain, n, dve.tensor_tensor(one[:, :, :], one[:, :, :], two[:, :, :], ALU.mult))
                        link(dve, s_chain, n, dve.tensor_scalar(allow[:, :, :], one[:, :, :], -1.0, -NEG, ALU.add, ALU.mult))
            w, wff = Pack(wa, awhere), Pack(wf, fwhere)
            with nc.Fori(0, LAYERS) as layer:
                with Phase(nc) as ph:
                    s_f = ph.sem("ffn_weights")
                    with nc.Block() as block:
                        @block.sync
                        def _(sp):
                            sp.dma_start(wf[:, :], self.dram["inner_ffn"][bass.ds(layer, 1), :, :].rearrange("o p n -> (o p) n")).then_inc(s_f, 16)
                            sp.wait_ge(s_f, 16)
                self.self_attention(y, w, y, self.c["rot_half"], weight=w["n1"], rms=True, biases=True)
                self.norm(y, self.nrm, self.xT, layer=False, eps=1e-6, weight=w["n2"])
                with self.sb("QT", [P, B * S]) as QT, self.sb("KT", [P, B * SC]) as KT, \
                        self.sb("Kx", [P, H, B * SC]) as Kx, self.sb("V9", [P, B, H, HD + 1]) as V9, self.sb("O", [P, NT, D]) as O:
                    jobs = self.turned(w["Wq_c"], self.xT, QT, scale=HD ** -0.5)
                    self.context_keys_values(jobs, w["Wk_c"], w["Wv_c"], KT, V9)
                    self.products(jobs)
                    self.expand_context(KT, Kx)
                    self.attend_context(self.head_scores(QT, Kx), V9, HD, O[:, :, :].rearrange("p t (h d) -> p t h d", d=HD),
                                        bias=allow, per_token=True)
                    self.project(O, w["Wo_c"], None, y)
                with Phase(nc) as ph:
                    s_a = ph.sem("attn_weights")
                    with nc.Block() as block:
                        @block.sync
                        def _(sp):
                            sp.dma_start(wa[:, :], self.dram["inner_attn"][bass.ds(layer + 1, 1), :, :].rearrange("o p n -> (o p) n")).then_inc(s_a, 16)
                            sp.wait_ge(s_a, 16)
                self.norm(y, self.nrm, self.xT, layer=False, eps=1e-6, weight=wff["n3"])
                with self.sb("sil", [P, 2, CH]) as sil, self.sb("hT", [P, FK, B * S]) as hT:
                    jobs = []
                    for n, (f, ch) in enumerate((f, ch) for f in range(FK) for ch in range(NCH)):
                        cols = slice(ch * CH, (ch + 1) * CH)
                        fs = slice(f * P, (f + 1) * P)
                        jobs.append(([(0, CH, P, wff["Wg"][:, fs], self.xT[:, cols], True, True)],
                                     ("act", ACT.Silu, hT[:, f, cols], self.whole(), 0.0, 1.0), None))
                        jobs.append(([(0, CH, P, wff["Wu"][:, fs], self.xT[:, cols], True, True)],
                                     ("dve", "mult", hT[:, f, cols], self.whole(), hT[:, f, cols], len(jobs) - 1), None))
                    self.products(jobs)
                    jobs = []
                    self.rows_added(jobs, hT, wff["Wd"], None, y, k=FK)
                    self.products(jobs)
            self.norm(y, self.nrm, None, layer=False, eps=1e-6)
            with Phase(nc) as ph:
                s_chain = ph.sem("chain")
                with nc.Block() as block:
                    @block.vector
                    def _(dve):
                        n = [0]
                        nf = wm["nf"].unsqueeze(1).to_broadcast([P, NT, D])
                        link(dve, s_chain, n, dve.tensor_tensor(self.nrm[:, :, :], self.nrm[:, :, :], nf, ALU.mult))
                        link(dve, s_chain, n, dve.tensor_tensor(self.x[:, :, :], self.x[:, :, :], self.nrm[:, :, :], ALU.add))

    def route(self, w, top, gate, bias=True):
        nc = self.nc
        eps = {"L1": float(np.finfo(np.float32).eps)}
        with self.sb("logits", [P, NT, E]) as lg, self.sb("best", [P, NT, 8]) as best, self.sb("which", [P, NT, 8], U32) as which, \
                self.sb("whichf", [P, NT, 8]) as wh, self.sb("ex", [P, NT, E]) as ex, self.sb("hot", [P, NT, E]) as hot, \
                self.sb("hot2", [P, NT, E]) as hot2, self.sb("total", [P, NT]) as total, self.sb("z", [P, NT]) as z, Phase(nc) as ph:
            s_logits, s_chain, s_sub, s_exp = ph.sem("logits"), ph.sem("chain"), ph.sem("sub"), ph.sem("exp")
            with nc.Block() as block:
                @block.tensor
                def _(pe):
                    for t in range(NT):
                        o = self.ps[:, t * E:(t + 1) * E]
                        last = pe.matmul(o, self.xT[:, t * P:(t + 1) * P], w["Wr"], start=True, stop=not bias)
                        if bias:
                            last = pe.matmul(o, self.c["ones_row"], w["br"], start=False, stop=True)
                    last.then_inc(s_logits, 1)

                @block.scalar
                def _(act):
                    act.wait_ge(s_sub, 1)
                    act.activation(ex[:, :, :], ex[:, :, :], ACT.Exp).then_inc(s_exp, 1)

                @block.vector
                def _(dve):
                    n = [0]
                    wide = lambda v: v.to_broadcast([P, NT, E])
                    iota = self.c["iota8"].unsqueeze(1).to_broadcast([P, NT, E])
                    dve.wait_ge(s_logits, 1)
                    link(dve, s_chain, n, dve.tensor_copy(lg[:, :, :], self.ps[:, 0:NT * E]))
                    for t in range(NT):
                        link(dve, s_chain, n, dve.max(best[:, t, :], lg[:, t, :]))
                    dve.tensor_tensor(ex[:, :, :], lg[:, :, :], wide(best[:, :, 0:1]), ALU.subtract).then_inc(s_sub, 1)
                    for t in range(NT):
                        link(dve, s_chain, n, dve.max_index(which[:, t, :], best[:, t, :], lg[:, t, :]))
                    link(dve, s_chain, n, dve.tensor_copy(wh[:, :, :], which[:, :, :]))
                    link(dve, s_chain, n, dve.tensor_tensor(hot[:, :, :], iota, wide(wh[:, :, 0:1]), ALU.is_equal))
                    if top == 2:
                        link(dve, s_chain, n, dve.tensor_tensor(hot2[:, :, :], iota, wide(wh[:, :, 1:2]), ALU.is_equal))
                        link(dve, s_chain, n, dve.tensor_tensor(hot[:, :, :], hot[:, :, :], hot2[:, :, :], ALU.add))
                    dve.wait_ge(s_exp, 1)
                    link(dve, s_chain, n, dve.tensor_reduce(total[:, :], ex[:, :, :], AX.X, ALU.add))
                    link(dve, s_chain, n, dve.reciprocal(z[:, :], total[:, :]))
                    link(dve, s_chain, n, dve.tensor_tensor(ex[:, :, :], ex[:, :, :], wide(z[:, :].unsqueeze(2)), ALU.mult))
                    link(dve, s_chain, n, dve.tensor_tensor(gate[:, :, :], ex[:, :, :], hot[:, :, :], ALU.mult))
                    if top == 2:
                        link(dve, s_chain, n, dve.tensor_reduce(total[:, :], gate[:, :, :], AX.X, ALU.add))
                        if not bias:
                            link(dve, s_chain, n, dve.tensor_scalar(total[:, :], total[:, :], eps["L1"], None, ALU.add))
                        link(dve, s_chain, n, dve.reciprocal(z[:, :], total[:, :]))
                        link(dve, s_chain, n, dve.tensor_tensor(gate[:, :, :], gate[:, :, :], wide(z[:, :].unsqueeze(2)), ALU.mult))

    def experts(self, stage, gate, gated):
        nc = self.nc
        where, width = self.where[stage]
        U = FK * NCH
        with self.sb("slot0", [P, width]) as w0, self.sb("slot1", [P, width]) as w1, \
                self.sb("hidden", [P, 2, FK, B * S]) as hid:
            with Phase(nc) as ph:
                s_w = ph.sem("first_weights")
                with nc.Block() as block:
                    @block.sync
                    def _(sp):
                        sp.dma_start(w0[:, :], self.dram[stage][0, :, :]).then_inc(s_w, 16)
                        sp.wait_ge(s_w, 16)
            packs = (Pack(w0, where), Pack(w1, where))
            with nc.Fori(0, E // 2) as pair, Phase(nc) as ph:
                expert = pair * 2
                s_slot1, s_slot0 = ph.sem("slot1_loaded"), ph.sem("slot0_loaded")
                s_up, s_act, s_hid = ph.sem("up"), ph.sem("act"), ph.sem("hidden")
                s_down, s_added, s_zero = ph.sem("down"), ph.sem("added"), ph.sem("zero")
                R = 6
                per = 2 if gated else 1
                s_full = s_hid if gated else s_act
                with nc.Block() as block:
                    @block.sync
                    def _(sp):
                        sp.dma_start(w1[:, :], self.dram[stage][bass.ds(expert + 1, 1), :, :].rearrange("o p n -> (o p) n")).then_inc(s_slot1, 16)
                        sp.wait_ge(s_down, NCH)
                        sp.dma_start(w0[:, :], self.dram[stage][bass.ds(expert + 2, 1), :, :].rearrange("o p n -> (o p) n")).then_inc(s_slot0, 16)
                        sp.wait_ge(s_slot0, 16)
                        sp.wait_ge(s_slot1, 16)

                    @block.tensor
                    def _(pe):
                        def up(x):
                            if x == 1:
                                pe.wait_ge(s_slot1, 16)
                            w = packs[x]
                            for u in range(U):
                                f, ch = u // NCH, u % NCH
                                for m, name in enumerate(("Wg", "Wu") if gated else ("W1",)):
                                    k = (x * U + u) * per + m
                                    if k >= R:
                                        old = (k - R) // per
                                        pe.wait_ge(s_full, old + 1)
                                    pe.matmul(self.bank(k % R), w[name][:, f * P:(f + 1) * P],
                                              self.xT[:, ch * CH:(ch + 1) * CH], start=True, stop=True).then_inc(s_up, 1)

                        def down(x):
                            w = packs[x]
                            pe.wait_ge(s_full, (x + 1) * U)
                            for g in range(NCH):
                                n = x * NCH + g
                                if n >= 2:
                                    pe.wait_ge(s_added, 4 * (n - 1))
                                for t in range(4 * g, 4 * g + 4):
                                    c = (t - 4 * g) * P
                                    for f in range(FK):
                                        last = pe.matmul(self.bank(R + n % 2)[:, c:c + P], hid[:, x, f, t * P:(t + 1) * P],
                                                         w["Wd" if gated else "W2"][:, f * D:(f + 1) * D], start=(f == 0), stop=(f == FK - 1))
                                last.then_inc(s_down, 1)
                        up(0)
                        down(0)
                        up(1)
                        down(1)

                    @block.scalar
                    def _(act):
                        for x in range(2):
                            for u in range(U):
                                f, ch = u // NCH, u % NCH
                                n = x * U + u
                                act.wait_ge(s_up, n * per + 1)
                                d = hid[:, x, f, ch * CH:(ch + 1) * CH]
                                if x == 1 and u == 0:
                                    act.wait_ge(s_slot1, 16)
                                if gated:
                                    act.activation(d, self.bank((n * per) % R), ACT.Relu).then_inc(s_act, 1)
                                else:
                                    act.activation(d, self.bank(n % R), ACT.Gelu, bias=packs[x]["b1"][:, f:f + 1]).then_inc(s_act, 1)

                    @block.vector
                    def _(dve):
                        def hidden(x, u):
                            f, ch = u // NCH, u % NCH
                            n = x * U + u
                            dve.wait_ge(s_up, 2 * n + 2)
                            dve.wait_ge(s_act, n + 1)
                            d = hid[:, x, f, ch * CH:(ch + 1) * CH]
                            dve.tensor_tensor(d, self.bank((2 * n + 1) % R), d, ALU.mult).then_inc(s_hid, 1)

                        def add(x, g):
                            n = x * NCH + g
                            dve.wait_ge(s_down, n + 1)
                            if x == 1:
                                dve.wait_ge(s_added, 4 * (g + 1))
                            for t in range(4 * g, 4 * g + 4):
                                c = (t - 4 * g) * P
                                dve.scalar_tensor_tensor(self.x[:, t, :], self.bank(R + n % 2)[:, c:c + P],
                                                         gate[:, t, bass.ds(expert + x, 1)], self.x[:, t, :],
                                                         ALU.mult, ALU.add).then_inc(s_added, 1)
                        for x in range(2):
                            if gated:
                                for u in range(U):
                                    hidden(x, u)
                            for g in range(NCH):
                                add(x, g)

    def add_gated_bias(self, gate, b2):
        nc = self.nc
        with self.sb("gateT", [E, B * S]) as gT:
            self.turn_tiles([(gate[:, t, :], gT[:, t * P:(t + 1) * P]) for t in range(NT)])
            jobs = []
            for g in range(NCH):
                mms = [((t - 4 * g) * P, (t - 4 * g + 1) * P, P, gT[:, t * P:(t + 1) * P], b2, True, True) for t in range(4 * g, 4 * g + 4)]
                d = self.x[:, 4 * g:4 * g + 4, :]
                jobs.append((mms, ("dve", "add", d, (lambda bank: bank[:, :].rearrange("p (t d) -> p t d", d=D)), d), None))
            self.products(jobs)

    def moe(self, layer, top):
        self.norm(self.x, self.nrm, self.xT)
        gated = layer == "L1"
        with self.weights(layer + "_ffn") as w, self.sb("gate", [P, NT, E]) as gate:
            self.route(w, top, gate, bias=not gated)
            if not gated:
                self.add_gated_bias(gate, w["b2"])
            self.experts(layer + "_experts", gate, gated)

    def L1_ffn(self):
        self.moe("L1", 2)

    def L2_ffn(self):
        self.moe("L2", 1)

    def L3_ffn(self):
        self.moe("L3", 2)

    def L2_attn(self):
        with self.weights("L2_attn") as w:
            self.self_attention(self.x, w, self.x, self.c["rot_inter"])

    def L2_xattn(self):
        nc = self.nc
        self.norm(self.x, self.nrm, self.xT)
        with self.weights("L2_xattn") as w, self.sb("QT", [P, 2, B * S]) as QT, self.sb("KT", [P, 2, B * SC]) as KT, \
                self.sb("Kx", [P, 2, H, B * SC]) as Kx, self.sb("V9", [P, B, H, HD + 1]) as V9, \
                self.sb("O", [P, NT, D]) as O, self.sb("lam", [P, H]) as lam:
            jobs = self.turned(w["q1"], self.xT, QT[:, 0, :], scale=HD ** -0.5) + self.turned(w["q2"], self.xT, QT[:, 1, :], scale=HD ** -0.5)
            self.context_keys_values(jobs, w["k1"], w["v1"], KT[:, 0, :], V9)
            jobs += self.turned(w["k2"], self.ctx["ctxT"], KT[:, 1, :], width=B * SC)
            self.products(jobs)
            with Phase(nc) as ph:
                s_chain = ph.sem("chain")
                with nc.Block() as block:
                    @block.vector
                    def _(dve):
                        n = [0]
                        link(dve, s_chain, n, dve.tensor_tensor(lam[:, :], w["l1"], w["l2"], ALU.subtract))
                        link(dve, s_chain, n, dve.tensor_scalar(lam[:, :], lam[:, :], 0.1, None, ALU.add))
            for m in range(2):
                self.expand_context(KT[:, m, :], Kx[:, m, :, :])
            heads = O[:, :, :].rearrange("p t (h d) -> p t h d", d=HD)
            self.attend_context(self.head_scores(QT[:, 0, :], Kx[:, 0, :, :]), V9, HD, heads)
            self.attend_context(self.head_scores(QT[:, 1, :], Kx[:, 1, :, :]), V9, HD, heads, combine=lam[:, :])
            self.norm(O, self.nrm, None, layer=False, eps=1e-6)
            self.project(self.nrm, w["proj"], w["b"], self.x, scale=w["norm"])

    def L3_attn(self):
        nc = self.nc
        c = self.c
        self.norm(self.x, self.nrm, self.xT)
        with self.weights("L3_attn") as w, self.sb("Qx", [P, ROWG, 4, B * S], F32R) as Qx, self.sb("Ks", [P, ROWG, B * S], F32R) as Ks, \
                self.sb("V32", [P, NT, H, VW]) as V, self.sb("O", [P, NT, D]) as O, self.sb("gate", [P, NT, D]) as gate, \
                self.sb("sg", [P, H]) as sg:
          with self.sb("QT", [P, 1, B * S]) as QT, self.sb("KT", [P, 1, B * S]) as KT, self.sb("raw", [P, 2, B * S]) as raw:
            jobs = []
            self.roped(jobs, [(w["Wq"], self.xT)], QT[:, 0, :], raw[:, 0, :], c["rot_inter"], c["cos8"], c["sin8"], bias=w["bq"])
            self.roped(jobs, [(w["Wk"], self.xT)], KT[:, 0, :], raw[:, 1, :], c["rot_inter"], c["cos8"], c["sin8"], bias=w["bk"])
            jobs += self.value_rows(w["Wv"], self.xT, V, bias=w["bv"])
            for g in range(NCH):
                mms = []
                for t in range(4 * g, 4 * g + 4):
                    k = (t - 4 * g) * P
                    mms.append((k, k + P, P, self.xT[:, t * P:(t + 1) * P], w["Wg"], True, False))
                    mms.append((k, k + P, P, c["ones_row"], w["bg"], False, True))
                jobs.append((mms, ("act", ACT.Silu, gate[:, 4 * g:4 * g + 4, :], self.whole(), 0.0, 1.0), None))
            self.products(jobs)
            self.stack_operands((KT, Ks), (QT, Qx), c["mask8"], V)
          with self.sb("decay", [P, H, HALVES, S]) as decay:
            with Phase(nc) as ph:
                s_sig, s_neg, s_decay = ph.sem("sigmoid"), ph.sem("negated"), ph.sem("decay")
                with nc.Block() as block:
                    @block.scalar
                    def _(act):
                        act.activation(sg[:, :], w["gamma"], ACT.Sigmoid).then_inc(s_sig, 1)
                        act.wait_ge(s_neg, 1)
                        for h in range(H):
                            act.activation(decay[:, h, :, :], c["distance"], ACT.Exp, scale=sg[:, h:h + 1]).then_inc(s_decay, 1)

                    @block.vector
                    def _(dve):
                        dve.wait_ge(s_sig, 1)
                        dve.tensor_scalar(sg[:, :], sg[:, :], -1.0, None, ALU.mult).then_inc(s_neg, 1)
            self.attend_turned(Ks, Qx, V, O, decay=decay, scale=1.0 / math.sqrt(HD))
            with Phase(nc) as ph:
                s_chain = ph.sem("chain")
                with nc.Block() as block:
                    @block.vector
                    def _(dve):
                        n = [0]
                        link(dve, s_chain, n, dve.tensor_tensor(O[:, :, :], O[:, :, :], gate[:, :, :], ALU.mult))
                        link(dve, s_chain, n, dve.tensor_tensor(self.x[:, :, :], self.x[:, :, :], O[:, :, :], ALU.add))

    def L3_xattn(self):
        nc = self.nc
        self.norm(self.x, self.nrm, self.xT)
        QK = H * DK3 // P
        with self.weights("L3_xattn") as w, self.sb("QT", [P, QK, B * S]) as QT, self.sb("KT", [P, QK, B * SC]) as KT, \
                self.sb("V65", [P, B, H, DK3 + 1]) as V, self.sb("O", [P, NT, H * DK3]) as O:
            jobs = []
            for k in range(QK):
                jobs += self.turned(w["Wq"][:, k * P:(k + 1) * P], self.xT, QT[:, k, :], eng="act" if k % 2 else "dve")
                jobs += self.turned(w["Wk"][:, k * P:(k + 1) * P], self.ctx["ctxT"], KT[:, k, :], width=B * SC)
            for b in range(B):
                for m in range(2):
                    jobs.append(([(0, CH, P, self.ctx["ctxT2"][:, b * P:(b + 1) * P], w["Wv"][:, m * CH:(m + 1) * CH], True, True)],
                                 ("dve", "copy", V[:, b, m * H // 2:(m + 1) * H // 2, 0:DK3], (lambda bank: bank[:, :].rearrange("p (h d) -> p h d", d=DK3))), None))
            self.products(jobs)

            def score(pe, t, banks, first):
                for h in range(H):
                    r = slice(DK3 * (h % 2), DK3 * (h % 2) + DK3)
                    c = (h % 2) * CH + (h // 2) * SC
                    last = pe.matmul(banks[:, c:c + SC], QT[r, h // 2, t * P:(t + 1) * P],
                                     KT[r, h // 2, (t // HALVES) * SC:(t // HALVES + 1) * SC], start=True, stop=True)
                return last
            self.attend_context(score, V, DK3, O[:, :, :].rearrange("p t (h d) -> p t h d", d=DK3))
            with Phase(nc) as ph:
                s_turn, s_mult = ph.sem("turn"), ph.sem("mult")
                with nc.Block() as block:
                    @block.tensor
                    def _(pe):
                        for k in range(QK):
                            for g in range(NCH):
                                n = k * NCH + g
                                if n >= 8:
                                    pe.wait_ge(s_mult, n - 7)
                                for t in range(4 * g, 4 * g + 4):
                                    last = pe.transpose(self.bank(n % 8)[:, (t - 4 * g) * P:(t - 4 * g + 1) * P],
                                                        O[:, t, k * P:(k + 1) * P], self.c["ident"])
                                last.then_inc(s_turn, 1)

                    @block.vector
                    def _(dve):
                        for k in range(QK):
                            for g in range(NCH):
                                n = k * NCH + g
                                dve.wait_ge(s_turn, n + 1)
                                d = QT[:, k, g * CH:(g + 1) * CH]
                                dve.tensor_tensor(d, self.bank(n % 8)[:, :], d, ALU.mult).then_inc(s_mult, 1)
            jobs = []
            self.rows_added(jobs, QT, w["proj"], w["b"], self.x, k=QK)
            self.products(jobs)


STAGES = ["L0_attn", "L0_xattn", "L0_ffn", "L1_attn", "L1_xattn", "L1_ffn",
          "L2_attn", "L2_xattn", "L2_ffn", "L3_attn", "L3_xattn", "L3_ffn"]


def decoder_kernel(nc, dram, where, x, seg, out):
    k = Kernel(nc, dram, where, x, out, seg)
    k.start()
    k.L0_attn()
    k.L0_xattn()
    k.L0_ffn()
    k.L1_attn()
    k.L1_xattn()
    k.L1_ffn()
    k.L2_attn()
    k.L2_xattn()
    k.L2_ffn()
    k.L3_attn()
    k.L3_xattn()
    k.L3_ffn()
    k.finish()


def kernel(**inputs):
    import concourse.bacc as bacc
    from concourse.bass_utils import run_bass_kernel_spmd

    nc = bacc.Bacc("TRN2", target_bir_lowering=False, num_devices=1)
    arrays, dram, where = {}, {}, {}

    def give(name, a):
        a = np.ascontiguousarray(a)
        arrays["in_" + name] = a
        return nc.dram_tensor("in_" + name, a.shape, mybir.dt.from_np(a.dtype), kind="ExternalInput").ap()

    for stage, one in stage_arrays(inputs).items():
        many = isinstance(one, list)
        where[stage] = layout_of(one[0] if many else one)
        dram[stage] = give(stage, np.stack([pack(o, *where[stage]) for o in one]) if many else pack(one, *where[stage]))
    x = give("x", np.asarray(inputs["x"]))
    seg = give("seg", np.asarray(inputs["itok_BxS_0_255"]).reshape(NT, P).T)
    out = nc.dram_tensor("out_0", (B, S, D), F32, kind="ExternalOutput").ap()
    decoder_kernel(nc, dram, where, x, seg, out)
    r = run_bass_kernel_spmd(nc, [arrays], core_ids=[0])
    return r.results[0]["out_0"]
```

```python
import math
from contextlib import ExitStack, contextmanager, nullcontext

import numpy as np

import concourse.bass as bass
from concourse import mybir
from concourse.alu_op_type import AluOpType as ALU

F32 = mybir.dt.float32
F32R = mybir.dt.float32r
BF16 = mybir.dt.bfloat16
I32 = mybir.dt.int32
U32 = mybir.dt.uint32
ACT = mybir.ActivationFunctionType
AX = mybir.AxisListType

B, S, D = 4, 256, 128
P = 128
NT = B * S // P
HALVES = S // P
SC = 64
H, HD = 16, 8
ROWG = 4
CH = 512
NCH = B * S // CH
NEG = -1e30
LAYERS = 4
E, F = 8, 512
FK = F // P
LW = 12
LT, LR = 2, 8 * LW
VW = 32
DK3 = 64
NF0 = 352
FT0 = [(0, 128), (128, 128), (256, 96)]
MIDS = [0.25, 0.75, 1.25, 1.75, 2.5, 3.5, 5.0]
LOW = 32
GROUP = 32
INNER = 256


def constant_arrays():
    p = np.arange(P)
    c = {"ident": np.eye(P, dtype=np.float32)}
    half = np.zeros((P, P), np.float32)
    inter = np.zeros((P, P), np.float32)
    for m in range(P):
        d = m % HD
        if d < HD // 2:
            half[m + HD // 2, m] = -1.0
        else:
            half[m - HD // 2, m] = 1.0
        if m % 2 == 0:
            inter[m + 1, m] = -1.0
        else:
            inter[m - 1, m] = 1.0
    c["rot_half"], c["rot_inter"] = half, inter
    t = np.arange(S, dtype=np.float32)
    inv8 = (1.0 / np.float32(10000.0) ** (np.arange(0, HD, 2, dtype=np.float32) / np.float32(HD))).astype(np.float32)
    ang8 = inv8[(p % HD) % (HD // 2)][:, None] * t[None]
    latent = (p % LW) >= HD
    inv4 = (np.float32(10000.0) ** (-np.arange(0, 4, 2, dtype=np.float32) / np.float32(4))).astype(np.float32)
    ang12 = np.where(latent, inv4[((p % LW - HD) % 4) // 2], 0)[:, None].astype(np.float32) * t[None]
    c["cos8"], c["sin8"], c["cos12"], c["sin12"] = np.cos(ang8), np.sin(ang8), np.cos(ang12)[:LR], np.sin(ang12)[:LR]
    c["cos8q"], c["sin8q"] = c["cos8"] * np.float32(HD ** -0.5), c["sin8"] * np.float32(HD ** -0.5)
    c["mask8"] = np.stack([(p % 32) // 8 == j for j in range(4)], 1)
    c["mask16"] = np.stack([p // 8 == h for h in range(H)], 1)
    c["mask12"] = np.stack([(p[:LR] % (2 * LW)) // LW == j for j in range(2)], 1)
    c["causal_neg"] = np.where(p[None] <= p[:, None], 0.0, NEG)
    c["causal_one"] = (p[:, None] <= p[None]).astype(np.float32)
    q, k = np.arange(S)[None], np.arange(S)[:, None]
    in_chunk = (q // GROUP == k // GROUP) & (k <= q)
    two = lambda a: np.concatenate([a[:P], a[P:]], 1).astype(np.float32)
    c["in_chunk"] = two(in_chunk)
    c["older_chunk"] = two(k // GROUP < q // GROUP)
    c["distance"] = two(np.maximum(q - k, 0))
    c["iota8"] = np.tile(np.arange(E), (P, 1))
    c["keys"] = np.tile(np.arange(SC), (P, 1))
    c["minus_half"] = np.full((P, NT), -0.5)
    c["ones_row"] = np.ones((1, P))
    return {k: np.asarray(v, np.float32) for k, v in c.items()}


def selection_arrays():
    c = {}
    for name, parts in (("high_a", (0, 2)), ("low_a", (1, 3)), ("high_b", (0, 1)), ("low_b", (2, 3))):
        for rows in (P, LR):
            g = rows // ROWG
            sel = np.zeros((rows, ROWG, rows), np.float32)
            for i in range(ROWG):
                for part in parts:
                    for r in range(g):
                        sel[g * i + r, i, g * part + r] = 1.0
            c[f"{name}{rows}"] = sel.reshape(rows, -1)
    return c


def tiles(a):
    k = a.shape[0] // P
    return a.reshape(k, P, -1).transpose(1, 0, 2).reshape(P, -1)


def col(v):
    v = np.asarray(v)
    return v.reshape(-1, min(P, v.size)).T


def twice(v):
    return np.concatenate([v, np.zeros((LOW - E, v.shape[1]), np.float32), v], 0)


def row(v):
    return np.asarray(v).reshape(1, -1)


def spread(v):
    return np.broadcast_to(np.asarray(v).reshape(1, -1), (P, np.asarray(v).size))


def stage_arrays(a):
    g = lambda n: np.asarray(a[n])
    ctx = g("ctx_1024")
    ctxT = ctx.transpose(2, 0, 1)
    out = {}
    constants = constant_arrays()
    take = lambda names: {n: constants.pop(n) for n in names}
    out["tables"] = take(("cos8", "sin8", "cos8q", "sin8q", "cos12", "sin12"))
    masked = take(("causal_neg",))
    inner_tables = take(("keys", "rot_half"))
    chunks, distance = take(("in_chunk", "older_chunk")), take(("distance",))
    out["const"] = constants
    out["selections"] = {**selection_arrays(), **masked}
    out["ctx"] = {
        "ctxT": ctxT.reshape(D, B * SC),
        "ctxT2": np.broadcast_to(ctxT[:, :, None], (D, B, 2, SC)).reshape(D, -1),
        "keep": spread(g("mask_BxS2_ff1")),
    }
    out["L0_attn"] = {n: g("L0_attn_" + n) for n in ("Wv", "Wg", "Win")}
    out["L0_attn"].update(
        **chunks, Wout=tiles(g("L0_attn_Wout")), bv=row(g("L0_attn_bv")), bg=col(g("L0_attn_bg")),
        bin=col(g("L0_attn_bin_")), bout=row(g("L0_attn_bout")),
        **{n: col(g("L0_attn_" + n)) for n in ("g_qq", "b_qq", "g_qk", "b_qk", "g_lq", "b_lq", "g_lk", "b_lk")})
    out["L0_xattn"] = {n: g("L0_xattn_" + n).T for n in ("Wq", "Wk", "Wv", "Wo")}
    out["L0_xattn"].update(bq=col(g("L0_xattn_bq")), bk=col(g("L0_xattn_bk")), bv=row(g("L0_xattn_bv")),
                           bo=row(g("L0_xattn_bo")))
    w0 = {}
    for n in ("w_gate", "w_up"):
        w = g("L0_ffn_" + n)
        for i, (f0, fn) in enumerate(FT0):
            w0[f"{n}{i}"] = w[f0:f0 + fn]
    w0["w_down"] = g("L0_ffn_w_down")
    out["L0_ffn"] = w0
    out["L1_attn"] = {n: g("L1_attn_" + n) for n in ("W_UV", "W_O")}
    heads12 = lambda plain, rotated: np.concatenate([plain.reshape(-1, H, HD), rotated.reshape(-1, H, LW - HD)], 2).reshape(-1, H * LW)
    out["L1_attn"].update(
        W_DQT=g("L1_attn_W_DQ").T, W_DKVT=g("L1_attn_W_DKV").T,
        W_Q=heads12(g("L1_attn_W_UQ"), g("L1_attn_W_QR")),
        W_KC=heads12(g("L1_attn_W_UK"), np.zeros((32, H * (LW - HD)), np.float32)),
        W_KR=heads12(np.zeros((D, D), np.float32), np.tile(g("L1_attn_W_KR"), (1, H))))
    x1 = {n: g("L1_xattn_" + n) for n in ("Wqkv", "bqkv", "Wo", "bo", "Wq_c", "Wkv_c", "Wo_c", "Wg", "Wu", "Wd",
                                           "n1", "n2", "n3")}
    out["inner_attn"] = [
        {"Wq": x1["Wqkv"][l, :D].T, "Wk": x1["Wqkv"][l, D:2 * D].T, "Wv": x1["Wqkv"][l, 2 * D:].T,
         "bq": col(x1["bqkv"][l, :D]), "bk": col(x1["bqkv"][l, D:2 * D]), "bv": row(x1["bqkv"][l, 2 * D:]),
         "Wo": x1["Wo"][l].T, "bo": row(x1["bo"][l]), "Wq_c": x1["Wq_c"][l].T, "Wk_c": x1["Wkv_c"][l, :D].T,
         "Wv_c": x1["Wkv_c"][l, D:].T, "Wo_c": x1["Wo_c"][l].T, "n1": col(x1["n1"][l]), "n2": col(x1["n2"][l])}
        for l in [*range(LAYERS), 0]]
    out["inner_ffn"] = [
        {"Wg": x1["Wg"][l].T, "Wu": x1["Wu"][l].T, "Wd": tiles(x1["Wd"][l].T), "n3": col(x1["n3"][l])}
        for l in range(LAYERS)]
    out["inner_misc"] = {**inner_tables, "nf": spread(g("L1_xattn_nf"))}
    out["L1_ffn"] = {"Wr": g("L1_ffn_Wr").T}
    out["L1_experts"] = [{"Wg": g("L1_ffn_Wg")[e].T, "Wu": g("L1_ffn_Wu")[e].T, "Wd": tiles(g("L1_ffn_Wd")[e].T)}
                         for e in [*range(E), 0]]
    out["L2_attn"] = {n: g("L2_attn_" + n).T for n in ("Wq", "Wk", "Wv", "Wo")}
    kv1, kv2 = g("L2_xattn_kv1_w"), g("L2_xattn_kv2_w")
    out["L2_xattn"] = {
        "q1": g("L2_xattn_q1_w").T, "q2": g("L2_xattn_q2_w").T, "k1": kv1[:D].T, "v1": kv1[D:].T, "k2": kv2[:D].T,
        "proj": g("L2_xattn_proj_w").T, "b": row(g("L2_xattn_proj_b")), "norm": col(g("L2_xattn_norm_w")),
        "l1": spread(g("L2_xattn_lambda_1")), "l2": spread(g("L2_xattn_lambda_2"))}
    out["L2_ffn"] = {"Wr": g("L2_ffn_Wr"), "br": row(g("L2_ffn_br")), "b2": twice(g("L2_ffn_b2"))}
    out["L2_experts"] = [{"W1": g("L2_ffn_W1")[e], "b1": col(g("L2_ffn_b1")[e]), "W2": tiles(g("L2_ffn_W2")[e])}
                         for e in [*range(E), 0]]
    out["L3_attn"] = {n: g("L3_attn_" + n).T for n in ("Wq", "Wk", "Wv", "Wg")}
    out["L3_attn"].update(**distance, bq=col(g("L3_attn_bq")), bk=col(g("L3_attn_bk")), bv=row(g("L3_attn_bv")),
                          bg=row(g("L3_attn_bg")), gamma=spread(g("L3_attn_gamma")))
    heads = lambda w: g(w).transpose(1, 0, 2).reshape(D, H * DK3)
    out["L3_xattn"] = {"Wq": heads("L3_xattn_w_qs"), "Wk": heads("L3_xattn_w_ks"), "Wv": heads("L3_xattn_w_vs"),
                       "proj": tiles(g("L3_xattn_w_proj").T), "b": row(g("L3_xattn_b_proj"))}
    out["L3_ffn"] = {"Wr": g("L3_ffn_router_w").T, "br": row(g("L3_ffn_router_b")), "b2": twice(g("L3_ffn_b2"))}
    out["L3_experts"] = [{"W1": g("L3_ffn_w1")[e].T, "b1": col(g("L3_ffn_b1")[e]), "W2": tiles(g("L3_ffn_w2")[e].T)}
                         for e in [*range(E), 0]]
    return out


def layout_of(arrays):
    at, where = 0, {}
    for name, v in arrays.items():
        where[name] = (v.shape[0], at, v.shape[1])
        at += v.shape[1]
    return where, at


def pack(arrays, where, width):
    out = np.zeros((P, width), np.float32)
    for name, v in arrays.items():
        p, at, n = where[name]
        out[:p, at:at + n] = v
    return out


class Pack:

    def __init__(self, buf, where, source=None):
        self.buf, self.where, self.source = buf, where, source

    def __getitem__(self, name):
        p, at, n = self.where[name]
        return self.buf[0:p, at:at + n]


class Phase:
    FIRST, EACH, count = 110, 24, 0

    def __init__(self, nc):
        self.nc, self.sems = nc, []
        Phase.count += 1
        self.next = self.FIRST + self.EACH * (Phase.count % 2)

    def sem(self, name):
        s = self.nc.alloc_semaphore(f"{name}_{self.nc.next_id()}", self.next)
        self.next += 1
        self.sems.append(s)
        return s

    def __enter__(self):
        return self

    def __exit__(self, kind, *_):
        if kind is None:
            self.nc.clear_and_free_semaphores(self.sems)


def link(eng, sem, count, ins):
    count[0] += 1
    ins.then_inc(sem, 1)
    eng.wait_ge(sem, count[0])


class Kernel:
    def __init__(self, nc, dram, where, x_dram, out_dram, seg_dram):
        self.nc, self.dram, self.where = nc, dram, where
        self.x_dram, self.out_dram, self.seg_dram = x_dram, out_dram, seg_dram
        self.stack = ExitStack()

    def sb(self, name, shape, dt=F32):
        return self.nc.sbuf_tensor(f"{name}_{self.nc.next_id()}", shape, dt)

    def keep(self, name, shape, dt=F32):
        return self.stack.enter_context(self.sb(name, shape, dt))

    def bank(self, n, count=1):
        return self.ps[:, n * CH:(n + count) * CH]

    @contextmanager
    def last_of_body(self):
        yield
        self.nc.all_engine_barrier()

    def start(self):
        nc = self.nc
        Phase.count = 0
        self.s_out = nc.alloc_semaphore("output_written")
        self.ps = self.stack.enter_context(nc.psum_tensor("ps", [P, 8 * CH], F32))
        self.x = self.keep("x", [P, NT, D])
        self.xT = self.keep("xT", [P, NT * P])
        self.nrm = self.keep("nrm", [P, NT, D])
        cwhere, cwidth = self.where["const"]
        xwhere, xwidth = self.where["ctx"]
        twhere, twidth = self.where["tables"]
        cbuf = self.keep("constants", [P, cwidth])
        xbuf = self.keep("context", [P, xwidth])
        tbuf = self.keep("tables", [P, twidth])
        self.c, self.ctx, self.tables = Pack(cbuf, cwhere), Pack(xbuf, xwhere), Pack(tbuf, twhere)
        self.identb = self.keep("identb", [P, P], BF16)
        self.causalb = self.keep("causalb", [P, P], BF16)
        self.sel = {f"{n}{r}": self.keep(n, [r, ROWG, r], F32R) for r in (P, LR) for n in ("high_a", "low_a", "high_b", "low_b")}
        self.keepb = self.keep("keepb", [P, B, SC], BF16)
        self.V2 = self.keep("V2", [P, B, H // 2, 4 * HD])
        self.late = ExitStack()
        swhere, swidth = self.where["selections"]
        sbuf = self.late.enter_context(self.sb("selections", [P, swidth]))
        self.selections = Pack(sbuf, swhere)
        self.s_late = nc.alloc_semaphore("late_constants_loaded")
        with Phase(nc) as ph:
            s_load, s_cast, s_v = ph.sem("load"), ph.sem("cast"), ph.sem("values_zeroed")
            with nc.Block() as block:
                @block.gpsimd
                def _(pool):
                    pool.memset(self.V2[:, :, :, :], 0.0).then_inc(s_v, 1)
                    pool.wait_ge(s_v, 1)
                    for a in range(2):
                        c = 2 * HD * a + HD
                        pool.memset(self.V2[SC * a:SC * (a + 1), :, :, c:c + 1], 1.0).then_inc(s_v, 1)

                @block.sync
                def _(sp):
                    sp.dma_start(self.x[:, :, :], self.x_dram.rearrange("b (h p) d -> p (b h) d", p=P)).then_inc(s_load, 16)
                    sp.dma_start(cbuf[:, :], self.dram["const"][:, :]).then_inc(s_load, 16)
                    for buf, name in ((xbuf, "ctx"), (tbuf, "tables"), (sbuf, "selections")):
                        sp.dma_start(buf[:, :], self.dram[name][:, :]).then_inc(self.s_late, 16)
                    sp.wait_ge(s_load, 32)

                @block.vector
                def _(dve):
                    dve.wait_ge(s_load, 32)
                    dve.tensor_copy(self.identb[:, :], self.c["ident"]).then_inc(s_cast, 1)

    def late_constants(self):
        nc = self.nc
        with self.sb("padding", [P, B * SC]) as padding, Phase(nc) as ph:
            s_mul, s_cast = ph.sem("mul"), ph.sem("cast")
            names = list(self.sel)
            with nc.Block() as block:
                @block.scalar
                def _(act):
                    act.wait_ge(self.s_late, 48)
                    for name in names[0::2]:
                        act.activation(self.sel[name][:, :, :], self.selections[name], ACT.Copy).then_inc(s_cast, 1)

                @block.vector
                def _(dve):
                    dve.wait_ge(self.s_late, 48)
                    dve.tensor_copy(self.causalb[:, :], self.selections["causal_neg"]).then_inc(s_cast, 1)
                    for name in names[1::2]:
                        dve.tensor_copy(self.sel[name][:, :, :], self.selections[name]).then_inc(s_cast, 1)
                    dve.tensor_scalar(padding[:, :], self.ctx["keep"], 1.0, NEG, ALU.not_equal, ALU.mult).then_inc(s_mul, 1)
                    dve.wait_ge(s_mul, 1)
                    dve.tensor_copy(self.keepb[:, :, :], padding[:, :].rearrange("p (b k) -> p b k", b=B)).then_inc(s_cast, 1)

                @block.sync
                def _(sp):
                    sp.wait_ge(self.s_late, 48)
        self.late.close()

    def finish(self):
        nc = self.nc
        s_out = self.s_out
        with nc.Block() as block:
                @block.sync
                def _(sp):
                    sp.dma_start(self.out_dram.rearrange("b (h p) d -> p (b h) d", p=P), self.x[:, :, :]).then_inc(s_out, 16)
                    sp.wait_ge(s_out, 16)
        self.stack.close()

    @contextmanager
    def weights(self, stage):
        where, width = self.where[stage]
        with self.sb("w_" + stage, [P, width]) as buf:
            yield Pack(buf, where, self.dram[stage])

    def norm(self, src, dst, dstT, layer=True, eps=1e-5, weight=None, load=()):
        nc = self.nc
        with self.sb("stats", [P, NT, 6]) as stats, self.sb("mv", [P, NT, 2]) as mv, \
                self.sb("var", [P, NT]) as var, self.sb("rstd", [P, NT]) as rstd, self.sb("sq", [P, NT, D]) as sq, Phase(nc) as ph:
            s_chain, s_var, s_rstd = ph.sem("chain"), ph.sem("var"), ph.sem("rstd")
            s_norm, s_turn, s_copy, s_load = ph.sem("norm"), ph.sem("turn"), ph.sem("copy"), ph.sem("load")
            with nc.Block() as block:
                if load:
                    @block.sync
                    def _(sp):
                        for pack in load:
                            half = pack.buf.shape[1] // 2
                            for cols in (slice(0, half), slice(half, pack.buf.shape[1])):
                                sp.dma_start(pack.buf[:, cols], pack.source[:, cols]).then_inc(s_load, 16)
                        sp.wait_ge(s_load, 32 * len(load))

                @block.vector
                def _(dve):
                    n = [0]
                    G = NT // 2
                    for g in range(2):
                        ts = slice(g * G, (g + 1) * G)
                        if layer:
                            for t in range(g * G, (g + 1) * G):
                                dve.bn_stats(stats[:, t, :], src[:, t, :]).then_inc(s_chain, 1)
                            n[0] += G
                            dve.wait_ge(s_chain, n[0])
                            for t in range(g * G, (g + 1) * G):
                                dve.bn_aggr(mv[:, t, :], stats[:, t, :]).then_inc(s_chain, 1)
                            n[0] += G
                            dve.wait_ge(s_chain, n[0])
                            dve.tensor_scalar(var[:, ts], mv[:, ts, 1], eps, None, ALU.add).then_inc(s_var, 1)
                        else:
                            link(dve, s_chain, n, dve.tensor_tensor(sq[:, ts, :], src[:, ts, :], src[:, ts, :], ALU.mult))
                            link(dve, s_chain, n, dve.tensor_reduce(mv[:, ts, 0], sq[:, ts, :], AX.X, ALU.add))
                            dve.tensor_scalar(var[:, ts], mv[:, ts, 0], 1.0 / D, eps, ALU.mult, ALU.add).then_inc(s_var, 1)
                    for t in range(NT):
                        if t % G == 0:
                            dve.wait_ge(s_rstd, t // G + 1)
                        if layer:
                            ins = dve.tensor_scalar(dst[:, t, :], src[:, t, :], mv[:, t, 0:1], rstd[:, t:t + 1],
                                                    ALU.subtract, ALU.mult)
                        else:
                            ins = dve.tensor_scalar(dst[:, t, :], src[:, t, :], rstd[:, t:t + 1], None, ALU.mult)
                        ins.then_inc(s_norm, 1)

                @block.gpsimd
                def _(pool):
                    for g in range(2):
                        ts = slice(g * NT // 2, (g + 1) * NT // 2)
                        pool.wait_ge(s_var, g + 1)
                        pool.tensor_tensor(rstd[:, ts], var[:, ts], self.c["minus_half"][:, ts], ALU.pow).then_inc(s_rstd, 1)

                if dstT is not None:
                    @block.tensor
                    def _(pe):
                        for t in range(NT):
                            pe.wait_ge(s_norm, t + 1)
                            pe.transpose(self.ps[:, t * P:(t + 1) * P], dst[:, t, :], self.c["ident"]).then_inc(s_turn, 1)

                    @block.scalar
                    def _(act):
                        for g in range(NCH):
                            act.wait_ge(s_turn, (g + 1) * NT // NCH)
                            cols = slice(g * CH, (g + 1) * CH)
                            if weight is None:
                                act.activation(dstT[:, cols], self.ps[:, cols], ACT.Copy).then_inc(s_copy, 1)
                            else:
                                act.activation(dstT[:, cols], self.ps[:, cols], ACT.Copy, scale=weight).then_inc(s_copy, 1)

    def products(self, jobs):
        nc = self.nc
        R = 8
        engine = [ev[0] for _, ev, _ in jobs]
        nth = [engine[:n + 1].count(engine[n]) for n in range(len(jobs))]
        with Phase(nc) as ph:
            s_product = ph.sem("product")
            s_taken = {"act": ph.sem("taken_act"), "dve": ph.sem("taken_dve")}
            s_chain = ph.sem("chain")
            with nc.Block() as block:
                @block.tensor
                def _(pe):
                    for n, (mms, ev, after) in enumerate(jobs):
                        if n >= R:
                            pe.wait_ge(s_taken[engine[n - R]], nth[n - R])
                        if after is not None:
                            pe.wait_ge(s_taken[engine[after]], nth[after])
                        bank = self.bank(n % R)
                        for c0, c1, rows, lhsT, rhs, start, stop in mms:
                            last = pe.matmul(bank[0:rows, c0:c1], lhsT, rhs, start=start, stop=stop)
                        last.then_inc(s_product, 1)

                @block.scalar
                def _(act):
                    for n, (_, ev, _) in enumerate(jobs):
                        if ev[0] != "act":
                            continue
                        act.wait_ge(s_product, n + 1)
                        _, func, dst, pick, bias, scale = ev
                        src = pick(self.bank(n % R))
                        act.activation(dst, src, func, bias=bias, scale=scale).then_inc(s_taken["act"], 1)

                @block.vector
                def _(dve):
                    chain = [0]
                    for n, (_, ev, _) in enumerate(jobs):
                        if ev[0] != "dve":
                            continue
                        dve.wait_ge(s_product, n + 1)
                        kind, dst, pick = ev[1:4]
                        if kind != "diagonal":
                            src = pick(self.bank(n % R))
                        if kind == "copy":
                            ins = dve.tensor_copy(dst, src)
                        elif kind == "diagonal":
                            dve.tensor_copy(dst(0), pick(self.bank(n % R), 0))
                            ins = dve.tensor_copy(dst(1), pick(self.bank(n % R), 1))
                        elif kind == "affine":
                            ins = dve.tensor_scalar(dst, src, ev[4], ev[5], ALU.add, ALU.mult)
                        elif kind == "mult":
                            if len(ev) > 5:
                                dve.wait_ge(s_taken["act"], nth[ev[5]])
                            ins = dve.tensor_tensor(dst, src, ev[4], ALU.mult)
                        elif kind == "add":
                            ins = dve.tensor_tensor(dst, src, ev[4], ALU.add)
                        elif kind == "rope":
                            raw, cos, sin = ev[4:7]
                            link(dve, s_chain, chain, dve.tensor_tensor(dst, raw, cos, ALU.mult))
                            link(dve, s_chain, chain, dve.tensor_tensor(raw, src, sin, ALU.mult))
                            ins = dve.tensor_tensor(dst, dst, raw, ALU.add)
                        ins.then_inc(s_taken["dve"], 1)

    @staticmethod
    def whole(rows=P, cols=CH):
        return lambda bank: bank[0:rows, 0:cols]

    @staticmethod
    def rows_of_heads():
        return lambda bank: bank[:, :].rearrange("p (t h d) -> p t h d", h=H, d=HD)

    def turned(self, W, src, dst, m=P, bias=0.0, scale=1.0, func=ACT.Identity, eng="act", width=B * S):
        jobs = []
        step = min(CH, width)
        for c in range(0, width, step):
            cols = slice(c, c + step)
            mms = [(0, step, m, W, src[:, cols], True, True)]
            pick = self.whole(m, step)
            if eng == "act":
                jobs.append((mms, ("act", func, dst[:, cols], pick, bias, scale), None))
            elif isinstance(bias, float):
                jobs.append((mms, ("dve", "copy", dst[:, cols], pick), None))
            else:
                jobs.append((mms, ("dve", "affine", dst[:, cols], pick, bias, scale), None))
        return jobs

    def roped(self, jobs, sources, dst, raw, rot, cos, sin, bias=0.0, m=P):
        first = len(jobs)
        two = lambda a: a.unsqueeze(1).to_broadcast([m, CH // S, S])
        v = lambda a: a.rearrange("p (b s) -> p b s", s=S)
        for c in range(NCH):
            cols = slice(c * CH, (c + 1) * CH)
            mms = [(0, CH, m, W, src[:, cols], k == 0, k == len(sources) - 1) for k, (W, src) in enumerate(sources)]
            jobs.append((mms, ("act", ACT.Identity, raw[:, cols], self.whole(m), bias, 1.0), None))
        for c in range(NCH):
            cols = slice(c * CH, (c + 1) * CH)
            jobs.append(([(0, CH, m, rot[0:m, 0:m], raw[:, cols], True, True)],
                         ("dve", "rope", v(dst[:, cols]), (lambda bank: v(bank[0:m, :])), v(raw[:, cols]), two(cos), two(sin)),
                         first + c))

    def value_rows(self, W, src, dst, bias=None, n=NT, k=P):
        jobs = []
        for g in range(0, n, 4):
            mms = []
            for t in range(g, min(g + 4, n)):
                c = (t - g) * P
                mms.append((c, c + P, P, src[0:k, t * P:(t + 1) * P], W, True, bias is None))
                if bias is not None:
                    mms.append((c, c + P, P, self.c["ones_row"], bias, False, True))
            jobs.append((mms, ("dve", "copy", dst[:, g:min(g + 4, n), :, 0:HD], self.rows_of_heads()), None))
        return jobs

    def stack_operands(self, plain, masked, masks, V=None, m=P, heads=4):
        nc = self.nc
        T = plain[0].shape[1]
        G = T * ROWG
        dst = masked[1]
        jobs = [(masked[0], dst[:, :, heads - 1, :], "b"), (*plain, "a")]
        units = [(n, t, i, c) for n in range(2) for t in range(T) for i in range(ROWG) for c in range(NCH)]
        parts = [(n, t, c) for n in range(2) for t in range(T) for c in range(NCH)]
        with self.sb("high", [m, 2, T, B * S], F32R) as high, self.sb("low", [m, 2, T, B * S], F32R) as low, Phase(nc) as ph:
            s_high, s_low, s_product = ph.sem("high"), ph.sem("low"), ph.sem("product")
            s_copied, s_v = ph.sem("copied"), ph.sem("values_padded")
            s_masked = {"act": ph.sem("masked_act"), "dve": ph.sem("masked_dve")}
            cols = lambda c: slice(c * CH, (c + 1) * CH)

            by_act = 1 if heads > 2 else 0

            def copy_of_last(g):
                return dst[:, g, heads - 1, :].bitcast(F32)

            with nc.Block() as block:
                @block.scalar
                def _(act):
                    for n, t, c in parts:
                        act.activation(high[:, n, t, cols(c)], jobs[n][0][:, t, cols(c)], ACT.Copy).then_inc(s_high, 1)
                    for k, (n, t, i, c) in enumerate(units):
                        g = t * ROWG + i
                        act.wait_ge(s_product, k + 1)
                        act.activation(jobs[n][1][:, g, cols(c)], self.bank(k % 8)[0:m, :], ACT.Copy).then_inc(s_copied, 1)
                        if by_act and k >= NCH and k % NCH == 0 and k <= G * NCH:
                            g = k // NCH - 1
                            act.wait_ge(s_copied, k)
                            act.activation(dst[:, g, 0, :], copy_of_last(g), ACT.Copy, scale=masks[:, 0:1]).then_inc(s_masked["act"], 1)

                @block.vector
                def _(dve):
                    for k, (n, t, c) in enumerate(parts):
                        dve.wait_ge(s_high, k + 1)
                        dve.tensor_tensor(low[:, n, t, cols(c)], jobs[n][0][:, t, cols(c)], high[:, n, t, cols(c)].bitcast(F32),
                                          ALU.subtract).then_inc(s_low, 1)

                    def last_head(g):
                        if by_act:
                            dve.wait_ge(s_masked["act"], g + 1)
                        dve.wait_ge(s_masked["dve"], (g + 1) * (heads - 1 - by_act))
                        dve.tensor_scalar(dst[:, g, heads - 1, :], copy_of_last(g), masks[:, heads - 1:heads], None, ALU.mult).then_inc(s_masked["dve"], 1)

                    for g in range(G):
                        dve.wait_ge(s_copied, (g + 1) * NCH)
                        for j in range(by_act, heads - 1):
                            dve.tensor_scalar(dst[:, g, j, :], copy_of_last(g), masks[:, j:j + 1], None, ALU.mult).then_inc(s_masked["dve"], 1)
                        if g >= 2:
                            last_head(g - 2)
                    last_head(G - 2)
                    last_head(G - 1)

                @block.tensor
                def _(pe):
                    for k, (n, t, i, c) in enumerate(units):
                        if k >= 8:
                            pe.wait_ge(s_copied, k - 7)
                        if i == 0:
                            pe.wait_ge(s_low, parts.index((n, t, c)) + 1)
                        side = jobs[n][2]
                        bank = self.bank(k % 8)[0:m, :]
                        pe.matmul(bank, self.sel[f"high_{side}{m}"][:, i, :], high[:, n, t, cols(c)], start=True, stop=False)
                        pe.matmul(bank, self.sel[f"low_{side}{m}"][:, i, :], low[:, n, t, cols(c)], start=False, stop=True).then_inc(s_product, 1)

                if V is not None:
                    @block.gpsimd
                    def _(pool):
                        pool.memset(V[:, :, :, HD:HD + 1], 1.0).then_inc(s_v, 1)
                        pool.memset(V[:, :, :, HD + 1:VW], 0.0).then_inc(s_v, 1)

    def attend(self, Qs, Kx, V, O):
        nc = self.nc
        units = [(b, q, i) for b in range(B) for q in range(HALVES) for i in range(ROWG)]
        N = len(units)
        first_pt, n_pt = {}, 0
        for n, (b, q, i) in enumerate(units):
            first_pt[n] = n_pt
            n_pt += q + 1
        sbanks = [range(n % 4, n % 4 + 1) if q == 0 else range(2 * (n % 2), 2 * (n % 2) + 2) for n, (b, q, i) in enumerate(units)]
        before = [max([m for m in range(n) if set(sbanks[m]) & set(sbanks[n])], default=None) for n in range(N)]
        with self.sb("probs", [P, 3, 2, 4, P]) as pr, self.sb("probsT", [P, 4, 4, P]) as pT, \
                self.sb("nmax", [P, 4, 4]) as nmax, self.sb("rsum", [P, 2, ROWG, 4]) as rsum, \
                self.sb("outT", [P, 2, ROWG, P]) as oT, Phase(nc) as ph:
            s_scores, s_max, s_exp = ph.sem("scores"), ph.sem("max"), ph.sem("exp")
            s_turn, s_out, s_ot = ph.sem("turn"), ph.sem("out"), ph.sem("out_copied")
            s_pt = {"act": ph.sem("pt_act"), "dve": ph.sem("pt_dve")}
            s_back, s_rec, s_norm = ph.sem("turned_back"), ph.sem("rec"), ph.sem("norm")
            blocks = [(n, kb) for n in range(N) for kb in range(units[n][1] + 1)]
            copier = ["act" if units[n][2] % 2 and units[n][1] == kb == 1 else "dve" for n, kb in blocks]

            def wait_copied(eng, m):
                eng.wait_ge(s_pt[copier[m]], copier[:m + 1].count(copier[m]))

            def copy_block(eng, name, m, copy):
                n, kb = blocks[m]
                if n >= 2:
                    eng.wait_ge(s_out, n - 1)
                eng.wait_ge(s_turn, m + 1)
                copy(pT[:, m % 4, :, :], self.bank(4 + m % 2)).then_inc(s_pt[name], 1)

            def sbank(n):
                return self.bank(sbanks[n].start, len(sbanks[n]))

            obank, rbank = self.bank(6), self.bank(7)

            with nc.Block() as block:
                @block.tensor
                def _(pe):
                    def scores(n):
                        b, q, i = units[n]
                        if before[n] is not None:
                            pe.wait_ge(s_exp, 4 * (before[n] + 1))
                        qs = Qs[:, i, b * S + q * P:b * S + (q + 1) * P]
                        for kb in range(q + 1):
                            o = sbank(n)[:, kb * CH:(kb + 1) * CH]
                            diag = kb == q
                            last = pe.matmul(o, qs, Kx[:, i, :, b * S + kb * P:b * S + (kb + 1) * P],
                                             start=True, stop=not diag)
                            if diag:
                                last = pe.matmul(o, self.identb[:, :],
                                                 self.causalb[:, :].unsqueeze(1).to_broadcast([P, 4, P]),
                                                 start=False, stop=True)
                        last.then_inc(s_scores, 1)

                    def turn(n):
                        b, q, i = units[n]
                        for kb in range(q + 1):
                            m = first_pt[n] + kb
                            if m >= 2:
                                wait_copied(pe, m - 2)
                            for j in range(4):
                                if kb == 0:
                                    pe.wait_ge(s_exp, 4 * n + j + 1)
                                last = pe.transpose(self.bank(4 + m % 2)[:, j * P:(j + 1) * P], pr[:, n % 3, kb, j, :],
                                                    self.c["ident"])
                            last.then_inc(s_turn, 1)

                    def out(n):
                        b, q, i = units[n]
                        g = n // ROWG
                        if i == 0 and g >= 1:
                            pe.wait_ge(s_ot, g)
                        for kb in range(q + 1):
                            m = first_pt[n] + kb
                            wait_copied(pe, m)
                            for j in range(4):
                                last = pe.matmul(obank[32 * j:32 * j + 32, i * P:(i + 1) * P], V[:, 2 * b + kb, 4 * i + j, :],
                                                 pT[:, m % 4, j, :], start=(kb == 0), stop=(kb == q))
                        last.then_inc(s_out, 1)

                    def back(g):
                        pe.wait_ge(s_ot, g + 1)
                        if g >= 1:
                            pe.wait_ge(s_norm, g)
                        for i in range(ROWG):
                            last = pe.transpose(rbank[:, i * P:(i + 1) * P], oT[:, g % 2, i, :], self.c["ident"])
                        last.then_inc(s_back, 1)

                    for n in range(N + 5):
                        if n < N:
                            scores(n)
                        if 2 <= n < N + 2:
                            turn(n - 2)
                        if n >= 8 and n % ROWG == 0:
                            back(n // ROWG - 2)
                        if 3 <= n < N + 3:
                            out(n - 3)

                @block.scalar
                def _(act):
                    for n in range(N + 4):
                        if n >= 7 and (n - 3) % ROWG == 0:
                            g = (n - 3) // ROWG - 1
                            act.wait_ge(s_out, ROWG * (g + 1))
                            if g >= 2:
                                act.wait_ge(s_back, g - 1)
                            act.activation(oT[:, g % 2, :, :], obank, ACT.Copy).then_inc(s_ot, 1)
                        for m, (unit, kb) in enumerate(blocks):
                            if unit == n - 2 and copier[m] == "act":
                                copy_block(act, "act", m, lambda dst, src: act.activation(dst, src, ACT.Copy))
                        if n < N:
                            b, q, i = units[n]
                            act.wait_ge(s_max, n + 1)
                            if n >= 3:
                                act.wait_ge(s_turn, first_pt[n - 2])
                            s = sbank(n)[:, 0:(q + 1) * CH].rearrange("p (k j c) -> p j k c", j=4, c=P)
                            for j in range(4):
                                act.activation(pr[:, n % 3, 0:q + 1, j, :], s[:, j, :, :], ACT.Exp,
                                               bias=nmax[:, n % 4, j:j + 1]).then_inc(s_exp, 1)

                @block.vector
                def _(dve):
                    def normalise(g):
                        dve.wait_ge(s_back, g + 1)
                        o = rbank.rearrange("p (i j d) -> p i j d", i=ROWG, d=VW)
                        dve.reciprocal(rsum[:, g % 2, :, :], o[:, :, :, HD]).then_inc(s_rec, 1)
                        dve.wait_ge(s_rec, g + 1)
                        dve.tensor_tensor(O[:, g, :].rearrange("p (h d) -> p h d", d=HD), rbank.rearrange("p (h d) -> p h d", d=VW)[:, :, 0:HD],
                                          rsum[:, g % 2, :, :].rearrange("p i j -> p (i j)").unsqueeze(2).to_broadcast([P, H, HD]), ALU.mult).then_inc(s_norm, 1)

                    for n in range(N + 5):
                        if n < N:
                            b, q, i = units[n]
                            dve.wait_ge(s_scores, n + 1)
                            if n >= 4:
                                dve.wait_ge(s_exp, 4 * (n - 3))
                            s = sbank(n)[:, 0:(q + 1) * CH].rearrange("p (k j c) -> p j k c", j=4, c=P)
                            dve.tensor_reduce(nmax[:, n % 4, :], s, AX.XY, ALU.max, negate=True).then_inc(s_max, 1)
                        for m, (unit, kb) in enumerate(blocks):
                            if unit == n - 2 and copier[m] == "dve":
                                copy_block(dve, "dve", m, dve.tensor_copy)
                        if n >= 8 and n % ROWG == 0:
                            normalise(n // ROWG - 2)

    def attend_context(self, score, V, O=None, bias=None, per_token=False, combine=None, gated=None, keys=None):
        nc = self.nc
        PAIRS = H // 2
        with self.sb("sub", [P, 2, H, SC]) as sub, self.sb("probsX", [P, 3, H, SC]) as pr, \
                self.sb("probsXT", [P, 2, PAIRS, HALVES, P]) as pT, self.sb("nmaxX", [P, 2, H]) as nmax, \
                self.sb("rsumX", [P, 2, HALVES, H]) as rsum, self.sb("outXT", [P, 2, HALVES, P]) as oT, \
                self.sb("part", [P, HALVES, H, HD]) as part, Phase(nc) as ph:
            s_scores, s_max, s_sub, s_exp = ph.sem("scores"), ph.sem("max"), ph.sem("sub"), ph.sem("exp")
            s_sum, s_rec, s_weights = ph.sem("sum"), ph.sem("rec"), ph.sem("weights_normalised")
            s_turn, s_pt, s_out, s_gated = ph.sem("turn"), ph.sem("pt"), ph.sem("out"), ph.sem("gated")
            s_ot, s_back, s_norm, s_combined = ph.sem("out_copied"), ph.sem("back"), ph.sem("norm"), ph.sem("combined")
            s_probs = s_exp if gated is None else s_weights
            s_first_keys, s_keys = ph.sem("first_keys"), ph.sem("later_keys")
            sbanks = lambda t: self.bank(2 * (t % 2), 2)

            def expand(eng, b):
                src, dst = keys
                ks = slice(b * SC, (b + 1) * SC)
                return eng.tensor_tensor(dst[:, :, ks], src[:, ks].unsqueeze(1).to_broadcast([P, H, SC]),
                                         self.c["mask16"].unsqueeze(2).to_broadcast([P, H, SC]), ALU.mult)

            obank, rbank = self.bank(6), self.bank(7)

            with nc.Block() as block:
                if keys is not None:
                    @block.gpsimd
                    def _(pool):
                        for b in range(1, B):
                            expand(pool, b).then_inc(s_keys, 1)

                @block.tensor
                def _(pe):
                    def scores(t):
                        if keys is not None and t == 0:
                            pe.wait_ge(s_first_keys, 1)
                        if keys is not None and t >= HALVES and t % HALVES == 0:
                            pe.wait_ge(s_keys, t // HALVES)
                        if t >= 2:
                            pe.wait_ge(s_sub, t - 1)
                        if bias is not None:
                            bt = bias[:, t, :] if per_token else bias[:, t // HALVES, :]
                            for g in range(2):
                                pe.matmul(sbanks(t)[:, g * CH:(g + 1) * CH], self.identb[:, :],
                                          bt.unsqueeze(1).to_broadcast([P, H // 2, SC]), start=True, stop=False)
                        score(pe, t, sbanks(t), bias is None).then_inc(s_scores, 1)

                    def turn(t):
                        pe.wait_ge(s_probs, t + 1)
                        for g in range(2):
                            if t >= 1:
                                pe.wait_ge(s_pt, 2 * t + g - 1)
                            for k in range(4):
                                k2 = 4 * g + k
                                last = pe.transpose(self.bank(4 + g)[:, k * P:(k + 1) * P],
                                                    pr[:, t % 3, 2 * k2:2 * k2 + 2, :], self.c["ident"])
                            last.then_inc(s_turn, 1)

                    def out(b):
                        pe.wait_ge(s_pt, 2 * HALVES * (b + 1))
                        if gated is None:
                            if b >= 1:
                                pe.wait_ge(s_ot, b)
                            for k in range(PAIRS):
                                g, j = k // 4, k % 4
                                last = pe.matmul(obank[32 * j:32 * j + 32, g * S:(g + 1) * S], V[:, b, k, :],
                                                 pT[:, b % 2, k, :, :], start=True, stop=True)
                            last.then_inc(s_out, 1)
                        else:
                            for u in range(PAIRS // 2):
                                n = b * PAIRS // 2 + u
                                if n >= 2:
                                    pe.wait_ge(s_gated, n - 1)
                                for k in range(2):
                                    last = pe.matmul(self.bank(6 + n % 2)[:, k * S:(k + 1) * S], V[:, b, 2 * u + k, :],
                                                     pT[:, b % 2, 2 * u + k, :, :], start=True, stop=True)
                                last.then_inc(s_out, 1)

                    def back(b):
                        pe.wait_ge(s_ot, b + 1)
                        if b >= 1:
                            pe.wait_ge(s_norm, b)
                        for q in range(HALVES):
                            for g in range(2):
                                last = pe.transpose(rbank[:, (2 * q + g) * P:(2 * q + g + 1) * P], oT[:, g, q, :], self.c["ident"])
                        last.then_inc(s_back, 1)

                    for n in range(NT + HALVES + 2):
                        if n < NT:
                            scores(n)
                        if 2 <= n < NT + 2:
                            turn(n - 2)
                        if n % 2 == 0 and n >= 4:
                            out((n - 4) // 2)
                        if gated is None and n % 2 == 1 and n >= 5:
                            back((n - 5) // 2)

                @block.scalar
                def _(act):
                    for n in range(NT + HALVES + 1):
                        if n < NT:
                            act.wait_ge(s_sub, n + 1)
                            if n >= 3:
                                act.wait_ge(s_turn, 2 * (n - 2))
                            act.activation(pr[:, n % 3, :, :], sub[:, n % 2, :, :], ACT.Exp).then_inc(s_exp, 1)
                        if 2 <= n < NT + 2:
                            t = n - 2
                            b, q = t // HALVES, t % HALVES
                            if b >= 2 and q == 0:
                                act.wait_ge(s_out, (b - 1) * (1 if gated is None else PAIRS // 2))
                            for g in range(2):
                                act.wait_ge(s_turn, 2 * t + g + 1)
                                act.activation(pT[:, b % 2, 4 * g:4 * g + 4, q, :], self.bank(4 + g), ACT.Copy).then_inc(s_pt, 1)
                        if gated is None and n % 2 == 0 and n >= 4:
                            b = (n - 4) // 2
                            act.wait_ge(s_out, b + 1)
                            if b >= 1:
                                act.wait_ge(s_back, b)
                            act.activation(oT[:, :, :, :], obank, ACT.Copy).then_inc(s_ot, 1)

                @block.vector
                def _(dve):
                    def normalise(b):
                        dve.wait_ge(s_back, b + 1)
                        rows = rbank.rearrange("p (q h d) -> p q h d", h=H, d=2 * HD)
                        r = rsum[:, b % 2, :, :]
                        dve.reciprocal(r, rows[:, :, :, HD]).then_inc(s_rec, 1)
                        dve.wait_ge(s_rec, b + 1)
                        if combine is not None:
                            dve.tensor_tensor(r, r, combine.unsqueeze(1).to_broadcast([P, HALVES, H]), ALU.mult).then_inc(s_sum, 1)
                            dve.wait_ge(s_sum, b + 1)
                            if b >= 1:
                                dve.wait_ge(s_combined, b)
                        o = O[:, 2 * b:2 * b + 2, :].rearrange("p q (h d) -> p (q h) d", d=HD)
                        d = o if combine is None else part[:, :, :, :].rearrange("p q h d -> p (q h) d")
                        dve.tensor_tensor(d, rows[:, :, :, 0:HD].rearrange("p q h d -> p (q h) d"),
                                          r.rearrange("p q h -> p (q h)").unsqueeze(2).to_broadcast([P, HALVES * H, HD]), ALU.mult).then_inc(s_norm, 1)
                        if combine is not None:
                            dve.wait_ge(s_norm, b + 1)
                            dve.tensor_tensor(o, o, d, ALU.subtract).then_inc(s_combined, 1)

                    def weigh(t):
                        dve.wait_ge(s_exp, t + 1)
                        r = rsum[:, t % 2, :, :]
                        p = pr[:, t % 3, :, :]
                        dve.tensor_reduce(r[:, 0, :], p, AX.X, ALU.add).then_inc(s_sum, 1)
                        dve.wait_ge(s_sum, t + 1)
                        dve.reciprocal(r[:, 1, :], r[:, 0, :]).then_inc(s_rec, 1)
                        dve.wait_ge(s_rec, t + 1)
                        dve.tensor_tensor(p, p, r[:, 1, :].unsqueeze(2).to_broadcast([P, H, SC]), ALU.mult).then_inc(s_weights, 1)

                    if keys is not None:
                        expand(dve, 0).then_inc(s_first_keys, 1)
                    for n in range(NT + HALVES + 2):
                        if n < NT:
                            s = sbanks(n).rearrange("p (h k) -> p h k", k=SC)
                            dve.wait_ge(s_scores, n + 1)
                            dve.tensor_reduce(nmax[:, n % 2, :], s, AX.X, ALU.max, negate=True).then_inc(s_max, 1)
                            dve.wait_ge(s_max, n + 1)
                            if n >= 2:
                                dve.wait_ge(s_exp, n - 1)
                            dve.tensor_tensor(sub[:, n % 2, :, :], s,
                                              nmax[:, n % 2, :].unsqueeze(2).to_broadcast([P, H, SC]), ALU.add).then_inc(s_sub, 1)
                        if gated is None:
                            if n % 2 == 1 and n >= 5:
                                normalise((n - 5) // 2)
                        else:
                            if 1 <= n <= NT:
                                weigh(n - 1)
                            if n % 2 == 0 and n >= 4:
                                b = (n - 4) // 2
                                for u in range(PAIRS // 2):
                                    k = b * PAIRS // 2 + u
                                    dve.wait_ge(s_out, k + 1)
                                    d = gated[:, 2 * u:2 * u + 2, b * S:(b + 1) * S]
                                    dve.tensor_tensor(d, self.bank(6 + k % 2).rearrange("p (k s) -> p k s", s=S), d, ALU.mult).then_inc(s_gated, 1)

    def head_scores(self, QT, Kx):
        def score(pe, t, banks, first):
            b = t // HALVES
            for g in range(2):
                last = pe.matmul(banks[:, g * CH:(g + 1) * CH], QT[:, t * P:(t + 1) * P],
                                 Kx[:, g * H // 2:(g + 1) * H // 2, b * SC:(b + 1) * SC], start=first, stop=True)
            return last
        return score

    def project(self, src, W, bias, dst, scale=None):
        nc = self.nc
        with self.sb("srcT", [P, NT * P]) as srcT, Phase(nc) as ph:
            s_turn, s_copy, s_product, s_sum = ph.sem("turn"), ph.sem("copy"), ph.sem("product"), ph.sem("sum")
            with nc.Block() as block:
                @block.tensor
                def _(pe):
                    for t in range(NT):
                        pe.transpose(self.ps[:, t * P:(t + 1) * P], src[:, t, :], self.c["ident"]).then_inc(s_turn, 1)
                    for t in range(NT):
                        pe.wait_ge(s_copy, t // 4 + 1)
                        o = self.ps[:, (NT + t) * P:(NT + t + 1) * P]
                        last = pe.matmul(o, srcT[:, t * P:(t + 1) * P], W, start=True, stop=bias is None)
                        if bias is not None:
                            last = pe.matmul(o, self.c["ones_row"], bias, start=False, stop=True)
                        last.then_inc(s_product, 1)

                @block.scalar
                def _(act):
                    for g in range(NCH):
                        cols = slice(g * CH, (g + 1) * CH)
                        act.wait_ge(s_turn, 4 * (g + 1))
                        act.activation(srcT[:, cols], self.ps[:, cols], ACT.Copy,
                                       scale=1.0 if scale is None else scale).then_inc(s_copy, 1)

                @block.vector
                def _(dve):
                    for g in range(NCH):
                        dve.wait_ge(s_product, 4 * (g + 1))
                        dve.tensor_tensor(dst[:, 4 * g:4 * g + 4, :],
                                          self.bank(2 + g)[:, :].rearrange("p (t d) -> p t d", d=D),
                                          dst[:, 4 * g:4 * g + 4, :], ALU.add).then_inc(s_sum, 1)

    def rows_added(self, jobs, srcT, W, bias, dst, k=1, after=(None, None)):
        for g in range(NCH):
            mms = []
            for t in range(4 * g, 4 * g + 4):
                c = (t - 4 * g) * P
                for kk in range(k):
                    mms.append((c, c + P, P, srcT[:, kk, t * P:(t + 1) * P], W[:, kk * D:(kk + 1) * D],
                                kk == 0, bias is None and kk == k - 1))
                if bias is not None:
                    mms.append((c, c + P, P, self.c["ones_row"], bias, False, True))
            d = dst[:, 4 * g:4 * g + 4, :]
            jobs.append((mms, ("dve", "add", d, (lambda bank: bank[:, :].rearrange("p (t d) -> p t d", d=D)), d), after[g]))

    def L0_attn(self):
        nc = self.nc
        EK = INNER // P
        with self.weights("L0_attn") as w, self.sb("v", [P, NT, INNER]) as v, self.sb("gateT", [P, EK, B * S]) as gateT, \
                self.sb("baseT", [P, B * S]) as baseT, self.sb("four", [P, 4, B * S]) as four, \
                self.sb("oT", [P, EK, B * S]) as oT:
            self.norm(self.x, self.nrm, self.xT, load=(w,))
            jobs = []
            for e in range(EK):
                jobs += self.turned(w["Wg"][:, e * P:(e + 1) * P], self.xT, gateT[:, e, :], bias=w["bg"][:, e:e + 1], func=ACT.Silu)
            jobs += self.turned(w["Win"], self.xT, baseT, bias=w["bin"], func=ACT.Silu)
            for g in range(0, NT, 2):
                mms = []
                for t in (g, g + 1):
                    c = (t - g) * INNER
                    mms.append((c, c + INNER, P, self.xT[:, t * P:(t + 1) * P], w["Wv"], True, False))
                    mms.append((c, c + INNER, P, self.c["ones_row"], w["bv"], False, True))
                jobs.append((mms, ("act", ACT.Silu, v[:, g:g + 2, :], self.whole(), 0.0, 1.0), None))
            self.products(jobs)
            QQ, QK, LQ, LK = range(4)
            with Phase(nc) as ph:
                s_aff = ph.sem("affine")
                with nc.Block() as block:
                    @block.vector
                    def _(dve):
                        for n, name in enumerate(("qq", "qk", "lq", "lk")):
                            dve.tensor_scalar(four[:, n, :], baseT[:, :], w["g_" + name], w["b_" + name],
                                              ALU.mult, ALU.add).then_inc(s_aff, 1)
            units = [(b, kb) for b in range(B) for kb in range(HALVES)]
            with self.sb("sq", [P, 2, S]) as sq, self.sb("mix", [P, 4, S]) as mix, Phase(nc) as ph:
                s_scores, s_relu, s_chain, s_mix = ph.sem("scores"), ph.sem("relu"), ph.sem("chain"), ph.sem("mix")
                s_out, s_gated = ph.sem("out"), ph.sem("gated")
                with nc.Block() as block:
                    @block.tensor
                    def _(pe):
                        def out(b):
                            pe.wait_ge(s_mix, 2 * b + 2)
                            if b >= 2:
                                pe.wait_ge(s_gated, b - 1)
                            for e in range(EK):
                                for kb in range(HALVES):
                                    last = pe.matmul(self.bank(4 + b % 2)[:, e * S:(e + 1) * S], v[:, 2 * b + kb, e * P:(e + 1) * P],
                                                     mix[:, (2 * b + kb) % 4, :], start=(kb == 0), stop=(kb == 1))
                            last.then_inc(s_out, 1)
                        for n, (b, kb) in enumerate(units):
                            if n >= 4:
                                pe.wait_ge(s_mix, n - 3)
                            ks = slice(b * S + kb * P, b * S + (kb + 1) * P)
                            qs = slice(b * S, (b + 1) * S)
                            pe.matmul(self.bank(n % 4)[:, 0:S], four[:, QK, ks], four[:, QQ, qs], start=True, stop=True)
                            pe.matmul(self.bank(n % 4)[:, S:2 * S], four[:, LK, ks], four[:, LQ, qs], start=True, stop=True).then_inc(s_scores, 1)
                            if n >= 3 and n % 2 == 1:
                                out(n // 2 - 1)
                        out(B - 1)

                    @block.scalar
                    def _(act):
                        for n in range(len(units)):
                            act.wait_ge(s_scores, n + 1)
                            if n >= 2:
                                act.wait_ge(s_mix, n - 1)
                            act.activation(sq[:, n % 2, :], self.bank(n % 4)[:, 0:S], ACT.Relu, scale=1.0 / INNER ** 0.5).then_inc(s_relu, 1)

                    @block.vector
                    def _(dve):
                        chain = [0]

                        def gate(b):
                            dve.wait_ge(s_out, b + 1)
                            dve.tensor_tensor(oT[:, :, b * S:(b + 1) * S], self.bank(4 + b % 2)[:, :].rearrange("p (e s) -> p e s", e=EK),
                                              gateT[:, :, b * S:(b + 1) * S], ALU.mult).then_inc(s_gated, 1)
                        for n, (b, kb) in enumerate(units):
                            dve.wait_ge(s_relu, n + 1)
                            if n >= 4:
                                dve.wait_ge(s_out, (n - 4) // 2 + 1)
                            m = slice(kb * S, (kb + 1) * S)
                            link(dve, s_chain, chain, dve.tensor_tensor(sq[:, n % 2, :], sq[:, n % 2, :], sq[:, n % 2, :], ALU.mult))
                            link(dve, s_chain, chain, dve.tensor_tensor(sq[:, n % 2, :], sq[:, n % 2, :], w["in_chunk"][:, m], ALU.mult))
                            link(dve, s_chain, chain, dve.tensor_tensor(mix[:, n % 4, :], self.bank(n % 4)[:, S:2 * S], w["older_chunk"][:, m], ALU.mult))
                            dve.tensor_tensor(mix[:, n % 4, :], mix[:, n % 4, :], sq[:, n % 2, :], ALU.add).then_inc(s_mix, 1)
                            if n >= 3 and n % 2 == 1:
                                gate(n // 2 - 1)
                        gate(B - 1)
            jobs = []
            self.rows_added(jobs, oT, w["Wout"], w["bout"], self.x, k=EK)
            self.products(jobs)

    def context_keys_values(self, jobs, Wk, Wv, KT, bk=0.0, bv=None):
        jobs += self.turned(Wk, self.ctx["ctxT"], KT, bias=bk, width=B * SC)
        mms = []
        for b in range(B):
            c = b * P
            mms.append((c, c + P, P, self.ctx["ctxT2"][:, c:c + P], Wv, True, bv is None))
            if bv is not None:
                mms.append((c, c + P, P, self.c["ones_row"], bv, False, True))
        half = lambda a: slice(SC * a, SC * (a + 1))
        jobs.append((mms, ("dve", "diagonal", (lambda a: self.V2[half(a), :, :, 2 * HD * a:2 * HD * a + HD]),
                           (lambda bank, a: bank[half(a), :].rearrange("p (b k a d) -> p b k a d", b=B, a=2, d=HD)[:, :, :, a, :])), None))

    def L0_xattn(self):
        with self.weights("L0_xattn") as w, self.sb("QT", [P, B * S]) as QT, self.sb("KT", [P, B * SC]) as KT, \
                self.sb("Kx", [P, H, B * SC]) as Kx, self.sb("O", [P, NT, D]) as O:
            self.norm(self.x, self.nrm, self.xT, load=(w,))
            jobs = []
            for c in range(NCH):
                cols = slice(c * CH, (c + 1) * CH)
                jobs.append(([(0, CH, P, w["Wq"], self.xT[:, cols], True, True)],
                             ("dve", "affine", QT[:, cols], self.whole(), w["bq"], HD ** -0.5), None))
            self.context_keys_values(jobs, w["Wk"], w["Wv"], KT, w["bk"], w["bv"])
            self.products(jobs)
            self.attend_context(self.head_scores(QT, Kx), self.V2, O, bias=self.keepb, keys=(KT, Kx))
            self.project(O, w["Wo"], w["bo"], self.x)

    def quantise(self, tensors):
        nc = self.nc
        STEPS = [0.5, 0.5, 0.5, 0.5, 1.0, 1.0, 2.0]
        KB = CH // 16
        units = [a[:, k:min(k + KB, a.shape[1]), :] for a in tensors for k in range(0, a.shape[1], KB)]
        with self.sb("sc", [P, 3, KB]) as sc, self.sb("inv", [P, 3, KB]) as inv, self.sb("scaled", [P, 2, KB, 16]) as scaled, \
                self.sb("sgn", [P, 3, KB, 16]) as sgn, self.sb("magnitude", [P, 3, KB, 16]) as magnitude, self.sb("exceeds", [P, 2, len(MIDS), CH], BF16) as exceeds, \
                self.sb("step", [P, 2, P], BF16) as step, Phase(nc) as ph:
            s_chain, s_scale, s_sign, s_signed = ph.sem("chain"), ph.sem("scale"), ph.sem("sign"), ph.sem("signed_scale")
            s_abs = ph.sem("magnitude")
            s_step, s_exceeds, s_grid, s_done = ph.sem("step"), ph.sem("exceeds"), ph.sem("grid"), ph.sem("done")
            with nc.Block() as block:
                @block.scalar
                def _(act):
                    for k, a in enumerate(units):
                        n = a.shape[1]
                        if k >= 3:
                            act.wait_ge(s_done, k - 2)
                        act.activation(magnitude[:, k % 3, 0:n, :], a, ACT.Abs).then_inc(s_abs, 1)
                        act.activation(sgn[:, k % 3, 0:n, :], a, ACT.Sign).then_inc(s_sign, 1)

                @block.gpsimd
                def _(pool):
                    for k, a in enumerate(units):
                        n = a.shape[1]
                        pool.wait_ge(s_scale, k + 1)
                        pool.wait_ge(s_sign, k + 1)
                        d = sgn[:, k % 3, 0:n, :]
                        pool.tensor_tensor(d, d, sc[:, k % 3, 0:n].unsqueeze(2).to_broadcast([P, n, 16]), ALU.mult).then_inc(s_signed, 1)

                @block.tensor
                def _(pe):
                    pe.wait_ge(s_step, 2)
                    weight = {0.5: step[:, 0, :], 1.0: self.identb[:, :], 2.0: step[:, 1, :]}
                    for k, a in enumerate(units):
                        w = a.shape[1] * 16
                        if k >= 4:
                            pe.wait_ge(s_done, k - 3)
                        pe.wait_ge(s_exceeds, k + 1)
                        for m, s in enumerate(STEPS):
                            last = pe.matmul(self.bank(k % 4)[:, 0:w], weight[s], exceeds[:, k % 2, m, 0:w],
                                             start=(m == 0), stop=(m == len(MIDS) - 1))
                        last.then_inc(s_grid, 1)

                @block.vector
                def _(dve):
                    chain = [0]
                    for m, value in enumerate((0.5, 2.0)):
                        dve.tensor_scalar(step[:, m, :], self.c["ident"], value, None, ALU.mult).then_inc(s_step, 1)

                    def finish(k):
                        a = units[k]
                        n = a.shape[1]
                        dve.wait_ge(s_grid, k + 1)
                        dve.wait_ge(s_signed, k + 1)
                        dve.tensor_tensor(a, self.bank(k % 4)[:, 0:16 * n].rearrange("p (n s) -> p n s", s=16), sgn[:, k % 3, 0:n, :],
                                          ALU.mult).then_inc(s_done, 1)

                    for k, a in enumerate(units):
                        n = a.shape[1]
                        scale, r, x = sc[:, k % 3, 0:n], inv[:, k % 3, 0:n], scaled[:, k % 2, 0:n, :]
                        if k >= 3:
                            dve.wait_ge(s_signed, k - 2)
                        y = magnitude[:, k % 3, 0:n, :]
                        dve.wait_ge(s_abs, k + 1)
                        link(dve, s_chain, chain, dve.tensor_reduce(scale, y, AX.X, ALU.max))
                        dve.tensor_scalar(scale, scale, 1.0 / 6.0, 1e-12, ALU.mult, ALU.max).then_inc(s_scale, 1)
                        dve.wait_ge(s_scale, k + 1)
                        link(dve, s_chain, chain, dve.reciprocal(r, scale))
                        link(dve, s_chain, chain, dve.tensor_tensor(x, y, r.unsqueeze(2).to_broadcast([P, n, 16]), ALU.mult))
                        if k >= 2:
                            dve.wait_ge(s_grid, k - 1)
                        for m, mid in enumerate(MIDS):
                            last = dve.tensor_scalar(exceeds[:, k % 2, m, 0:16 * n], x.rearrange("p n s -> p (n s)"), mid, None,
                                                     ALU.is_gt)
                        last.then_inc(s_exceeds, 1)
                        if k >= 1:
                            finish(k - 1)
                    finish(len(units) - 1)

    def turn_tiles(self, moves):
        nc = self.nc
        with Phase(nc) as ph:
            s_turn, s_copy = ph.sem("turn"), ph.sem("copy")
            with nc.Block() as block:
                @block.tensor
                def _(pe):
                    for n, (src, dst) in enumerate(moves):
                        r, c = src.shape[0], src.shape[1]
                        if n >= 8:
                            pe.wait_ge(s_copy, n - 7)
                        pe.transpose(self.bank(n % 8)[0:c, 0:r], src, self.c["ident"][0:r, 0:r]).then_inc(s_turn, 1)

                @block.scalar
                def _(act):
                    for n, (src, dst) in enumerate(moves):
                        r, c = src.shape[0], src.shape[1]
                        act.wait_ge(s_turn, n + 1)
                        act.activation(dst, self.bank(n % 8)[0:c, 0:r], ACT.Copy).then_inc(s_copy, 1)

    def L0_ffn(self):
        blocks = lambda a: a.rearrange("p (n s) -> p n s", s=16)
        NK = len(FT0)
        with self.weights("L0_ffn") as w, self.sb("wgT", [P, NF0]) as wgT, self.sb("wuT", [P, NF0]) as wuT, \
                self.sb("wdT", [P, NK, D]) as wdT, self.sb("g", [P, NK, B * S]) as gT, self.sb("h", [P, NT, NF0]) as h:
            self.norm(self.x, self.nrm, None, load=(w,))
            self.quantise([self.nrm[:, :, :].rearrange("p t (n s) -> p (t n) s", s=16), blocks(w.buf[:, :])])
            moves = [(self.nrm[:, t, :], self.xT[:, t * P:(t + 1) * P]) for t in range(NT)]
            for n, dst in (("w_gate", wgT), ("w_up", wuT)):
                moves += [(w[f"{n}{i}"], dst[:, f0:f0 + fn]) for i, (f0, fn) in enumerate(FT0)]
            moves += [(w["w_down"][:, f0:f0 + fn], wdT[0:fn, i, :]) for i, (f0, fn) in enumerate(FT0)]
            self.turn_tiles(moves)
            with self.sb("act", [P, NT, NF0]) as sil:
                jobs = []
                for t in range(NT):
                    xs = self.xT[:, t * P:(t + 1) * P]
                    jobs.append(([(0, NF0, P, xs, wgT[:, :], True, True)],
                                 ("act", ACT.Silu, sil[:, t, :], self.whole(P, NF0), 0.0, 1.0), None))
                    jobs.append(([(0, NF0, P, xs, wuT[:, :], True, True)],
                                 ("dve", "mult", h[:, t, :], self.whole(P, NF0), sil[:, t, :], len(jobs) - 1), None))
                self.products(jobs)
            self.quantise([h[:, :, :].rearrange("p t (n s) -> p (t n) s", s=16)])
            self.turn_tiles([(h[:, t, f0:f0 + fn], gT[0:fn, i, t * P:(t + 1) * P]) for t in range(NT) for i, (f0, fn) in enumerate(FT0)])
            jobs = []
            for g in range(NCH):
                mms = []
                for t in range(4 * g, 4 * g + 4):
                    c = (t - 4 * g) * P
                    for i, (f0, fn) in enumerate(FT0):
                        mms.append((c, c + P, P, gT[0:fn, i, t * P:(t + 1) * P], wdT[0:fn, i, :], i == 0, i == NK - 1))
                d = self.x[:, 4 * g:4 * g + 4, :]
                jobs.append((mms, ("dve", "add", d, (lambda bank: bank[:, :].rearrange("p (t d) -> p t d", d=D)), d), None))
            self.products(jobs)

    def attend_turned(self, Ks, Qx, V, O, clip=None, decay=None, rates=None, distance=None, scale=1.0):
        nc = self.nc
        units = [(b, i, kb) for b in range(B) for i in range(ROWG) for kb in range(HALVES)]
        N = len(units)
        first = lambda kb: kb if clip else 0
        HS = Qx.shape[2]
        R = 8 if clip else 6

        def by_head(a):
            return a.rearrange("p (q j c) -> p j q c", q=2, c=P) if HS == 4 else a.rearrange("p (j q c) -> p j q c", q=2, c=P)

        with self.sb("clipped", [P, 2, 2 * CH]) if clip else nullcontext() as cl, self.sb("probsK", [P, R, 2 * CH]) as pr, \
                self.sb("rsumK", [P, HALVES, H]) as rsum, Phase(nc) as ph:
            oT = self.xT[:, :].rearrange("p (i s) -> p i s", i=ROWG)
            s_scores, s_clip, s_exp, s_mask = ph.sem("scores"), ph.sem("clip"), ph.sem("exp"), ph.sem("mask")
            s_out, s_ot, s_back, s_rec, s_norm = ph.sem("out"), ph.sem("out_copied"), ph.sem("back"), ph.sem("rec"), ph.sem("norm")
            s_ready = s_mask if clip else s_clip
            s_decay = ph.sem("decay")

            def sbank(n):
                return self.bank(2 * (n % 2), 2)

            obanks, rbanks = self.bank(4, 2), self.bank(6, 2)

            with nc.Block() as block:
                if clip:
                    @block.gpsimd
                    def _(pool):
                        for n, (b, i, kb) in enumerate(units):
                            pool.wait_ge(s_exp, n + 1)
                            d = by_head(pr[:, n % R, :])[:, :, kb, :]
                            pool.tensor_tensor(d, d, self.c["causal_one"].unsqueeze(1).to_broadcast([P, 4, P]), ALU.mult).then_inc(s_mask, 1)

                @block.tensor
                def _(pe):
                    def scores(n):
                        b, i, kb = units[n]
                        ks = slice(b * S + kb * P, b * S + (kb + 1) * P)
                        if HS == 4:
                            for q in range(HALVES):
                                if n >= 2:
                                    pe.wait_ge(s_clip, 2 * (n - 2) + q + 1)
                                pe.matmul(sbank(n)[:, q * CH:(q + 1) * CH], Ks[:, i, ks],
                                          Qx[:, i, :, b * S + q * P:b * S + (q + 1) * P], start=True, stop=True).then_inc(s_scores, 1)
                        else:
                            for g in range(2):
                                q0 = first(kb) * P
                                o = sbank(n)[:, g * CH:(g + 1) * CH].rearrange("p (j s) -> p j s", j=2)[:, :, q0:S]
                                if n >= 2:
                                    pe.wait_ge(s_clip, 2 * (n - 2) + g + 1)
                                pe.matmul(o, Ks[:, 2 * i + g, ks], Qx[:, 2 * i + g, :, b * S + q0:(b + 1) * S],
                                          start=True, stop=True).then_inc(s_scores, 1)

                    def out(n, q):
                        b, i, _ = units[n]
                        if i == 0 and b >= 1 and q == 0:
                            pe.wait_ge(s_ot, b)
                        pe.wait_ge(s_ready, (n + 2) * (1 if clip else 2))
                        kbs = [kb for kb in range(HALVES) if first(kb) <= q]
                        for kb in kbs:
                            for j in range(4):
                                last = pe.matmul(obanks[32 * j:32 * j + 32, i * S + q * P:i * S + (q + 1) * P], V[:, 2 * b + kb, 4 * i + j, :],
                                                 by_head(pr[:, (n + kb) % R, :])[:, j, q, :], start=(kb == kbs[0]), stop=(kb == kbs[-1]))
                        if q == HALVES - 1:
                            last.then_inc(s_out, 1)

                    def back(b):
                        pe.wait_ge(s_ot, b + 1)
                        if b >= 1:
                            pe.wait_ge(s_norm, b)
                        for q in range(HALVES):
                            for i in range(ROWG):
                                last = pe.transpose(rbanks[:, q * CH + i * P:q * CH + (i + 1) * P], oT[:, i, q * P:(q + 1) * P], self.c["ident"])
                        last.then_inc(s_back, 1)

                    for n in range(N + 7):
                        if n < N:
                            scores(n)
                        if 5 <= n < N + 5:
                            out(n - 5 - (n + 1) % 2, (n + 1) % 2)
                        if n % 8 == 6 and n > 8:
                            back(n // 8 - 1)

                @block.scalar
                def _(act):
                    if not clip:
                        for h in range(H):
                            act.activation(decay[:, h, :, :], distance, ACT.Exp, scale=rates[:, h:h + 1]).then_inc(s_decay, 1)
                    for n in range(N + 6):
                        if n < N and clip:
                            b, i, kb = units[n]
                            act.wait_ge(s_clip, 2 * (n + 1))
                            if n >= R:
                                act.wait_ge(s_out, (n - R) // 2 + 1)
                            f = first(kb)
                            act.activation(by_head(pr[:, n % R, :])[:, :, f:HALVES, :], by_head(cl[:, n % 2, :])[:, :, f:HALVES, :], ACT.Exp, scale=scale).then_inc(s_exp, 1)
                        if n % 8 == 5 and n > 8:
                            b = n // 8 - 1
                            act.wait_ge(s_out, ROWG * (b + 1))
                            if b >= 1:
                                act.wait_ge(s_back, b)
                            act.activation(oT[:, :, :], obanks, ACT.Copy).then_inc(s_ot, 1)

                @block.vector
                def _(dve):
                    def take(b):
                        dve.wait_ge(s_back, b + 1)
                        dst = O[:, 2 * b:2 * b + 2, :].rearrange("p q (h d) -> p (q h) d", d=HD)
                        rows = rbanks.rearrange("p (h d) -> p h d", d=VW)
                        if clip:
                            dve.reciprocal(rsum[:, :, :], rows[:, :, HD]).then_inc(s_rec, 1)
                            dve.wait_ge(s_rec, b + 1)
                            last = dve.tensor_tensor(dst, rows[:, :, 0:HD], rsum[:, :, :].rearrange("p q h -> p (q h)").unsqueeze(2).to_broadcast([P, 2 * H, HD]), ALU.mult)
                        else:
                            last = dve.tensor_scalar(dst, rows[:, :, 0:HD], scale, None, ALU.mult)
                        last.then_inc(s_norm, 1)
                    for n in range(N + 7):
                        if n < N:
                            b, i, kb = units[n]
                            f = first(kb)
                            if clip and n >= 2:
                                dve.wait_ge(s_exp, n - 1)
                            if not clip and b == 0:
                                dve.wait_ge(s_decay, 4 * (i + 1))
                            if not clip and n >= R:
                                dve.wait_ge(s_out, (n - R) // 2 + 1)
                            for g in range(2):
                                bank = slice(g * CH, (g + 1) * CH)
                                dve.wait_ge(s_scores, 2 * n + g + 1)
                                if clip:
                                    v = lambda a: a.rearrange("p (j q c) -> p j q c", q=2, c=P)[:, :, f:HALVES, :]
                                    dve.tensor_scalar(v(cl[:, n % 2, bank]), v(sbank(n)[:, bank]), -clip, clip, ALU.max, ALU.min).then_inc(s_clip, 1)
                                else:
                                    v = lambda a: a.rearrange("p (j c) -> p j c", c=P)
                                    dve.tensor_tensor(v(pr[:, n % R, bank]), v(sbank(n)[:, bank]),
                                                      decay[:, 4 * i:4 * i + 4, kb, g * P:(g + 1) * P], ALU.mult).then_inc(s_clip, 1)
                        if n % 8 == 6 and n > 8:
                            take(n // 8 - 1)

    def L1_attn(self):
        c = self.c
        with self.weights("L1_attn") as w, self.sb("Qx", [LR, 2 * ROWG, 2, B * S], F32R) as Qx, \
                self.sb("Ks", [LR, 2 * ROWG, B * S], F32R) as Ks, self.sb("V32", [P, NT, H, VW]) as V:
            self.norm(self.x, self.nrm, self.xT, load=(w,))
            with self.sb("QT", [LR, LT, B * S]) as QT, self.sb("KT", [LR, LT, B * S]) as KT:
                with self.sb("raw", [LR, 2, LT, B * S]) as raw, self.sb("w_q", [P, H * LW]) as wq, \
                        self.sb("w_k", [P, H * LW]) as wk, self.sb("w_v", [P, D]) as wv:
                    self.products([
                        ([(0, H * LW, P, w["W_DQT"], w["W_Q"], True, True)], ("act", ACT.Identity, wq[:, :], self.whole(P, H * LW), 0.0, 1.0), None),
                        ([(0, H * LW, P, w["W_DKVT"], w["W_KC"], True, True)], ("dve", "add", wk[:, :], self.whole(P, H * LW), w["W_KR"]), None),
                        ([(0, D, P, w["W_DKVT"], w["W_UV"], True, True)], ("act", ACT.Identity, wv[:, :], self.whole(P, D), 0.0, 1.0), None)])
                    jobs = []
                    for t in range(LT):
                        ws = slice(t * LR, (t + 1) * LR)
                        for dst, weight, k in ((QT, wq, 0), (KT, wk, 1)):
                            self.roped(jobs, [(weight[:, ws], self.xT)], dst[:, t, :], raw[:, k, t, :], c["rot_inter"],
                                       self.tables["cos12"], self.tables["sin12"], m=LR)
                    jobs += self.value_rows(wv[:, :], self.xT, V)
                    self.products(jobs)
                self.stack_operands((KT, Ks), (QT, Qx), c["mask12"], V, m=LR, heads=2)
            with self.sb("O", [P, NT, D]) as O:
                self.attend_turned(Ks, Qx, V, O, clip=80.0, scale=1.0 / math.sqrt(12.0))
                self.project(O, w["W_O"], None, self.x)

    def self_attention(self, src, w, dst, rot, weight=None, rms=False, norm=True, biases=False, load=()):
        c = self.c
        if norm:
            self.norm(src, self.nrm, self.xT, layer=not rms, eps=1e-6 if rms else 1e-5, weight=weight, load=load)
        with self.sb("Qs", [P, ROWG, B * S], F32R) as Qs, self.sb("Kx", [P, ROWG, 4, B * S], F32R) as Kx, \
                self.sb("V32", [P, NT, H, VW]) as V, self.sb("O", [P, NT, D]) as O:
            with self.sb("QT", [P, B * S]) as QT, self.sb("KT", [P, B * S]) as KT, self.sb("raw", [P, 2, B * S]) as raw:
                jobs = []
                bq, bk, bv, bo = (w["bq"], w["bk"], w["bv"], w["bo"]) if biases else (0.0, 0.0, None, None)
                self.roped(jobs, [(w["Wq"], self.xT)], QT, raw[:, 0, :], rot, self.tables["cos8q"], self.tables["sin8q"], bias=bq)
                self.roped(jobs, [(w["Wk"], self.xT)], KT, raw[:, 1, :], rot, self.tables["cos8"], self.tables["sin8"], bias=bk)
                jobs += self.value_rows(w["Wv"], self.xT, V, bias=bv)
                self.products(jobs)
                one = lambda a: a.unsqueeze(1)
                self.stack_operands((one(QT[:, :]), Qs), (one(KT[:, :]), Kx), c["mask8"], V)
            self.attend(Qs, Kx, V, O)
            self.project(O, w["Wo"], bo, dst)

    def L1_xattn(self):
        nc = self.nc
        awhere, awidth = self.where["inner_attn"]
        fwhere, fwidth = self.where["inner_ffn"]
        with self.sb("y", [P, NT, D]) as y, self.sb("w_attn", [P, awidth]) as wa, self.sb("w_ffn", [P, fwidth]) as wf, \
                self.weights("inner_misc") as wm, self.sb("allow", [P, NT, SC], BF16) as allow, self.sb("seg", [P, NT], I32) as seg:
            first = Pack(wa, awhere, self.dram["inner_attn"][0, :, :])
            self.norm(self.x, y, None, load=(wm, first))
            with self.sb("segf", [P, NT]) as segf, self.sb("one", [P, NT, SC]) as one, self.sb("low", [P, NT]) as low, \
                    self.sb("two", [P, NT, SC]) as two, Phase(nc) as ph:
                s_load, s_chain = ph.sem("load"), ph.sem("chain")
                with nc.Block() as block:
                    @block.sync
                    def _(sp):
                        sp.dma_start(seg[:, :], self.seg_dram[:, :]).then_inc(s_load, 16)
                        sp.wait_ge(s_load, 16)

                    @block.vector
                    def _(dve):
                        n = [0]
                        keys = wm["keys"].unsqueeze(1).to_broadcast([P, NT, SC])
                        wide = lambda v: v[:, :].unsqueeze(2).to_broadcast([P, NT, SC])
                        dve.wait_ge(s_load, 16)
                        link(dve, s_chain, n, dve.tensor_copy(segf[:, :], seg[:, :]))
                        link(dve, s_chain, n, dve.tensor_scalar(low[:, :], segf[:, :], -128.0, None, ALU.add))
                        link(dve, s_chain, n, dve.tensor_tensor(one[:, :, :], keys, wide(segf), ALU.is_le))
                        link(dve, s_chain, n, dve.tensor_tensor(two[:, :, :], keys, wide(low), ALU.is_gt))
                        link(dve, s_chain, n, dve.tensor_tensor(one[:, :, :], one[:, :, :], two[:, :, :], ALU.mult))
                        link(dve, s_chain, n, dve.tensor_scalar(allow[:, :, :], one[:, :, :], -1.0, -NEG, ALU.add, ALU.mult))
            w, wff = Pack(wa, awhere), Pack(wf, fwhere)
            of_layer = lambda name, n: self.dram[name][bass.ds(n, 1), :, :].rearrange("o p n -> (o p) n")
            with nc.Fori(0, LAYERS) as layer, self.last_of_body():
                wff.source = of_layer("inner_ffn", layer)
                self.self_attention(y, w, y, wm["rot_half"], weight=w["n1"], rms=True, biases=True, load=(wff,))
                self.norm(y, self.nrm, self.xT, layer=False, eps=1e-6, weight=w["n2"])
                with self.sb("QT", [P, B * S]) as QT, self.sb("KT", [P, B * SC]) as KT, \
                        self.sb("Kx", [P, H, B * SC]) as Kx, self.sb("O", [P, NT, D]) as O:
                    jobs = self.turned(w["Wq_c"], self.xT, QT, scale=HD ** -0.5)
                    self.context_keys_values(jobs, w["Wk_c"], w["Wv_c"], KT)
                    self.products(jobs)
                    self.attend_context(self.head_scores(QT, Kx), self.V2, O, bias=allow, per_token=True, keys=(KT, Kx))
                    self.project(O, w["Wo_c"], None, y)
                w.source = of_layer("inner_attn", layer + 1)
                self.norm(y, self.nrm, self.xT, layer=False, eps=1e-6, weight=wff["n3"], load=(w,))
                with self.sb("hT", [P, FK, B * S]) as hT:
                    jobs = []
                    for n, (f, ch) in enumerate((f, ch) for f in range(FK) for ch in range(NCH)):
                        cols = slice(ch * CH, (ch + 1) * CH)
                        fs = slice(f * P, (f + 1) * P)
                        jobs.append(([(0, CH, P, wff["Wg"][:, fs], self.xT[:, cols], True, True)],
                                     ("act", ACT.Silu, hT[:, f, cols], self.whole(), 0.0, 1.0), None))
                        jobs.append(([(0, CH, P, wff["Wu"][:, fs], self.xT[:, cols], True, True)],
                                     ("dve", "mult", hT[:, f, cols], self.whole(), hT[:, f, cols], len(jobs) - 1), None))
                    self.rows_added(jobs, hT, wff["Wd"], None, y, k=FK, after=[len(jobs) - 3, len(jobs) - 1])
                    self.products(jobs)
            self.norm(y, self.nrm, None, layer=False, eps=1e-6)
            with Phase(nc) as ph:
                s_chain = ph.sem("chain")
                with nc.Block() as block:
                    @block.vector
                    def _(dve):
                        n = [0]
                        nf = wm["nf"].unsqueeze(1).to_broadcast([P, NT, D])
                        link(dve, s_chain, n, dve.tensor_tensor(self.nrm[:, :, :], self.nrm[:, :, :], nf, ALU.mult))
                        link(dve, s_chain, n, dve.tensor_tensor(self.x[:, :, :], self.x[:, :, :], self.nrm[:, :, :], ALU.add))

    def route(self, w, top, gate, bias=True, clear=(), split=()):
        nc = self.nc
        eps = {"L1": float(np.finfo(np.float32).eps)}
        with self.sb("logits", [P, NT, E]) as lg, self.sb("best", [P, NT, 8]) as best, self.sb("which", [P, NT, 8], U32) as which, \
                self.sb("whichf", [P, NT, 8]) as wh, self.sb("ex", [P, NT, E]) as ex, self.sb("hot", [P, NT, E]) as hot, \
                self.sb("hot2", [P, NT, E]) as hot2, self.sb("total", [P, NT]) as total, self.sb("z", [P, NT]) as z, Phase(nc) as ph:
            s_logits, s_chain, s_sub, s_exp = ph.sem("logits"), ph.sem("chain"), ph.sem("sub"), ph.sem("exp")
            s_clear, s_high, s_low = ph.sem("clear"), ph.sem("high"), ph.sem("low")
            with nc.Block() as block:
                @block.gpsimd
                def _(pool):
                    for buf in clear:
                        pool.memset(buf, 0.0).then_inc(s_clear, 1)
                    for n, (src, h, l) in enumerate(split):
                        pool.wait_ge(s_high, n + 1)
                        pool.tensor_tensor(l, src, h.bitcast(F32), ALU.subtract).then_inc(s_low, 1)

                @block.tensor
                def _(pe):
                    for t in range(NT):
                        o = self.ps[:, t * E:(t + 1) * E]
                        last = pe.matmul(o, self.xT[:, t * P:(t + 1) * P], w["Wr"], start=True, stop=not bias)
                        if bias:
                            last = pe.matmul(o, self.c["ones_row"], w["br"], start=False, stop=True)
                    last.then_inc(s_logits, 1)

                @block.scalar
                def _(act):
                    for src, h, l in split:
                        act.activation(h, src, ACT.Copy).then_inc(s_high, 1)
                    act.wait_ge(s_sub, 1)
                    act.activation(ex[:, :, :], ex[:, :, :], ACT.Exp).then_inc(s_exp, 1)

                @block.vector
                def _(dve):
                    n = [0]
                    wide = lambda v: v.to_broadcast([P, NT, E])
                    iota = self.c["iota8"].unsqueeze(1).to_broadcast([P, NT, E])
                    dve.wait_ge(s_logits, 1)
                    link(dve, s_chain, n, dve.tensor_copy(lg[:, :, :], self.ps[:, 0:NT * E]))
                    for t in range(NT):
                        link(dve, s_chain, n, dve.max(best[:, t, :], lg[:, t, :]))
                    dve.tensor_tensor(ex[:, :, :], lg[:, :, :], wide(best[:, :, 0:1]), ALU.subtract).then_inc(s_sub, 1)
                    for t in range(NT):
                        link(dve, s_chain, n, dve.max_index(which[:, t, :], best[:, t, :], lg[:, t, :]))
                    link(dve, s_chain, n, dve.tensor_copy(wh[:, :, :], which[:, :, :]))
                    link(dve, s_chain, n, dve.tensor_tensor(hot[:, :, :], iota, wide(wh[:, :, 0:1]), ALU.is_equal))
                    if top == 2:
                        link(dve, s_chain, n, dve.tensor_tensor(hot2[:, :, :], iota, wide(wh[:, :, 1:2]), ALU.is_equal))
                        link(dve, s_chain, n, dve.tensor_tensor(hot[:, :, :], hot[:, :, :], hot2[:, :, :], ALU.add))
                    dve.wait_ge(s_exp, 1)
                    link(dve, s_chain, n, dve.tensor_reduce(total[:, :], ex[:, :, :], AX.X, ALU.add))
                    link(dve, s_chain, n, dve.reciprocal(z[:, :], total[:, :]))
                    link(dve, s_chain, n, dve.tensor_tensor(ex[:, :, :], ex[:, :, :], wide(z[:, :].unsqueeze(2)), ALU.mult))
                    link(dve, s_chain, n, dve.tensor_tensor(gate[:, :, :], ex[:, :, :], hot[:, :, :], ALU.mult))
                    if top == 2:
                        link(dve, s_chain, n, dve.tensor_reduce(total[:, :], gate[:, :, :], AX.X, ALU.add))
                        if not bias:
                            link(dve, s_chain, n, dve.tensor_scalar(total[:, :], total[:, :], eps["L1"], None, ALU.add))
                        link(dve, s_chain, n, dve.reciprocal(z[:, :], total[:, :]))
                        link(dve, s_chain, n, dve.tensor_tensor(gate[:, :, :], gate[:, :, :], wide(z[:, :].unsqueeze(2)), ALU.mult))

    def experts(self, stage, slots, gate, gated, buffers, b2=None):
        nc = self.nc
        where, width = self.where[stage]
        U = FK * NCH
        N = 2 * U
        PIECES = [slice(c, min(c + CH, width)) for c in range(0, width, CH)]
        K = len(PIECES)
        whole = B * S
        wh0, wh1, wl0, wl1, xh, xl, gw, yT = buffers
        with self.sb("gates", [P, E, whole]) as gates:
            wbuf, wh, wl = (slots[0].buf, slots[1].buf), (wh0, wh1), (wl0, wl1)
            high, low = (Pack(wh0, where), Pack(wh1, where)), (Pack(wl0, where), Pack(wl1, where))
            with self.sb("gate_parts", [P, whole], F32R) as gp, \
                    self.sb("expert_rows", [P, E, P], F32R) as er, Phase(nc) as ph:
                s_wide = ph.sem("gate_wide")
                s_turn, s_gh, s_gl, s_er = ph.sem("turn"), ph.sem("gate_high"), ph.sem("gate_low"), ph.sem("expert_row")
                s_bias, s_y = ph.sem("bias"), ph.sem("outputs_started")
                s_spread, s_taken = ph.sem("spread"), {"act": ph.sem("taken_act"), "dve": ph.sem("taken_dve")}
                engines = ("act", "dve")
                chunks = [slice(c * CH, (c + 1) * CH) for c in range(NCH)]
                with nc.Block() as block:
                    @block.tensor
                    def _(pe):
                        pe.wait_ge(s_wide, 2)
                        for g in range(NCH):
                            for t in range(4 * g, 4 * g + 4):
                                last = pe.transpose(self.bank(g)[:, (t - 4 * g) * P:(t - 4 * g + 1) * P], gw[:, t, :], self.c["ident"])
                            last.then_inc(s_turn, 1)
                        pe.wait_ge(s_er, 1)
                        pe.wait_ge(s_gl, NCH)
                        if b2 is not None:
                            for g in range(NCH):
                                last = pe.matmul(self.bank(g), b2, gp[0:LOW + E, chunks[g]].bitcast(F32), start=True, stop=True)
                            last.then_inc(s_bias, 1)
                        for n in range(E * NCH):
                            e, c = n // NCH, n % NCH
                            if n >= 6:
                                pe.wait_ge(s_taken[engines[n % 2]], (n - 6) // 2 + 1)
                            pe.matmul(self.bank(2 + n % 6), er[:, e, :], gp[:, chunks[c]], start=True, stop=True).then_inc(s_spread, 1)

                    @block.scalar
                    def _(act):
                        for g in range(NCH):
                            act.wait_ge(s_turn, g + 1)
                            act.activation(gp[:, chunks[g]], self.bank(g), ACT.Copy).then_inc(s_gh, 1)
                        for n in range(0, E * NCH, 2):
                            act.wait_ge(s_spread, n + 1)
                            act.activation(gates[:, n // NCH, chunks[n % NCH]], self.bank(2 + n % 6), ACT.Copy).then_inc(s_taken["act"], 1)

                    @block.vector
                    def _(dve):
                        for at in (0, LOW):
                            dve.tensor_copy(gw[:, :, at:at + E], gate[:, :, :]).then_inc(s_wide, 1)
                        column = lambda at: self.c["ident"][:, at:at + E].unsqueeze(2).to_broadcast([P, E, P])
                        dve.tensor_tensor(er[:, :, :], column(0), column(LOW), ALU.add).then_inc(s_er, 1)
                        low_rows = slice(LOW, LOW + E)
                        for g in range(NCH):
                            dve.wait_ge(s_gh, g + 1)
                            dve.tensor_tensor(gp[low_rows, chunks[g]], self.bank(g)[low_rows, :], gp[low_rows, chunks[g]].bitcast(F32),
                                              ALU.subtract).then_inc(s_gl, 1)
                        if b2 is not None:
                            dve.wait_ge(s_bias, 1)
                            dve.tensor_copy(yT[:, :], self.bank(0, NCH)).then_inc(s_y, 1)
                        for n in range(1, E * NCH, 2):
                            dve.wait_ge(s_spread, n + 1)
                            dve.tensor_copy(gates[:, n // NCH, chunks[n % NCH]], self.bank(2 + n % 6)).then_inc(s_taken["dve"], 1)

            with self.sb("activated", [P, 4, CH]) as ac, self.sb("hidden", [P, 4, CH]) as hid, \
                    self.sb("hidden_high", [P, 4, CH], F32R) as hh, self.sb("hidden_low", [P, 4, CH], F32R) as hl, \
                    nc.Fori(0, E // 2) as pair, self.last_of_body(), Phase(nc) as ph:
                expert = pair * 2
                s_slot1, s_slot0 = ph.sem("slot1_loaded"), ph.sem("slot0_loaded")
                s_wh, s_wl = ph.sem("weights_high"), ph.sem("weights_low")
                s_up, s_act, s_up_gated, s_hid = ph.sem("up"), ph.sem("activated"), ph.sem("up_gated"), ph.sem("hidden")
                s_high, s_low, s_down, s_added = ph.sem("hidden_high"), ph.sem("hidden_low"), ph.sem("down"), ph.sem("added")
                R = 6
                per = 2 if gated else 1
                unit = lambda n: (n // U, (n % U) // NCH, n % NCH)
                cols = lambda ch: slice(ch * CH, (ch + 1) * CH)
                with nc.Block() as block:
                    @block.sync
                    def _(sp):
                        sp.dma_start(wbuf[1][:, :], self.dram[stage][bass.ds(expert + 1, 1), :, :].rearrange("o p n -> (o p) n")).then_inc(s_slot1, 16)
                        sp.wait_ge(s_act, U)
                        sp.dma_start(wbuf[0][:, :], self.dram[stage][bass.ds(expert + 2, 1), :, :].rearrange("o p n -> (o p) n")).then_inc(s_slot0, 16)
                        sp.wait_ge(s_slot0, 16)
                        sp.wait_ge(s_slot1, 16)

                    @block.tensor
                    def _(pe):
                        def product(o, w, name, c, h, l, start, stop):
                            pe.matmul(o, high[w][name][:, c], h, start=start, stop=False)
                            pe.matmul(o, high[w][name][:, c], l, start=False, stop=False)
                            return pe.matmul(o, low[w][name][:, c], h, start=False, stop=stop)

                        def up(n):
                            x, f, ch = unit(n)
                            if n == U:
                                pe.wait_ge(s_wl, K)
                            for m, name in enumerate(("Wg", "Wu") if gated else ("W1",)):
                                k = n * per + m
                                if k >= R:
                                    pe.wait_ge(s_act, (k - R) // per + 1)
                                    if gated:
                                        pe.wait_ge(s_up_gated, (k - R) // per + 1)
                                product(self.bank(k % R), x, name, slice(f * P, (f + 1) * P), xh[:, cols(ch)], xl[:, cols(ch)],
                                        True, True).then_inc(s_up, 1)

                        def down(n):
                            x, f, ch = unit(n)
                            pe.wait_ge(s_low, n + 1)
                            last = product(self.bank(R + ch), x, "Wd" if gated else "W2", slice(f * D, (f + 1) * D),
                                           hh[:, n % 4, :], hl[:, n % 4, :], n < NCH, n >= N - NCH)
                            last.then_inc(s_down, 1)

                        for n in range(N + 3):
                            if n < N:
                                up(n)
                            if n >= 3:
                                down(n - 3)

                    @block.scalar
                    def _(act):
                        def split(x, p):
                            act.wait_ge(s_slot1 if x else s_slot0, 16)
                            if x == 0:
                                act.wait_ge(s_down, U)
                            act.activation(wh[x][:, PIECES[p]], wbuf[x][:, PIECES[p]], ACT.Copy).then_inc(s_wh, 1)

                        for n in range(N + 1):
                            if n < N:
                                x, f, ch = unit(n)
                                act.wait_ge(s_up, n * per + 1)
                                if n == U:
                                    act.wait_ge(s_slot1, 16)
                                if n >= 4:
                                    act.wait_ge(s_hid, n - 3)
                                if gated:
                                    act.activation(ac[:, n % 4, :], self.bank((n * per) % R), ACT.Relu).then_inc(s_act, 1)
                                else:
                                    act.activation(ac[:, n % 4, :], self.bank(n % R), ACT.Gelu, bias=slots[x]["b1"][:, f:f + 1]).then_inc(s_act, 1)
                            if n >= 1:
                                m = n - 1
                                act.wait_ge(s_hid, m + 1)
                                if m >= 4:
                                    act.wait_ge(s_down, m - 3)
                                act.activation(hh[:, m % 4, :], hid[:, m % 4, :], ACT.Copy).then_inc(s_high, 1)
                            if 3 <= n < 3 + K:
                                split(1, n - 3)
                            if N - K < n <= N:
                                split(0, n - (N - K) - 1)

                    @block.gpsimd
                    def _(pool):
                        for k in range(2 * K):
                            x, p = 1 - k // K, k % K
                            pool.wait_ge(s_wh, k + 1)
                            pool.tensor_tensor(wl[x][:, PIECES[p]], wbuf[x][:, PIECES[p]], wh[x][:, PIECES[p]].bitcast(F32), ALU.subtract).then_inc(s_wl, 1)

                    @block.vector
                    def _(dve):
                        for n in range(N + 1):
                            if n < N:
                                x, f, ch = unit(n)
                                g = gates[:, bass.ds(expert + x, 1), cols(ch)].rearrange("p o c -> p (o c)")
                                h = hid[:, n % 4, :]
                                if n >= 4:
                                    dve.wait_ge(s_high, n - 3)
                                if gated:
                                    dve.wait_ge(s_up, 2 * n + 2)
                                    dve.tensor_tensor(h, self.bank((2 * n + 1) % R), g, ALU.mult).then_inc(s_up_gated, 1)
                                    dve.wait_ge(s_up_gated, n + 1)
                                    dve.wait_ge(s_act, n + 1)
                                    dve.tensor_tensor(h, h, ac[:, n % 4, :], ALU.mult).then_inc(s_hid, 1)
                                else:
                                    dve.wait_ge(s_act, n + 1)
                                    dve.tensor_tensor(h, ac[:, n % 4, :], g, ALU.mult).then_inc(s_hid, 1)
                            if n >= 1:
                                m = n - 1
                                dve.wait_ge(s_high, m + 1)
                                if m >= 4:
                                    dve.wait_ge(s_down, m - 3)
                                dve.tensor_tensor(hl[:, m % 4, :], hid[:, m % 4, :], hh[:, m % 4, :].bitcast(F32), ALU.subtract).then_inc(s_low, 1)
                        for ch in range(NCH):
                            dve.wait_ge(s_down, N - NCH + ch + 1)
                            dve.tensor_tensor(yT[:, cols(ch)], self.bank(R + ch), yT[:, cols(ch)], ALU.add).then_inc(s_added, 1)

            with Phase(nc) as ph:
                s_turn, s_sum = ph.sem("turn"), ph.sem("sum")
                with nc.Block() as block:
                    @block.tensor
                    def _(pe):
                        for g in range(NCH):
                            for t in range(4 * g, 4 * g + 4):
                                last = pe.transpose(self.bank(g)[:, (t - 4 * g) * P:(t - 4 * g + 1) * P], yT[:, t * P:(t + 1) * P], self.c["ident"])
                            last.then_inc(s_turn, 1)

                    @block.vector
                    def _(dve):
                        for g in range(NCH):
                            ts = slice(4 * g, 4 * g + 4)
                            dve.wait_ge(s_turn, g + 1)
                            dve.tensor_tensor(self.x[:, ts, :], self.bank(g).rearrange("p (t d) -> p t d", d=D), self.x[:, ts, :], ALU.add).then_inc(s_sum, 1)

    def moe(self, layer, top):
        gated = layer == "L1"
        stage = layer + "_experts"
        where, width = self.where[stage]
        with self.weights(layer + "_ffn") as w, self.sb("gate", [P, NT, E]) as gate, \
                self.sb("slot0", [P, width]) as w0, self.sb("slot1", [P, width]) as w1, \
                self.sb("high0", [P, width], F32R) as wh0, self.sb("high1", [P, width], F32R) as wh1, \
                self.sb("low0", [P, width], F32R) as wl0, self.sb("low1", [P, width], F32R) as wl1, \
                self.sb("x_high", [P, B * S], F32R) as xh, self.sb("x_low", [P, B * S], F32R) as xl, \
                self.sb("gate_wide", [P, NT, P]) as gw, self.sb("yT", [P, B * S]) as yT:
            slots = (Pack(w0, where, self.dram[stage][0, :, :]), Pack(w1, where))
            self.norm(self.x, self.nrm, self.xT, load=(w, slots[0]))
            pieces = lambda n: [slice(c, min(c + CH, n)) for c in range(0, n, CH)]
            self.route(w, top, gate, bias=not gated, clear=(gw[:, :, :], yT[:, :]) if gated else (gw[:, :, :],),
                       split=[(self.xT[:, c], xh[:, c], xl[:, c]) for c in pieces(B * S)]
                       + [(w0[:, c], wh0[:, c], wl0[:, c]) for c in pieces(width)])
            self.experts(stage, slots, gate, gated, (wh0, wh1, wl0, wl1, xh, xl, gw, yT),
                         None if gated else w["b2"])

    def L1_ffn(self):
        self.moe("L1", 2)

    def L2_ffn(self):
        self.moe("L2", 1)

    def L3_ffn(self):
        self.moe("L3", 2)

    def L2_attn(self):
        with self.weights("L2_attn") as w:
            self.self_attention(self.x, w, self.x, self.c["rot_inter"], load=(w,))

    def L2_xattn(self):
        nc = self.nc
        with self.weights("L2_xattn") as w, self.sb("QT", [P, 2, B * S]) as QT, self.sb("KT", [P, 2, B * SC]) as KT, \
                self.sb("Kx", [P, 2, H, B * SC]) as Kx, \
                self.sb("O", [P, NT, D]) as O, self.sb("lam", [P, H]) as lam:
            self.norm(self.x, self.nrm, self.xT, load=(w,))
            jobs = self.turned(w["q1"], self.xT, QT[:, 0, :], scale=HD ** -0.5) + self.turned(w["q2"], self.xT, QT[:, 1, :], scale=HD ** -0.5)
            self.context_keys_values(jobs, w["k1"], w["v1"], KT[:, 0, :])
            jobs += self.turned(w["k2"], self.ctx["ctxT"], KT[:, 1, :], width=B * SC)
            self.products(jobs)
            with Phase(nc) as ph:
                s_chain = ph.sem("chain")
                with nc.Block() as block:
                    @block.vector
                    def _(dve):
                        n = [0]
                        link(dve, s_chain, n, dve.tensor_tensor(lam[:, :], w["l1"], w["l2"], ALU.subtract))
                        link(dve, s_chain, n, dve.tensor_scalar(lam[:, :], lam[:, :], 0.1, None, ALU.add))
            self.attend_context(self.head_scores(QT[:, 0, :], Kx[:, 0, :, :]), self.V2, O, keys=(KT[:, 0, :], Kx[:, 0, :, :]))
            self.attend_context(self.head_scores(QT[:, 1, :], Kx[:, 1, :, :]), self.V2, O, combine=lam[:, :],
                                keys=(KT[:, 1, :], Kx[:, 1, :, :]))
            self.norm(O, self.nrm, None, layer=False, eps=1e-6)
            self.project(self.nrm, w["proj"], w["b"], self.x, scale=w["norm"])

    def L3_attn(self):
        nc = self.nc
        c = self.c
        with self.weights("L3_attn") as w, self.sb("Qx", [P, ROWG, 4, B * S], F32R) as Qx, self.sb("Ks", [P, ROWG, B * S], F32R) as Ks, \
                self.sb("V32", [P, NT, H, VW]) as V, self.sb("O", [P, NT, D]) as O, self.sb("sg", [P, H]) as sg:
            self.norm(self.x, self.nrm, self.xT, load=(w,))
            gate = self.nrm
            with self.sb("QT", [P, 1, B * S]) as QT, self.sb("KT", [P, 1, B * S]) as KT, self.sb("raw", [P, 2, B * S]) as raw:
                jobs = []
                self.roped(jobs, [(w["Wq"], self.xT)], QT[:, 0, :], raw[:, 0, :], c["rot_inter"], self.tables["cos8"], self.tables["sin8"], bias=w["bq"])
                self.roped(jobs, [(w["Wk"], self.xT)], KT[:, 0, :], raw[:, 1, :], c["rot_inter"], self.tables["cos8"], self.tables["sin8"], bias=w["bk"])
                jobs += self.value_rows(w["Wv"], self.xT, V, bias=w["bv"])
                for g in range(NCH):
                    mms = []
                    for t in range(4 * g, 4 * g + 4):
                        k = (t - 4 * g) * P
                        mms.append((k, k + P, P, self.xT[:, t * P:(t + 1) * P], w["Wg"], True, False))
                        mms.append((k, k + P, P, c["ones_row"], w["bg"], False, True))
                    jobs.append((mms, ("act", ACT.Silu, gate[:, 4 * g:4 * g + 4, :], self.whole(), 0.0, 1.0), None))
                self.products(jobs)
                self.stack_operands((KT, Ks), (QT, Qx), c["mask8"], V)
            with self.sb("decay", [P, H, HALVES, S]) as decay:
                with Phase(nc) as ph:
                    s_sig, s_neg = ph.sem("sigmoid"), ph.sem("negated")
                    with nc.Block() as block:
                        @block.scalar
                        def _(act):
                            act.activation(sg[:, :], w["gamma"], ACT.Sigmoid).then_inc(s_sig, 1)

                        @block.vector
                        def _(dve):
                            dve.wait_ge(s_sig, 1)
                            dve.tensor_scalar(sg[:, :], sg[:, :], -1.0, None, ALU.mult).then_inc(s_neg, 1)
                self.attend_turned(Ks, Qx, V, O, decay=decay, rates=sg, distance=w["distance"], scale=1.0 / math.sqrt(HD))
                with Phase(nc) as ph:
                    s_chain = ph.sem("chain")
                    with nc.Block() as block:
                        @block.vector
                        def _(dve):
                            n = [0]
                            link(dve, s_chain, n, dve.tensor_tensor(O[:, :, :], O[:, :, :], gate[:, :, :], ALU.mult))
                            link(dve, s_chain, n, dve.tensor_tensor(self.x[:, :, :], self.x[:, :, :], O[:, :, :], ALU.add))

    def L3_xattn(self):
        nc = self.nc
        QK = H * DK3 // P
        with self.weights("L3_xattn") as w, self.sb("QT", [P, QK, B * S]) as QT, \
                self.sb("K2", [P, QK, B, 2, SC]) as K2, self.sb("V2w", [P, B, QK, 2, DK3]) as V2:
            self.norm(self.x, self.nrm, self.xT, load=(w,))
            with Phase(nc) as ph:
                s_k, s_v = ph.sem("keys_zeroed"), ph.sem("values_zeroed")
                with nc.Block() as block:
                    @block.gpsimd
                    def _(pool):
                        pool.memset(V2[:, :, :, :, :], 0.0).then_inc(s_v, 1)

                    @block.vector
                    def _(dve):
                        dve.memset(K2[:, :, :, :, :], 0.0).then_inc(s_k, 1)
            half = lambda a: slice(DK3 * a, DK3 * (a + 1))
            jobs = []
            for k in range(QK):
                jobs.append(([(0, B * SC, P, w["Wk"][:, k * P:(k + 1) * P], self.ctx["ctxT"], True, True)],
                             ("dve", "diagonal", (lambda a, k=k: K2[half(a), k, :, a, :]),
                              (lambda bank, a: bank[half(a), 0:B * SC].rearrange("p (b s) -> p b s", b=B))), None))
                jobs += self.turned(w["Wq"][:, k * P:(k + 1) * P], self.xT, QT[:, k, :])
            for b in range(B):
                for m in range(2):
                    jobs.append(([(0, CH, P, self.ctx["ctxT2"][:, b * P:(b + 1) * P], w["Wv"][:, m * CH:(m + 1) * CH], True, True)],
                                 ("dve", "diagonal", (lambda a, b=b, m=m: V2[half(a), b, 4 * m:4 * m + 4, a, :]),
                                  (lambda bank, a: bank[half(a), :].rearrange("p (k a d) -> p k a d", a=2, d=DK3)[:, :, a, :])), None))
            self.products(jobs)

            def score(pe, t, banks, first):
                for k in range(QK):
                    last = pe.matmul(banks[:, k * P:(k + 1) * P], QT[:, k, t * P:(t + 1) * P],
                                     K2[:, k, t // HALVES, :, :], start=True, stop=True)
                return last
            self.attend_context(score, V2, gated=QT)
            jobs = []
            self.rows_added(jobs, QT, w["proj"], w["b"], self.x, k=QK)
            self.products(jobs)


STAGES = ["L0_attn", "L0_xattn", "L0_ffn", "L1_attn", "L1_xattn", "L1_ffn",
          "L2_attn", "L2_xattn", "L2_ffn", "L3_attn", "L3_xattn", "L3_ffn"]


def decoder_kernel(nc, dram, where, x, seg, out):
    k = Kernel(nc, dram, where, x, out, seg)
    k.start()
    k.L0_attn()
    k.late_constants()
    k.L0_xattn()
    k.L0_ffn()
    k.L1_attn()
    k.L1_xattn()
    k.L1_ffn()
    k.L2_attn()
    k.L2_xattn()
    k.L2_ffn()
    k.L3_attn()
    k.L3_xattn()
    k.L3_ffn()
    k.finish()


def kernel(**inputs):
    import concourse.bacc as bacc
    from concourse.bass_utils import run_bass_kernel_spmd

    nc = bacc.Bacc("TRN2", target_bir_lowering=False, num_devices=1)
    arrays, dram, where = {}, {}, {}

    def give(name, a):
        a = np.ascontiguousarray(a)
        arrays["in_" + name] = a
        return nc.dram_tensor("in_" + name, a.shape, mybir.dt.from_np(a.dtype), kind="ExternalInput").ap()

    for stage, one in stage_arrays(inputs).items():
        many = isinstance(one, list)
        where[stage] = layout_of(one[0] if many else one)
        dram[stage] = give(stage, np.stack([pack(o, *where[stage]) for o in one]) if many else pack(one, *where[stage]))
    x = give("x", np.asarray(inputs["x"]))
    seg = give("seg", np.asarray(inputs["itok_BxS_0_255"]).reshape(NT, P).T)
    out = nc.dram_tensor("out_0", (B, S, D), F32, kind="ExternalOutput").ap()
    decoder_kernel(nc, dram, where, x, seg, out)
    r = run_bass_kernel_spmd(nc, [arrays], core_ids=[0])
    return r.results[0]["out_0"]
```
